# Optimizing a Trainium2 kernel written in Bass

```python
import numpy as np
import jax
import jax.numpy as jnp

def _softmax(x, axis=-1):
    return jax.nn.softmax(x, axis=axis)

def _gelu(x):
    return jax.nn.gelu(x, approximate=True)

def _silu(x):
    return jax.nn.silu(x)

def _sigmoid(x):
    return jax.nn.sigmoid(x)

def _layernorm(x, axis=-1, eps=1e-05):
    m = jnp.mean(x, axis=axis, keepdims=True)
    v = jnp.var(x, axis=axis, keepdims=True)
    return (x - m) / jnp.sqrt(v + eps)

def _scatter_add(tgt, idx, src, axis=0):
    return tgt.at[idx].add(src)

def _segment_sum(src, seg, n):
    return jax.ops.segment_sum(src, seg, n)
kernel_name = 'mk_hybrid_d1_jaxref_r8_f2486a'

def setup_inputs(seed: int=0):
    np.random.seed(seed)
    _w = jnp.asarray

    def _L0_attn_a_setup():
        import jax, jax.numpy as jnp
        import numpy as np
        EPS = 1e-06

        def rms_norm(x, scale):
            x32 = x.astype(jnp.float32)
            mean2 = jnp.mean(jnp.square(x32), axis=-1, keepdims=True)
            return x32 * jax.lax.rsqrt(mean2 + EPS) * scale
        key = jax.random.key(seed)
        ks = jax.random.split(key, 7)
        B, S, E, H, D = (2, 256, 256, 16, 128)
        w_std = 1.0 / np.sqrt(E)
        x = jax.random.normal(ks[0], (B, S, E), jnp.float32)
        wq = jax.random.normal(ks[1], (E, H, D), jnp.float32) * w_std
        wk = jax.random.normal(ks[2], (E, H, D), jnp.float32) * w_std
        wv = jax.random.normal(ks[3], (E, H, D), jnp.float32) * w_std
        wo = jax.random.normal(ks[4], (H, D, E), jnp.float32) * (1.0 / np.sqrt(H * D))
        q_scale = jnp.ones((D,), jnp.float32)
        k_scale = jnp.ones((D,), jnp.float32)
        return {'x': x, 'wq': wq, 'wk': wk, 'wv': wv, 'wo': wo, 'q_scale': q_scale, 'k_scale': k_scale}
    _L0_attn_a_in = _L0_attn_a_setup()

    def _L0_attn_b_setup():
        import jax, jax.numpy as jnp
        import numpy as np
        N_HEAD = 16
        N_EMBED = 256
        N_BLOCK = 256
        THETA = 10000.0

        def _rope_cos_sin(n_head, head_dim):
            freqs = THETA ** (-(jnp.arange(0, head_dim, 2, dtype=jnp.float32) / head_dim))
            t = jnp.arange(n_head, dtype=jnp.float32)
            ang = jnp.outer(t, freqs)
            return (jnp.cos(ang)[None, :, None, :], jnp.sin(ang)[None, :, None, :])

        def _apply_rope(x, cos, sin):
            B, H, T, hd = x.shape
            xp = x.reshape(B, H, T, hd // 2, 2)
            a, b = (xp[..., 0], xp[..., 1])
            out = jnp.stack([a * cos - b * sin, a * sin + b * cos], axis=-1)
            return out.reshape(B, H, T, hd)
        key = jax.random.key(seed)
        ks = jax.random.split(key, 5)
        E = N_EMBED
        x = jax.random.normal(ks[0], (2, 256, E), dtype=jnp.float32)
        s = 1.0 / np.sqrt(E)
        w_attn = jax.random.normal(ks[1], (E, 3 * E), dtype=jnp.float32) * s
        b_attn = jnp.zeros((3 * E,), dtype=jnp.float32)
        w_proj = jax.random.normal(ks[2], (E, E), dtype=jnp.float32) * s
        b_proj = jnp.zeros((E,), dtype=jnp.float32)
        return {'x': x, 'w_attn': w_attn, 'b_attn': b_attn, 'w_proj': w_proj, 'b_proj': b_proj}
    _L0_attn_b_in = _L0_attn_b_setup()

    def _L0_ffn_setup():
        import jax, jax.numpy as jnp
        import numpy as np
        DIM = 256
        INTER = 176
        N_EXPERTS = 16
        TOP_K = 2
        N_SHARED = 2
        SHARED_INTER = N_SHARED * INTER

        def _swiglu(t, wa, wb, wo):
            h = jax.nn.silu(t @ wa.T) * (t @ wb.T)
            return h @ wo.T
        key = jax.random.key(seed)
        ks = jax.random.split(key, 9)
        s = 0.02
        return {'x': jax.random.normal(ks[0], (4, 256, DIM), dtype=jnp.float32), 'gate_w': jax.random.normal(ks[1], (N_EXPERTS, DIM), dtype=jnp.float32) * s, 'w1': jax.random.normal(ks[2], (N_EXPERTS, INTER, DIM), dtype=jnp.float32) * s, 'w2': jax.random.normal(ks[3], (N_EXPERTS, DIM, INTER), dtype=jnp.float32) * s, 'w3': jax.random.normal(ks[4], (N_EXPERTS, INTER, DIM), dtype=jnp.float32) * s, 'sw1': jax.random.normal(ks[5], (SHARED_INTER, DIM), dtype=jnp.float32) * s, 'sw2': jax.random.normal(ks[6], (DIM, SHARED_INTER), dtype=jnp.float32) * s, 'sw3': jax.random.normal(ks[7], (SHARED_INTER, DIM), dtype=jnp.float32) * s}
    _L0_ffn_in = _L0_ffn_setup()
    _d = {'L0_attn_a_x': _L0_attn_a_in['x'], 'L0_attn_a_wq': _L0_attn_a_in['wq'], 'L0_attn_a_wk': _L0_attn_a_in['wk'], 'L0_attn_a_wv': _L0_attn_a_in['wv'], 'L0_attn_a_wo': _L0_attn_a_in['wo'], 'L0_attn_a_q_scale': _L0_attn_a_in['q_scale'], 'L0_attn_a_k_scale': _L0_attn_a_in['k_scale'], 'L0_attn_b_w_attn': _L0_attn_b_in['w_attn'], 'L0_attn_b_b_attn': _L0_attn_b_in['b_attn'], 'L0_attn_b_w_proj': _L0_attn_b_in['w_proj'], 'L0_attn_b_b_proj': _L0_attn_b_in['b_proj'], 'L0_ffn_gate_w': _L0_ffn_in['gate_w'], 'L0_ffn_w1': _L0_ffn_in['w1'], 'L0_ffn_w2': _L0_ffn_in['w2'], 'L0_ffn_w3': _L0_ffn_in['w3'], 'L0_ffn_sw1': _L0_ffn_in['sw1'], 'L0_ffn_sw2': _L0_ffn_in['sw2'], 'L0_ffn_sw3': _L0_ffn_in['sw3']}
    _x0 = _d['L0_attn_a_x']
    _d['L0_attn_a_x'] = jax.random.normal(jax.random.fold_in(jax.random.key(seed), 1), (1, 1024, 256), dtype=_x0.dtype)
    del _x0
    return _d

def reference(L0_attn_a_x, L0_attn_a_wq, L0_attn_a_wk, L0_attn_a_wv, L0_attn_a_wo, L0_attn_a_q_scale, L0_attn_a_k_scale, L0_attn_b_w_attn, L0_attn_b_b_attn, L0_attn_b_w_proj, L0_attn_b_b_proj, L0_ffn_gate_w, L0_ffn_w1, L0_ffn_w2, L0_ffn_w3, L0_ffn_sw1, L0_ffn_sw2, L0_ffn_sw3):

    def _L0_attn_a_ref(x, wq, wk, wv, wo, q_scale, k_scale):
        import jax, jax.numpy as jnp
        import numpy as np
        EPS = 1e-06

        def rms_norm(x, scale):
            x32 = x.astype(jnp.float32)
            mean2 = jnp.mean(jnp.square(x32), axis=-1, keepdims=True)
            return x32 * jax.lax.rsqrt(mean2 + EPS) * scale
        q = jnp.einsum('bse,ehd->bshd', x, wq)
        k = jnp.einsum('bse,ehd->bshd', x, wk)
        v = jnp.einsum('bse,ehd->bshd', x, wv)
        qn = rms_norm(q, q_scale)
        kn = rms_norm(k, k_scale)
        scores = jnp.einsum('bqhd,bkhd->bhqk', qn, kn)
        attn = jax.nn.softmax(scores, axis=-1)
        out = jnp.einsum('bhqk,bkhd->bqhd', attn, v)
        return jnp.einsum('bqhd,hde->bqe', out, wo)

    def _L0_attn_b_ref(x, w_attn, b_attn, w_proj, b_proj):
        import jax, jax.numpy as jnp
        import numpy as np
        N_HEAD = 16
        N_EMBED = 256
        N_BLOCK = 256
        THETA = 10000.0

        def _rope_cos_sin(n_head, head_dim):
            freqs = THETA ** (-(jnp.arange(0, head_dim, 2, dtype=jnp.float32) / head_dim))
            t = jnp.arange(n_head, dtype=jnp.float32)
            ang = jnp.outer(t, freqs)
            return (jnp.cos(ang)[None, :, None, :], jnp.sin(ang)[None, :, None, :])

        def _apply_rope(x, cos, sin):
            B, H, T, hd = x.shape
            xp = x.reshape(B, H, T, hd // 2, 2)
            a, b = (xp[..., 0], xp[..., 1])
            out = jnp.stack([a * cos - b * sin, a * sin + b * cos], axis=-1)
            return out.reshape(B, H, T, hd)
        B, T, E = x.shape
        H = N_HEAD
        hd = E // H
        qkv = x @ w_attn + b_attn
        q, k, v = jnp.split(qkv, 3, axis=-1)
        q = q.reshape(B, T, H, hd).transpose(0, 2, 1, 3)
        k = k.reshape(B, T, H, hd).transpose(0, 2, 1, 3)
        v = v.reshape(B, T, H, hd).transpose(0, 2, 1, 3)
        cos, sin = _rope_cos_sin(H, hd)
        q = _apply_rope(q, cos, sin)
        k = _apply_rope(k, cos, sin)
        scores = jnp.einsum('bhtd,bhsd->bhts', q, k)
        causal = jnp.tril(jnp.ones((T, T), dtype=bool))
        scores = jnp.where(causal[None, None], scores, jnp.float32(-jnp.inf))
        attn = jax.nn.softmax(scores, axis=-1) * E ** (-0.5)
        o = jnp.einsum('bhts,bhsd->bhtd', attn, v)
        o = o.transpose(0, 2, 1, 3).reshape(B, T, E)
        return o @ w_proj + b_proj

    def _L0_ffn_ref(x, gate_w, w1, w2, w3, sw1, sw2, sw3):
        import jax, jax.numpy as jnp
        import numpy as np
        DIM = 256
        INTER = 176
        N_EXPERTS = 16
        TOP_K = 2
        N_SHARED = 2
        SHARED_INTER = N_SHARED * INTER

        def _swiglu(t, wa, wb, wo):
            h = jax.nn.silu(t @ wa.T) * (t @ wb.T)
            return h @ wo.T
        shape = x.shape
        t = x.reshape(-1, DIM)
        scores = jax.nn.softmax(t @ gate_w.T, axis=-1)
        weights, indices = jax.lax.top_k(scores, TOP_K)
        y = jnp.zeros_like(t)
        for e in range(N_EXPERTS):
            w_e = jnp.sum(jnp.where(indices == e, weights, 0.0), axis=-1)
            y = y + _swiglu(t, w1[e], w3[e], w2[e]) * w_e[:, None]
        z = _swiglu(t, sw1, sw3, sw2)
        return (y + z).reshape(shape)
    x = L0_attn_a_x
    x = x + _L0_attn_a_ref(_layernorm(x, axis=-1), L0_attn_a_wq, L0_attn_a_wk, L0_attn_a_wv, L0_attn_a_wo, L0_attn_a_q_scale, L0_attn_a_k_scale)
    x = x + _L0_ffn_ref(_layernorm(x, axis=-1), L0_ffn_gate_w, L0_ffn_w1, L0_ffn_w2, L0_ffn_w3, L0_ffn_sw1, L0_ffn_sw2, L0_ffn_sw3)
    x = x + _L0_attn_b_ref(_layernorm(x, axis=-1), L0_attn_b_w_attn, L0_attn_b_b_attn, L0_attn_b_w_proj, L0_attn_b_b_proj)
    x = x + _L0_ffn_ref(_layernorm(x, axis=-1), L0_ffn_gate_w, L0_ffn_w1, L0_ffn_w2, L0_ffn_w3, L0_ffn_sw1, L0_ffn_sw2, L0_ffn_sw3)
    return x

_drawn_inputs = setup_inputs


def setup_inputs(seed=0):
    import zlib

    import numpy as np

    out = dict(_drawn_inputs(seed))
    spreads = {'L0_attn_a_q_scale': (1.0, 0.2),
     'L0_attn_a_k_scale': (1.0, 0.2),
     'L0_attn_b_b_attn': (0.0, 0.8),
     'L0_attn_b_b_proj': (0.0, 0.1)}
    factors = {'L0_ffn_gate_w': 8.0,
     'L0_ffn_w1': 8.0,
     'L0_ffn_w2': 8.0,
     'L0_ffn_w3': 8.0,
     'L0_ffn_sw1': 3.005,
     'L0_ffn_sw2': 2.726,
     'L0_ffn_sw3': 4.414}
    for name, (base, spread) in spreads.items():
        noise = np.random.default_rng([zlib.crc32(name.encode()), seed]).standard_normal(out[name].shape)
        drawn = base * np.exp(spread * noise) if base else spread * noise
        out[name] = jnp.asarray(drawn.astype(out[name].dtype))
    for name, factor in factors.items():
        out[name] = (out[name] * factor).astype(out[name].dtype)
    return out
```

```python
from contextlib import ExitStack

import numpy as np

import concourse.bass as bass
from concourse import mybir

F32 = mybir.dt.float32
F32R = mybir.dt.float32r
BF16 = mybir.dt.bfloat16
ALU = mybir.AluOpType
ACT = mybir.ActivationFunctionType
AX = mybir.AxisListType
ds = bass.ds

P = 128
N = 1024
E = 256
NT = N // P
NE = E // P
HA, DA = 16, 128
HB, DB = 16, 16
EXPERTS, INTER = 16, 176
UNITS = EXPERTS // 2 + 1
F = 2 * INTER
F3 = F - 2 * P
LN_EPS = 1e-5
RMS_EPS = 1e-6
MASKED = -1e30


class Chain:

    def __init__(self, eng, sem):
        self.eng, self.sem, self.base, self.n = eng, sem, 0, 0

    def begin(self, base):
        self.base, self.n = base, 0

    def __call__(self, ins):
        ins.then_inc(self.sem, 1)
        self.n += 1
        self.eng.wait_ge(self.sem, self.base + self.n)


def after(eng, sem, value):
    if isinstance(value, int) and value <= 0:
        return
    eng.wait_ge(sem, value)


def own_slot(eng, met):
    eng.sem_inc(met, 1)


def f32(ap):
    return ap.bitcast(F32)


def layer_norm(nc, scope, tag, m, load=None, split_f32=False):
    mk = m.inner(scope, tag)
    stats = mk.sb("stats", [P, NT, 6])
    mv = mk.sb("mv", [P, NT, 2])
    veps = mk.sb("veps", [P, NT])
    minus_half = mk.sb("minus_half", [P, NT])
    rstd = mk.sb("rstd", [P, NT])
    xn = mk.sb("xn", [P, NT, E])
    xps = [mk.ps(f"xps{u}", [P, 2, 2 * P]) for u in range(NT // 2)]
    x_in = [mk.sem(f"x_in{u}") for u in range(2)]
    half_set = mk.sem("half_set")
    var_ready = mk.sem("var_ready")
    rstd_ready = mk.sem("rstd_ready")
    xn_ready = mk.sem("xn_ready")
    transposed = mk.sem("transposed")
    hi_ready = mk.sem("hi_ready")
    lo_ready = mk.sem("lo_ready")
    chain_sem = mk.sem("chain")

    with nc.Block() as block:
        if load is not None:
            @block.sync
            def _(sp):
                for u in range(2):
                    sp.dma_start(m.x[:, 4 * u:4 * u + 4, :], load[:, 4 * u:4 * u + 4, :]).then_inc(x_in[u], 16)

        @block.gpsimd
        def _(pool):
            nc.gpsimd.memset(minus_half[:], -0.5).then_inc(half_set, 1)
            pool.wait_ge(half_set, 1)
            pool.wait_ge(var_ready, 1)
            nc.gpsimd.tensor_tensor(rstd[:], veps[:], minus_half[:], ALU.pow).then_inc(rstd_ready, 1)

        @block.vector
        def _(dve):
            chain = Chain(dve, chain_sem)
            for t in range(NT):
                if load is not None and t % 4 == 0:
                    dve.wait_ge(x_in[t // 4], 16)
                last = nc.vector.bn_stats(stats[:, t, :], m.x[:, t, :])
            chain(last)
            for t in range(NT):
                last = nc.vector.bn_aggr(mv[:, t, :], stats[:, t, :])
            chain(last)
            nc.vector.tensor_scalar(veps[:], mv[:, :, 1], LN_EPS, None, ALU.add).then_inc(var_ready, 1)
            dve.wait_ge(rstd_ready, 1)
            for t in range(NT):
                nc.vector.tensor_scalar(xn[:, t, :], m.x[:, t, :], mv[:, t, 0:1], rstd[:, t:t + 1],
                                        ALU.subtract, ALU.mult).then_inc(xn_ready, 1)
            for u in range(NT // 2):
                dve.wait_ge(hi_ready, u + 1)
                cols = slice(2 * P * u, 2 * P * (u + 1))
                nc.vector.tensor_tensor(m.xnt_lo[:, :, cols], xps[u][:, :, :], f32(m.xnt_hi[:, :, cols]),
                                        ALU.subtract).then_inc(lo_ready, 1)

        @block.tensor
        def _(pe):
            for u in range(NT // 2):
                pe.wait_ge(xn_ready, 2 * u + 2)
                for e in range(NE):
                    for j in range(2):
                        last = nc.tensor.transpose(xps[u][:, e, j * P:(j + 1) * P],
                                                   xn[:, 2 * u + j, e * P:(e + 1) * P], m.ident[:, :])
                last.then_inc(transposed, 1)

        @block.scalar
        def _(act):
            for u in range(NT // 2):
                act.wait_ge(transposed, u + 1)
                cols = slice(2 * P * u, 2 * P * (u + 1))
                if split_f32:
                    nc.scalar.activation(m.xnt[:, :, cols], xps[u][:, :, :], ACT.Copy)
                nc.scalar.activation(m.xnt_hi[:, :, cols], xps[u][:, :, :], ACT.Copy).then_inc(hi_ready, 1)


def three(nc, out, w_hi, w_lo, x_hi, x_lo, start, stop, **kw):
    nc.tensor.matmul(out, w_hi, x_hi, start=start, stop=False, **kw)
    nc.tensor.matmul(out, w_hi, x_lo, start=False, stop=False, **kw)
    return nc.tensor.matmul(out, w_lo, x_hi, start=False, stop=stop, **kw)


def attention_a(nc, scope, m, w_qkv, w_o, q_scale, k_scale):
    mk = m.inner(scope, "a")
    sb, ps, sem = mk.sb, mk.ps, mk.sem
    C3 = 3 * DA
    w_raw = [sb(f"w_raw{i}", [P, NE, C3]) for i in range(2)]
    w_hi = sb("w_hi", [P, NE, C3], F32R)
    w_lo = sb("w_lo", [P, NE, C3], F32R)
    wo_raw = sb("wo_raw", [P, HA, E])
    wo_hi = sb("wo_hi", [P, E], F32R)
    wo_lo = sb("wo_lo", [P, E], F32R)
    qkv = sb("qkv", [P, NT, C3])
    junk = sb("junk", [P, DA])
    ssq = sb("ssq", [P, NT, 2])
    msq = sb("msq", [P, NT, 2])
    minus_half = sb("minus_half", [P, NT])
    rrms = sb("rrms", [P, NT, 2])
    scales = sb("scales", [P, 2])
    qk_hi = [sb(f"qk_hi{i}", [P, 2, N], F32R) for i in range(2)]
    qk_lo = [sb(f"qk_lo{i}", [P, 2, N], F32R) for i in range(2)]
    v_hi = [sb(f"v_hi{i}", [P, NT, DA], F32R) for i in range(2)]
    v_lo = [sb(f"v_lo{i}", [P, NT, DA], F32R) for i in range(2)]
    probs = [sb(f"probs{i}", [P, N]) for i in range(2)]
    pt_hi = [sb(f"pt_hi{i}", [P, NT, 2 * P], F32R) for i in range(2)]
    pt_lo = [sb(f"pt_lo{i}", [P, NT, 2 * P], F32R) for i in range(2)]
    neg_max = sb("neg_max", [P, 2])
    sums = [sb(f"sums{i}", [P, NT]) for i in range(2)]
    rsums = [sb(f"rsums{i}", [P, NT]) for i in range(2)]
    ot_hi = sb("ot_hi", [P, N], F32R)
    ot_lo = sb("ot_lo", [P, N], F32R)

    s_ps = [ps(f"s_ps{i}", [P, N]) for i in range(2)]
    t_ps = [ps(f"t_ps{i}", [P, 4, P]) for i in range(2)]
    pv_ps = ps("pv_ps", [P, 512])
    mm_ps = ps("mm_ps", [P, 512])

    w_in = [sem(f"w_in{i}") for i in range(2)]
    const_in = sem("const_in")
    half_set = sem("half_set")
    w_split = sem("w_split")
    met = sem("met")
    wo_split = sem("wo_split")
    qkv_mm = sem("qkv_mm")
    qkv_out = sem("qkv_out")
    ms_ready = sem("ms_ready")
    rr_ready = sem("rr_ready")
    qk_scaled = sem("qk_scaled")
    qk_t = sem("qk_t")
    qk_hi_out = sem("qk_hi_out")
    qk_lo_out = sem("qk_lo_out")
    v_hi_out = sem("v_hi_out")
    v_lo_out = sem("v_lo_out")
    s_mm = sem("s_mm")
    s_max = sem("s_max")
    s_exp = sem("s_exp")
    p_t = sem("p_t")
    p_hi_out = sem("p_hi_out")
    p_lo_out = sem("p_lo_out")
    pv_mm = sem("pv_mm")
    o_hi_out = sem("o_hi_out")
    o_lo_out = sem("o_lo_out")
    op_mm = sem("op_mm")
    op_out = sem("op_out")
    rs_ready = sem("rs_ready")
    chain_sem = sem("chain")

    PAIRS = HA // 2

    def each_head(eng, head):
        for c in range(2):
            head(c, c, True)
        with eng.Fori(1, PAIRS - 1) as i:
            for c in range(2):
                head(i * 2 + c, c, True)
        head(HA - 2, 0, True)
        head(HA - 1, 1, False)

    with nc.Block() as block:
        @block.sync
        def _(sp):
            sp.dma_start(w_raw[0][:, :, :], w_qkv[0]).then_inc(w_in[0], 16)
            sp.dma_start(w_raw[1][:, :, :], w_qkv[1]).then_inc(w_in[1], 16)
            sp.dma_start(scales[:, 0:1], q_scale).then_inc(const_in, 16)
            sp.dma_start(scales[:, 1:2], k_scale).then_inc(const_in, 16)
            sp.dma_start(wo_raw[:, :, :], w_o).then_inc(const_in, 16)
            with sp.Fori(1, PAIRS) as i:
                for c in range(2):
                    sp.wait_ge(w_split, i * 2 + (c - 1))
                    sp.dma_start(w_raw[c][:, :, :],
                                 w_qkv[ds(i * 2 + c, 1)].rearrange("a p e c -> (a p) e c")).then_inc(w_in[c], 16)

        @block.gpsimd
        def _(pool):
            def split_w(h, c):
                pool.wait_ge(w_in[c], (h // 2 if isinstance(h, int) else h[0]) * 16 + 16)
                after(pool, qkv_mm, (h if isinstance(h, int) else h[1]) * 8)
                own_slot(pool, met)
                nc.gpsimd.tensor_copy(w_hi[:, :, :], w_raw[c][:, :, :]).then_inc(pool_chain.sem, 1)
                pool_chain.n += 1
                pool.wait_ge(pool_chain.sem, pool_chain.base + pool_chain.n)
                nc.gpsimd.tensor_tensor(w_lo[:, :, :], w_raw[c][:, :, :], f32(w_hi[:, :, :]),
                                        ALU.subtract).then_inc(w_split, 1)

            pool_chain = Chain(pool, half_set)

            def prep_batch(p, b):
                tiles = slice(4 * b, 4 * b + 4)
                pool.wait_ge(ms_ready, p * 2 + (b + 1))
                nc.gpsimd.tensor_tensor(rrms[:, tiles, :].rearrange("p t c -> p (t c)"),
                                        msq[:, tiles, :].rearrange("p t c -> p (t c)"),
                                        minus_half[:, :], ALU.pow).then_inc(rr_ready, 1)
                pool.wait_ge(rr_ready, p * 2 + (b + 1))
                qk = qkv[:, tiles, 0:2 * DA].rearrange("p t (c d) -> p t c d", d=DA)
                nc.gpsimd.tensor_tensor(qk, qk, rrms[:, tiles, :].unsqueeze(3).broadcast_to([P, 4, 2, DA]),
                                        ALU.mult).then_inc(qk_scaled, 1)

            def prep_v(p, c):
                pool.wait_ge(v_hi_out, p + 1)
                nc.gpsimd.tensor_tensor(v_lo[c][:, :, :], qkv[:, :, 2 * DA:C3], f32(v_hi[c][:, :, :]),
                                        ALU.subtract).then_inc(v_lo_out, 1)

            nc.gpsimd.memset(minus_half[:], -0.5).then_inc(half_set, 1)
            pool_chain.n = 1
            split_w(0, 0)
            prep_batch(0, 0)
            prep_batch(0, 1)
            split_w(1, 1)
            prep_v(0, 0)
            pool.wait_ge(const_in, 48)
            base = pool_chain.n

            def split_wo(h):
                after(pool, op_mm, h * 4)
                own_slot(pool, met)
                nc.gpsimd.tensor_copy(wo_hi[:, :], wo_raw[:, ds(h, 1), :].rearrange("p a e -> p (a e)"))\
                    .then_inc(half_set, 1)
                pool_chain.n += 1
                pool.wait_ge(half_set, pool_chain.base + pool_chain.n)
                own_slot(pool, met)
                nc.gpsimd.tensor_tensor(wo_lo[:, :], wo_raw[:, ds(h, 1), :].rearrange("p a e -> p (a e)"),
                                        f32(wo_hi[:, :]), ALU.subtract).then_inc(wo_split, 1)

            def head(h, par, prep, i=None):
                first = isinstance(h, int) and h == 0
                pool_chain.begin(base + h * 2 - (0 if first else 1))
                if not first:
                    split_wo(h - 1)
                if prep:
                    prep_batch(h + 1, 0)
                    prep_batch(h + 1, 1)
                    if not (isinstance(h, int) and h == HA - 2):
                        split_w(h + 2 if isinstance(h, int) else (i + 1, h + 2), par)
                    prep_v(h + 1, 1 - par)

            head(0, 0, True)
            head(1, 1, True)
            with pool.Fori(1, PAIRS - 1) as i:
                for c in range(2):
                    head(i * 2 + c, c, True, i)
            head(HA - 2, 0, True)
            pool_chain.begin(base + (HA - 1) * 2 - 2)
            split_wo(HA - 2)
            pool_chain.begin(base + (HA - 1) * 2 - 1)
            split_wo(HA - 1)

        @block.scalar
        def _(act):
            def qkv_tile(p, i):
                act.wait_ge(qkv_mm, p * 8 + (i + 1))
                if i == 0:
                    after(act, qk_t, p * 4)
                    after(act, v_lo_out, p)
                nc.scalar.activation(qkv[:, i, :], mm_ps[:, 0:C3], ACT.Copy).then_inc(qkv_out, 1)

            def qk_out(p, c, b):
                for r in range(2):
                    act.wait_ge(qk_t, p * 4 + (2 * b + r + 1))
                    if b == 0 and r == 0:
                        after(act, s_mm, (p - 1) * 8)
                    nc.scalar.activation(qk_hi[c][:, r, 512 * b:512 * (b + 1)],
                                         t_ps[r][:, :, :].rearrange("p a b -> p (a b)"), ACT.Copy,
                                         scale=scales[:, r:r + 1]).then_inc(qk_hi_out, 1)

            def v_out(p, c):
                act.wait_ge(qkv_out, p * 8 + 8)
                after(act, pv_mm, (p - 1) * 8)
                nc.scalar.activation(v_hi[c][:, :, :], qkv[:, :, 2 * DA:C3], ACT.Copy).then_inc(v_hi_out, 1)

            def exp_of(g, q, c, t):
                act.wait_ge(s_max, g + 1)
                after(act, p_t, g * 2 - 2)
                if t == 0:
                    after(act, rs_ready, (g - 8) // 8 if isinstance(g, int) else rs_before[0])
                nc.scalar.activation(probs[q][:, :], s_ps[q][:, :], ACT.Exp, bias=neg_max[:, q:q + 1],
                                     accum_out=sums[c][:, t:t + 1]).then_inc(s_exp, 1)

            rs_before = [None]

            def pt_out(g, t):
                J = t // 2
                for a in range(2):
                    act.wait_ge(p_t, g * 2 + (a + 1))
                    if t % 2 == 0 and a == 0:
                        after(act, pv_mm, g - 2)
                    nc.scalar.activation(pt_hi[J % 2][:, 4 * a:4 * a + 4, (t % 2) * P:(t % 2 + 1) * P],
                                         t_ps[a][:, :, :], ACT.Copy).then_inc(p_hi_out, 1)

            def o_out(J, j):
                act.wait_ge(pv_mm, J * 2 + 2)
                after(act, op_mm, J - 3)
                nc.scalar.activation(ot_hi[:, 2 * P * j:2 * P * (j + 1)], pv_ps[:, 0:2 * P], ACT.Copy)\
                    .then_inc(o_hi_out, 1)

            def head(h, par, prep):
                static = isinstance(h, int)
                for t in range(NT):
                    g = h * 8 + t
                    first = static and h == 0
                    if prep and t < 4:
                        qkv_tile(h + 1, 2 * t)
                    if not (first and t == 0):
                        pt_out(g - 1, (t - 1) % NT)
                    if t < NT - 1 or prep:
                        rs_before[0] = h
                        nt = (t + 1) % NT
                        exp_of(g + 1, (t + 1) % 2, par if t < NT - 1 else 1 - par, nt)
                    if prep and t < 4:
                        qkv_tile(h + 1, 2 * t + 1)
                    if t % 2 == 0 and not (first and t < 4):
                        j = (t // 2 + 2) % 4
                        o_out(h * 4 + (t // 2 - 2), j)
                    if prep and t in (4, 6):
                        qk_out(h + 1, 1 - par, (t - 4) // 2)
                    if prep and t == 5:
                        v_out(h + 1, 1 - par)

            act.wait_ge(const_in, 48)
            for i in range(NT):
                qkv_tile(0, i)
            for b in range(2):
                qk_out(0, 0, b)
            v_out(0, 0)
            exp_of(0, 0, 0, 0)
            each_head(act, head)
            pt_out(8 * HA - 1, NT - 1)
            o_out(4 * HA - 2, 2)
            o_out(4 * HA - 1, 3)

        @block.vector
        def _(dve):
            chain = Chain(dve, chain_sem)

            def squares(p, i):
                dve.wait_ge(qkv_out, p * 8 + (i + 1))
                for r in range(2):
                    qk = qkv[:, i, r * DA:(r + 1) * DA]
                    last = nc.vector.tensor_tensor_reduce(out=junk[:, :], in0=qk, in1=qk, scale=1.0, scalar=0.0,
                                                          op0=ALU.mult, op1=ALU.add,
                                                          accum_out=ssq[:, i, r:r + 1])
                    chain(last)

            def mean_squares(p, b):
                tiles = slice(4 * b, 4 * b + 4)
                nc.vector.tensor_scalar(msq[:, tiles, :], ssq[:, tiles, :], 1.0 / DA, RMS_EPS,
                                        ALU.mult, ALU.add).then_inc(ms_ready, 1)

            def qk_out(p, c, b):
                for r in range(2):
                    dve.wait_ge(qk_hi_out, p * 4 + (2 * b + r + 1))
                    cols = slice(512 * b, 512 * (b + 1))
                    nc.vector.scalar_tensor_tensor(
                        out=qk_lo[c][:, r, cols], in0=t_ps[r][:, :, :].rearrange("p a b -> p (a b)"),
                        scalar=scales[:, r:r + 1], in1=f32(qk_hi[c][:, r, cols]),
                        op0=ALU.mult, op1=ALU.subtract).then_inc(qk_lo_out, 1)

            def max_of(g, q):
                dve.wait_ge(s_mm, g + 1)
                after(dve, s_exp, g - 1)
                nc.vector.tensor_reduce(neg_max[:, q:q + 1], s_ps[q][:, :], AX.X, ALU.max,
                                        negate=True).then_inc(s_max, 1)

            def pt_out(g, t):
                for a in range(2):
                    dve.wait_ge(p_hi_out, g * 2 + (a + 1))
                    where = (slice(None), slice(4 * a, 4 * a + 4), slice((t % 2) * P, (t % 2 + 1) * P))
                    nc.vector.tensor_tensor(pt_lo[t // 2 % 2][where], t_ps[a][:, :, :],
                                            f32(pt_hi[t // 2 % 2][where]), ALU.subtract).then_inc(p_lo_out, 1)

            def o_out(J, j):
                dve.wait_ge(o_hi_out, J + 1)
                cols = slice(2 * P * j, 2 * P * (j + 1))
                nc.vector.tensor_tensor(ot_lo[:, cols], pv_ps[:, 0:2 * P], f32(ot_hi[:, cols]),
                                        ALU.subtract).then_inc(o_lo_out, 1)

            def invert(h, c):
                dve.wait_ge(s_exp, h * 8 + 8)
                nc.vector.reciprocal(rsums[c][:, :], sums[c][:, :]).then_inc(rs_ready, 1)
                dve.wait_ge(rs_ready, h + 1)

            def project(h, c, j):
                dve.wait_ge(op_mm, h * 4 + (j + 1))
                for k in range(2):
                    t = 2 * j + k
                    last = nc.vector.scalar_tensor_tensor(
                        out=m.x[:, t, :], in0=mm_ps[:, k * E:(k + 1) * E], scalar=rsums[c][:, t:t + 1],
                        in1=m.x[:, t, :], op0=ALU.mult, op1=ALU.add)
                last.then_inc(op_out, 1)

            def head(h, par, prep):
                first = isinstance(h, int) and h == 0
                chain.begin(base + h * 16)
                for t in range(NT):
                    g = h * 8 + t
                    if t < NT - 1:
                        max_of(g + 1, (t + 1) % 2)
                    if prep and t < 4:
                        squares(h + 1, 2 * t)
                    if not (first and t == 0):
                        pt_out(g - 1, (t - 1) % NT)
                    if t == 0 and not first:
                        invert(h - 1, 1 - par)
                    if prep and t < 4:
                        squares(h + 1, 2 * t + 1)
                        if t % 2:
                            mean_squares(h + 1, t // 2)
                    if t % 2 == 0 and not (first and t < 4):
                        o_out(h * 4 + (t // 2 - 2), (t // 2 + 2) % 4)
                    if 3 <= t < 7 and not first:
                        project(h - 1, 1 - par, t - 3)
                    if prep and t in (4, 6):
                        qk_out(h + 1, 1 - par, (t - 4) // 2)
                    if prep and t == NT - 1:
                        max_of(g + 1, 0)

            for i in range(NT):
                squares(0, i)
                if i % 4 == 3:
                    mean_squares(0, i // 4)
            for b in range(2):
                qk_out(0, 0, b)
            max_of(0, 0)
            base = chain.n
            each_head(dve, head)
            pt_out(8 * HA - 1, NT - 1)
            o_out(4 * HA - 2, 2)
            o_out(4 * HA - 1, 3)
            invert(HA - 1, 1)
            for j in range(4):
                project(HA - 1, 1, j)

        @block.tensor
        def _(pe):
            def qkv_tile(p, i):
                if i == 0:
                    pe.wait_ge(w_split, p + 1)
                    after(pe, op_out, (p - 2) * 4)
                    after(pe, qkv_out, p * 8)
                else:
                    pe.wait_ge(qkv_out, p * 8 + i)
                for e in range(NE):
                    rows = slice(i * P, (i + 1) * P)
                    last = three(nc, mm_ps[:, 0:C3], m.xnt_hi[:, e, rows], m.xnt_lo[:, e, rows],
                                 w_hi[:, e, :], w_lo[:, e, :], e == 0, e == NE - 1)
                last.then_inc(qkv_mm, 1)

            def qk_batch(p, b, g):
                pe.wait_ge(qk_scaled, p * 2 + (b + 1))
                for r in range(2):
                    if g is None:
                        after(pe, qk_lo_out, p * 4 + 2 * (b - 1) + r + 1)
                    else:
                        pe.wait_ge(p_lo_out, g * 2 + (r + 1))
                    for i in range(4):
                        last = nc.tensor.transpose(t_ps[r][:, i, :], qkv[:, 4 * b + i, r * DA:(r + 1) * DA],
                                                   m.ident[:, :])
                    last.then_inc(qk_t, 1)

            def scores(g, t, c):
                after(pe, s_exp, g - 1)
                for half in range(2):
                    cols = slice(512 * half, 512 * (half + 1))
                    rows = slice(t * P, (t + 1) * P)
                    last = three(nc, s_ps[t % 2][:, cols], qk_hi[c][:, 0, rows], qk_lo[c][:, 0, rows],
                                 qk_hi[c][:, 1, cols], qk_lo[c][:, 1, cols], True, True)
                last.then_inc(s_mm, 1)

            def transpose_p(g, t, qk_before):
                pe.wait_ge(s_exp, g + 1)
                for a in range(2):
                    after(pe, p_lo_out, g * 2 + (a - 1))
                    if qk_before is not None:
                        pe.wait_ge(qk_lo_out, qk_before + a)
                    for k in range(4):
                        kb = 4 * a + k
                        last = nc.tensor.transpose(t_ps[a][:, k, :], probs[t % 2][:, kb * P:(kb + 1) * P],
                                                   m.ident[:, :])
                    last.then_inc(p_t, 1)

            def pv_half(J, j, a, c):
                if a == 0:
                    pe.wait_ge(p_lo_out, J * 4 + 4)
                    after(pe, o_lo_out, J)
                    if j == 0:
                        pe.wait_ge(v_lo_out, pv_head[0] + 1)
                for k in range(4):
                    kb = 4 * a + k
                    last = three(nc, pv_ps[:, 0:2 * P], v_hi[c][:, kb, :], v_lo[c][:, kb, :],
                                 pt_hi[j % 2][:, kb, :], pt_lo[j % 2][:, kb, :], kb == 0, kb == NT - 1)
                last.then_inc(pv_mm, 1)

            pv_head = [0]

            def project(h, j):
                if j == 0:
                    pe.wait_ge(wo_split, h + 1)
                pe.wait_ge(o_lo_out, h * 4 + (j + 1))
                after(pe, op_out, h * 4 + j)
                for k in range(2):
                    rows = slice((2 * j + k) * P, (2 * j + k + 1) * P)
                    last = three(nc, mm_ps[:, k * E:(k + 1) * E], ot_hi[:, rows], ot_lo[:, rows],
                                 wo_hi[:, :], wo_lo[:, :], True, True)
                last.then_inc(op_mm, 1)

            def head(h, par, prep):
                first = isinstance(h, int) and h == 0
                for t in range(NT):
                    g = h * 8 + t
                    if t < NT - 1:
                        scores(g + 1, t + 1, par)
                    if prep and t < 4:
                        qkv_tile(h + 1, 2 * t)
                    if not (first and t == 0):
                        between = None
                        if t in (5, 7) and prep:
                            between = (h + 1) * 4 + (t - 4)
                        transpose_p(g - 1, (t - 1) % NT, between)
                    if not (first and t < 3):
                        s = t - 3
                        j = (s // 2) % 4
                        pv_head[0] = h if s >= 0 else h - 1
                        pv_half(h * 4 + s // 2, j, s % 2, par if s >= 0 else 1 - par)
                    if prep and t < 4:
                        qkv_tile(h + 1, 2 * t + 1)
                    if 3 <= t < 7 and not first:
                        if t == 3 and prep:
                            pe.wait_ge(qkv_out, h * 8 + 16)
                        project(h - 1, t - 3)
                    if prep and t in (4, 6):
                        qk_batch(h + 1, (t - 4) // 2, g - 1)
                    if prep and t == NT - 1:
                        pe.wait_ge(qk_lo_out, h * 4 + 8)
                        scores(g + 1, 0, 1 - par)

            for i in range(NT):
                qkv_tile(0, i)
            for b in range(2):
                qk_batch(0, b, None)
            pe.wait_ge(qk_lo_out, 4)
            scores(0, 0, 0)
            each_head(pe, head)
            transpose_p(8 * HA - 1, NT - 1, None)
            pv_head[0] = HA - 1
            pv_half(4 * HA - 2, 2, 1, 1)
            pv_half(4 * HA - 1, 3, 0, 1)
            pv_half(4 * HA - 1, 3, 1, 1)
            for j in range(4):
                project(HA - 1, j)


def mixture(nc, scope, tag, m, gate, w13, w2a, w2b, out=None):
    mk = m.inner(scope, tag)
    sb, ps, sem = mk.sb, mk.ps, mk.sem
    gate_sb = sb("gate", [P, NE, EXPERTS])
    raw13 = [sb(f"raw13{i}", [P, NE, 2 * F]) for i in range(2)]
    hi13 = [sb(f"hi13{i}", [P, NE, 2 * F], F32R) for i in range(2)]
    lo13 = [sb(f"lo13{i}", [P, NE, 2 * F], F32R) for i in range(2)]
    raw2 = [sb(f"raw2{i}", [P, 3, E]) for i in range(2)]
    hi2 = [sb(f"hi2{i}", [P, 3, E], F32R) for i in range(2)]
    lo2 = [sb(f"lo2{i}", [P, 3, E], F32R) for i in range(2)]
    G = [P, NT, EXPERTS]
    shifted, prob, rest = sb("shifted", G), sb("prob", G), sb("rest", G)
    rank, hit, pick1, pick2 = sb("rank", G), sb("hit", G), sb("pick1", G), sb("pick2", G)
    col = {k: sb(k, [P, NT]) for k in ("top", "total", "rtotal", "key")}
    weight = sb("weight", [P, NT, 2 * UNITS])
    gated = [sb(f"gated{i}", [P, F]) for i in range(2)]
    hidden = [sb(f"hidden{i}", [P, 3 * P]) for i in range(2)]
    ht_hi = [sb(f"ht_hi{i}", [P, 3, P], F32R) for i in range(2)]
    ht_lo = [sb(f"ht_lo{i}", [P, 3, P], F32R) for i in range(2)]

    a_ps, b_ps = ps("a_ps", [P, 512]), ps("b_ps", [P, 512])
    h_ps = [ps(f"h_ps{i}", [P, 512]) for i in range(2)]
    y_ps = [ps(f"y_ps{i}", [P, 2, E]) for i in range(NT // 2)]

    met = sem("met")
    gate_in = sem("gate_in")
    w_in = [sem(f"w_in{i}") for i in range(2)]
    w_split = sem("w_split")
    consts = sem("consts")
    logits = sem("logits")
    less_max = sem("less_max")
    exped = sem("exped")
    a_mm = sem("a_mm")
    b_mm = sem("b_mm")
    silu_out = sem("silu_out")
    h_out = sem("h_out")
    h_t = sem("h_t")
    h_hi_out = sem("h_hi_out")
    h_lo_out = sem("h_lo_out")
    y_mm = sem("y_mm")
    x_out = sem("x_out")
    stored = sem("stored")
    chain_sem = sem("chain")
    pool_sem = sem("pool_chain")

    def each_unit(eng, unit):
        unit(0, 0, False)
        with eng.Fori(0, 3) as i:
            unit(i * 2 + 1, 1, False)
            unit(i * 2 + 2, 0, False)
        unit(7, 1, False)
        unit(8, 0, True)

    def bc(ap):
        return ap.unsqueeze(2).broadcast_to([P, NT, EXPERTS])

    with nc.Block() as block:
        @block.sync
        def _(sp):
            def load(u, c):
                if isinstance(u, int):
                    s13, s2a, s2b = w13[u], w2a[u], w2b[u]
                else:
                    s13 = w13[ds(u, 1)].rearrange("a p e c -> (a p) e c")
                    s2a = w2a[ds(u, 1)].rearrange("a p e c -> (a p) e c")
                    s2b = w2b[ds(u, 1)].rearrange("a p c -> (a p) c")
                sp.dma_start(raw13[c][:, :, :], s13).then_inc(w_in[c], 16)
                sp.dma_start(raw2[c][:, 0:2, :], s2a).then_inc(w_in[c], 16)
                sp.dma_start(raw2[c][0:F3, 2, :], s2b).then_inc(w_in[c], 16)

            load(0, 0)
            sp.dma_start(gate_sb[:, :, :], gate).then_inc(gate_in, 16)
            load(1, 1)
            with sp.Fori(1, 4) as i:
                for c in range(2):
                    sp.wait_ge(w_split, i * 2 + (c - 1))
                    load(i * 2 + c, c)
            sp.wait_ge(w_split, UNITS - 2)
            load(UNITS - 1, 0)
            if out is not None:
                for t in range(NT // 2):
                    sp.wait_ge(x_out, t + 1)
                    sp.dma_start(out[:, 2 * t:2 * t + 2, :], m.x[:, 2 * t:2 * t + 2, :]).then_inc(stored, 16)
                sp.wait_ge(stored, 16 * (NT // 2))

        @block.gpsimd
        def _(pool):
            chain = Chain(pool, pool_sem)
            nc.gpsimd.memset(weight[:, :, 2 * UNITS - 2:2 * UNITS], 1.0)
            for i in range(2):
                nc.gpsimd.memset(hidden[i][:, F:3 * P], 0.0)
            for e in range(EXPERTS):
                last = nc.gpsimd.memset(rank[:, :, e], float(EXPERTS - e))
            last.then_inc(consts, 1)

            def split(u, c, done, loaded):
                pool.wait_ge(w_in[c], loaded)
                after(pool, y_mm, done)
                own_slot(pool, met)
                nc.gpsimd.tensor_copy(hi13[c][:, :, :], raw13[c][:, :, :]).then_inc(pool_sem, 1)
                nc.gpsimd.tensor_copy(hi2[c][:, 0:2, :], raw2[c][:, 0:2, :]).then_inc(pool_sem, 1)
                nc.gpsimd.tensor_copy(hi2[c][0:F3, 2, :], raw2[c][0:F3, 2, :]).then_inc(pool_sem, 1)
                pool.wait_ge(pool_sem, u * 3 + 3)
                nc.gpsimd.tensor_tensor(lo13[c][:, :, :], raw13[c][:, :, :], f32(hi13[c][:, :, :]), ALU.subtract)
                nc.gpsimd.tensor_tensor(lo2[c][:, 0:2, :], raw2[c][:, 0:2, :], f32(hi2[c][:, 0:2, :]),
                                        ALU.subtract)
                nc.gpsimd.tensor_tensor(lo2[c][0:F3, 2, :], raw2[c][0:F3, 2, :], f32(hi2[c][0:F3, 2, :]),
                                        ALU.subtract).then_inc(w_split, 1)

            split(0, 0, 0, 48)
            split(1, 1, 0, 48)
            with pool.Fori(1, 4) as i:
                for c in range(2):
                    split(i * 2 + c, c, i * 16 + (c - 1) * 8, i * 48 + 48)
            split(8, 0, 56, 240)

        @block.scalar
        def _(act):
            act.wait_ge(less_max, 1)
            nc.scalar.activation(prob[:, :, :], shifted[:, :, :], ACT.Exp).then_inc(exped, 1)

            def gate_out(n, q):
                act.wait_ge(a_mm, n + 1)
                after(act, h_out, n - 1)
                nc.scalar.activation(gated[q][:, :], a_ps[:, 0:F], ACT.Silu).then_inc(silu_out, 1)

            def ht_out(n, q):
                act.wait_ge(h_t, n + 1)
                after(act, y_mm, n - 1)
                nc.scalar.activation(ht_hi[q][:, :, :].rearrange("p a b -> p (a b)"), h_ps[q][:, 0:3 * P],
                                     ACT.Copy).then_inc(h_hi_out, 1)

            gate_out(0, 0)

            def unit(u, c, last):
                for t in range(NT):
                    n = u * NT + t
                    ht_out(n, t % 2)
                    if not (last and t == NT - 1):
                        gate_out(n + 1, (t + 1) % 2)

            each_unit(act, unit)

        @block.vector
        def _(dve):
            chain = Chain(dve, chain_sem)
            dve.wait_ge(logits, 1)
            lg = h_ps[1][:, 0:NT * EXPERTS].rearrange("p (t e) -> p t e", e=EXPERTS)
            chain(nc.vector.tensor_reduce(col["top"][:, :], lg, AX.X, ALU.max))
            nc.vector.tensor_tensor(shifted[:, :, :], lg, bc(col["top"][:, :]), ALU.subtract).then_inc(less_max, 1)
            dve.wait_ge(exped, 1)
            chain(nc.vector.tensor_reduce(col["total"][:, :], prob[:, :, :], AX.X, ALU.add))
            chain(nc.vector.reciprocal(col["rtotal"][:, :], col["total"][:, :]))
            chain(nc.vector.tensor_tensor(prob[:, :, :], prob[:, :, :], bc(col["rtotal"][:, :]), ALU.mult))
            dve.wait_ge(consts, 1)

            def pick(scores, picked):
                chain(nc.vector.tensor_reduce(col["top"][:, :], scores[:, :, :], AX.X, ALU.max))
                chain(nc.vector.tensor_tensor(hit[:, :, :], scores[:, :, :], bc(col["top"][:, :]), ALU.is_equal))
                chain(nc.vector.tensor_tensor(hit[:, :, :], hit[:, :, :], rank[:, :, :], ALU.mult))
                chain(nc.vector.tensor_reduce(col["key"][:, :], hit[:, :, :], AX.X, ALU.max))
                chain(nc.vector.tensor_tensor(picked[:, :, :], hit[:, :, :], bc(col["key"][:, :]), ALU.is_equal))

            pick(prob, pick1)
            chain(nc.vector.scalar_tensor_tensor(out=rest[:, :, :], in0=pick1[:, :, :], scalar=-2.0,
                                                 in1=prob[:, :, :], op0=ALU.mult, op1=ALU.add))
            pick(rest, pick2)
            chain(nc.vector.tensor_tensor(pick1[:, :, :], pick1[:, :, :], pick2[:, :, :], ALU.add))
            chain(nc.vector.tensor_tensor(weight[:, :, 0:EXPERTS], pick1[:, :, :], prob[:, :, :], ALU.mult))

            def hidden_of(n, u, t):
                dve.wait_ge(silu_out, n + 1)
                dve.wait_ge(b_mm, n + 1)
                after(dve, h_t, n - 1)
                for k in range(2):
                    cols = slice(k * INTER, (k + 1) * INTER)
                    w = weight[:, t, 2 * u + k:2 * u + k + 1] if isinstance(u, int) else weight[:, t, ds(u * 2 + k, 1)]
                    last = nc.vector.scalar_tensor_tensor(
                        out=hidden[t % 2][:, cols], in0=gated[t % 2][:, cols], scalar=w,
                        in1=b_ps[:, cols], op0=ALU.mult, op1=ALU.mult)
                last.then_inc(h_out, 1)

            def ht_out(n, q):
                dve.wait_ge(h_hi_out, n + 1)
                nc.vector.tensor_tensor(ht_lo[q][:, :, :].rearrange("p a b -> p (a b)"), h_ps[q][:, 0:3 * P],
                                        f32(ht_hi[q][:, :, :]).rearrange("p a b -> p (a b)"),
                                        ALU.subtract).then_inc(h_lo_out, 1)

            hidden_of(0, 0, 0)

            def unit(u, c, last):
                for t in range(NT):
                    n = u * NT + t
                    ht_out(n, t % 2)
                    if t < NT - 1:
                        hidden_of(n + 1, u, t + 1)
                    elif not last:
                        hidden_of(n + 1, u + 1, 0)

            each_unit(dve, unit)
            for b in range(NT // 2):
                dve.wait_ge(y_mm, (UNITS - 1) * NT + 2 * b + 2)
                nc.vector.tensor_tensor(m.x[:, 2 * b:2 * b + 2, :], m.x[:, 2 * b:2 * b + 2, :], y_ps[b][:, :, :],
                                        ALU.add).then_inc(x_out, 1)

        @block.tensor
        def _(pe):
            pe.wait_ge(gate_in, 16)
            for t in range(NT):
                for e in range(NE):
                    last = nc.tensor.matmul(h_ps[1][:, t * EXPERTS:(t + 1) * EXPERTS],
                                            m.xnt[:, e, t * P:(t + 1) * P], gate_sb[:, e, :],
                                            start=e == 0, stop=e == NE - 1)
            last.then_inc(logits, 1)

            def up(n, t, c):
                rows = slice(t * P, (t + 1) * P)
                for bank, free, done, off in ((a_ps, silu_out, a_mm, 0), (b_ps, h_out, b_mm, F)):
                    after(pe, free, n)
                    for e in range(NE):
                        last = three(nc, bank[:, 0:F], m.xnt_hi[:, e, rows], m.xnt_lo[:, e, rows],
                                     hi13[c][:, e, off:off + F], lo13[c][:, e, off:off + F], e == 0, e == NE - 1)
                    last.then_inc(done, 1)

            def transpose_h(n, q):
                pe.wait_ge(h_out, n + 1)
                if isinstance(n, int) and n == 1:
                    pe.wait_ge(exped, 1)
                after(pe, h_lo_out, n - 1)
                for k in range(3):
                    last = nc.tensor.transpose(h_ps[q][:, k * P:(k + 1) * P], hidden[q][:, k * P:(k + 1) * P],
                                               m.ident[:, :])
                last.then_inc(h_t, 1)

            def down(n, t, c, first, final):
                pe.wait_ge(h_lo_out, n + 1)
                q = t % 2
                for k in range(3):
                    r = P if k < 2 else F3
                    last = three(nc, y_ps[t // 2][:, t % 2, :], ht_hi[q][0:r, k, :], ht_lo[q][0:r, k, :],
                                 hi2[c][0:r, k, :], lo2[c][0:r, k, :], first and k == 0 and t % 2 == 0,
                                 final and k == 2, skip_group_check=True)
                last.then_inc(y_mm, 1)

            pe.wait_ge(w_split, 1)
            up(0, 0, 0)

            def unit(u, c, last):
                first = isinstance(u, int) and u == 0
                for t in range(NT):
                    n = u * NT + t
                    if t < NT - 1:
                        up(n + 1, t + 1, c)
                    elif not last:
                        pe.wait_ge(w_split, u + 2)
                        up(n + 1, 0, 1 - c)
                    transpose_h(n, t % 2)
                    if t > 0:
                        down(n - 1, t - 1, c, first, last)
                    elif not first:
                        down(n - 1, NT - 1, 1 - c, isinstance(u, int) and u == 1, False)

            each_unit(pe, unit)
            down(UNITS * NT - 1, NT - 1, 0, False, True)


def attention_b(nc, scope, m, w_attn, b_attn, rope, w_proj, b_proj):
    mk = m.inner(scope, "b")
    S = 8 * DB
    VW = 32
    GH = 4
    v_ext = mk.sb("v_ext", [P, NT, HB, VW])
    qst = mk.sb("qst", [P, HB, N], BF16)
    kst = mk.sb("kst", [P, HB, N], BF16)
    o_sb = mk.sb("o_sb", [P, NT, E])

    QS = "hhmmhlml"
    KS = "hmhmlhlm"
    with ExitStack() as inner:
        pk = m.inner(inner, "bp")
        w_raw = pk.sb("w_raw", [P, NE, 3 * E])
        w_hi = pk.sb("w_hi", [P, NE, 3 * E], F32R)
        w_lo = pk.sb("w_lo", [P, NE, 3 * E], F32R)
        bias = pk.sb("bias", [P, 3 * E])
        turn = pk.sb("turn", [P, 2, 2 * E])
        qk = [pk.sb(f"qk{i}", [P, 2 * E]) for i in range(2)]
        qk_cos = [pk.sb(f"qk_cos{i}", [P, 2 * E]) for i in range(2)]
        qk_sin = [pk.sb(f"qk_sin{i}", [P, 2 * E]) for i in range(2)]
        res = [pk.sb(f"res{i}", [P, 2 * E]) for i in range(2)]
        stack = [pk.sb(f"stack{i}", [P, 2, HB, 8, DB], BF16) for i in range(2)]
        qk_ps = [pk.ps(f"qk_ps{i}", [P, 512]) for i in range(2)]
        v_ps = [pk.ps(f"v_ps{i}", [P, 512]) for i in range(2)]
        st_ps = [pk.ps(f"st_ps{i}", [P, 8, P], BF16) for i in range(4)]
        w_in, const_in, w_split, hi_set = pk.sem("w_in"), pk.sem("const_in"), pk.sem("w_split"), pk.sem("hi_set")
        v_set, qkv_mm, qk_out, v_out = pk.sem("v_set"), pk.sem("qkv_mm"), pk.sem("qk_out"), pk.sem("v_out")
        turned, summed, high, resid, mid = (pk.sem("turned"), pk.sem("summed"), pk.sem("high"), pk.sem("resid"),
                                            pk.sem("mid"))
        stacked, st_t = pk.sem("stacked"), pk.sem("st_t")
        q_stored, k_stored, chain_sem = pk.sem("q_stored"), pk.sem("k_stored"), pk.sem("chain")

        with nc.Block() as block:
            @block.sync
            def _(sp):
                sp.dma_start(w_raw[:, :, :], w_attn).then_inc(w_in, 16)
                sp.dma_start(bias[:, :], b_attn.broadcast_to([P, 3 * E])).then_inc(const_in, 16)
                sp.dma_start(turn[:, :, :], rope.broadcast_to([P, 2, 2 * E])).then_inc(const_in, 16)

            @block.gpsimd
            def _(pool):
                nc.gpsimd.memset(v_ext[:, :, :, DB:DB + 1], 1.0)
                nc.gpsimd.memset(v_ext[:, :, :, DB + 1:VW], 0.0).then_inc(v_set, 1)
                pool.wait_ge(const_in, 32)
                for t in range(NT):
                    b = t % 2
                    pool.wait_ge(qk_out, t + 1)
                    after(pool, summed, t - 1)
                    nc.gpsimd.tensor_tensor(qk_cos[b][:, :], qk[b][:, :], turn[:, 0, :], ALU.mult)
                    x2 = qk[b][:, :].rearrange("p (c two) -> p c two", two=2)
                    s2 = qk_sin[b][:, :].rearrange("p (c two) -> p c two", two=2)
                    t2 = turn[:, 1, :].rearrange("p (c two) -> p c two", two=2)
                    for k in range(2):
                        last = nc.gpsimd.tensor_tensor(s2[:, :, k], x2[:, :, 1 - k], t2[:, :, k], ALU.mult)
                    last.then_inc(turned, 1)

            @block.scalar
            def _(act):
                act.wait_ge(w_in, 16)
                nc.scalar.activation(w_hi[:, :, :], w_raw[:, :, :], ACT.Copy).then_inc(hi_set, 1)

                def parts(t):
                    b = t % 2
                    act.wait_ge(summed, t + 1)
                    after(act, st_t, (t - 1) * 4)
                    both = stack[b][:, :, :, :, :]
                    src = qk[b][:, :].rearrange("p (r h d) -> p r h d", r=2, d=DB)
                    for r in range(2):
                        last = nc.scalar.activation(both[:, r, :, 0, :], src[:, r], ACT.Copy)
                    last.then_inc(high, 1)
                    act.wait_ge(resid, t + 1)
                    src = res[b][:, :].rearrange("p (r h d) -> p r h d", r=2, d=DB)
                    for r in range(2):
                        last = nc.scalar.activation(both[:, r, :, 3, :], src[:, r], ACT.Copy)
                    last.then_inc(mid, 1)

                def store(t):
                    for k in range(2):
                        act.wait_ge(st_t, t * 4 + k + 1)
                        nc.scalar.activation(qst[:, 8 * k:8 * k + 8, t * P:(t + 1) * P], st_ps[k][:, :, :],
                                             ACT.Copy).then_inc(q_stored, 1)

                for t in range(NT + 1):
                    if t < NT:
                        parts(t)
                    if t > 0:
                        store(t - 1)

            @block.vector
            def _(dve):
                chain = Chain(dve, chain_sem)
                dve.wait_ge(hi_set, 1)
                nc.vector.tensor_tensor(w_lo[:, :, :], w_raw[:, :, :], f32(w_hi[:, :, :]),
                                        ALU.subtract).then_inc(w_split, 1)
                dve.wait_ge(const_in, 32)
                dve.wait_ge(v_set, 1)

                def take(t):
                    b = t % 2
                    dve.wait_ge(qkv_mm, t + 1)
                    nc.vector.tensor_tensor(qk[b][:, :], qk_ps[b][:, :], bias[:, 0:2 * E], ALU.add)\
                        .then_inc(qk_out, 1)
                    nc.vector.tensor_tensor(v_ext[:, t, :, 0:DB],
                                            v_ps[b][:, 0:E].rearrange("p (h d) -> p h d", d=DB),
                                            bias[:, 2 * E:3 * E].rearrange("p (h d) -> p h d", d=DB),
                                            ALU.add).then_inc(v_out, 1)

                def slots(letters, part, first):
                    return [i for i, x in enumerate(letters) if x == part and i != first]

                def parts(t):
                    b = t % 2
                    dve.wait_ge(turned, t + 1)
                    nc.vector.tensor_tensor(qk[b][:, :], qk_cos[b][:, :], qk_sin[b][:, :], ALU.add)\
                        .then_inc(summed, 1)
                    dve.wait_ge(high, t + 1)
                    x4 = qk[b][:, :].rearrange("p (r h d) -> p r h d", r=2, d=DB)
                    r4 = res[b][:, :].rearrange("p (r h d) -> p r h d", r=2, d=DB)
                    for r in range(2):
                        last = nc.vector.tensor_tensor(r4[:, r], x4[:, r], stack[b][:, r, :, 0, :], ALU.subtract)
                    last.then_inc(resid, 1)
                    dve.wait_ge(mid, t + 1)
                    low = (QS.index("l"), KS.index("l"))
                    for r in range(2):
                        last = nc.vector.tensor_tensor(stack[b][:, r, :, low[r], :], r4[:, r],
                                                       stack[b][:, r, :, 3, :], ALU.subtract)
                    chain(last)
                    for r, letters in ((0, QS), (1, KS)):
                        for part, first in (("h", 0), ("m", 3), ("l", low[r])):
                            for s in slots(letters, part, first):
                                last = nc.vector.tensor_copy(stack[b][:, r, :, s, :], stack[b][:, r, :, first, :])
                    last.then_inc(stacked, 1)

                def store(t):
                    for k in range(2):
                        dve.wait_ge(st_t, t * 4 + k + 3)
                        nc.vector.tensor_copy(kst[:, 8 * k:8 * k + 8, t * P:(t + 1) * P], st_ps[2 + k][:, :, :])\
                            .then_inc(k_stored, 1)

                for t in range(NT + 1):
                    if t < NT:
                        take(t)
                        parts(t)
                    if t > 0:
                        store(t - 1)

            @block.tensor
            def _(pe):
                pe.wait_ge(w_split, 1)

                def project(t):
                    after(pe, v_out, t - 1)
                    rows = slice(t * P, (t + 1) * P)
                    for bank, cols in ((qk_ps[t % 2][:, :], slice(0, 2 * E)), (v_ps[t % 2][:, 0:E], slice(2 * E, 3 * E))):
                        for e in range(NE):
                            last = three(nc, bank, m.xnt_hi[:, e, rows], m.xnt_lo[:, e, rows],
                                         w_hi[:, e, cols], w_lo[:, e, cols], e == 0, e == NE - 1)
                    last.then_inc(qkv_mm, 1)

                def transpose_stacks(t):
                    pe.wait_ge(stacked, t + 1)
                    for k in range(4):
                        after(pe, q_stored if k < 2 else k_stored, t * 2 - 1 + k % 2)
                        for i in range(8):
                            last = nc.tensor.transpose(
                                st_ps[k][:, i, :],
                                stack[t % 2][:, k // 2, 8 * (k % 2) + i, :, :].rearrange("p s d -> p (s d)"),
                                m.ident_bf[:, :])
                        last.then_inc(st_t, 1)

                project(0)
                for t in range(NT):
                    if t + 1 < NT:
                        project(t + 1)
                    transpose_stacks(t)

    with ExitStack() as inner:
        ak = m.inner(inner, "ba")
        vg = [ak.sb(f"vg{i}", [P, NT, GH * VW]) for i in range(1)][0]
        probs = [ak.sb(f"probs{i}", [P, N]) for i in range(2)]
        pt = [[ak.sb(f"pt{q}{i}", [P, NT, P]) for i in range(GH)] for q in range(2)]
        neg_max = ak.sb("neg_max", [P, 2])
        ot = [ak.sb(f"ot{i}", [P, P]) for i in range(2)]
        rsum = ak.sb("rsum", [P, GH])
        s_ps = [ak.ps(f"s_ps{i}", [P, N]) for i in range(2)]
        t_ps = [ak.ps(f"t_ps{i}", [P, 4, P]) for i in range(2)]
        pv_ps = ak.ps("pv_ps", [P, 512])
        ob_ps = ak.ps("ob_ps", [P, 512])
        met = ak.sem("met")
        vg_ready, s_mm, s_max, s_exp = ak.sem("vg_ready"), ak.sem("s_mm"), ak.sem("s_max"), ak.sem("s_exp")
        t_mm, t_out = [ak.sem(f"t_mm{i}") for i in range(2)], [ak.sem(f"t_out{i}") for i in range(2)]
        pv_mm, ot_out, ob_t, o_out, rs = ak.sem("pv_mm"), ak.sem("ot_out"), ak.sem("ob_t"), ak.sem("o_out"), ak.sem("rs")
        GROUPS = HB // GH
        NU = NT * GH
        WIDE = GH * (NT - 4)

        def units():
            return [(t, i) for t in range(NT) for i in range(GH)]

        def over_groups(eng, group):
            group(0)
            with eng.Fori(1, GROUPS) as g:
                group(g)

        def wide_before(n):
            return max(0, n - 4 * GH)

        with nc.Block() as block:
            @block.gpsimd
            def _(pool):
                def group(g):
                    after(pool, pv_mm, g * NT)
                    src = v_ext[:, :, 0:GH, :] if isinstance(g, int) else v_ext[:, :, ds(g * GH, GH), :]
                    own_slot(pool, met)
                    nc.gpsimd.tensor_copy(vg[:, :, :].rearrange("p t (h d) -> p t h d", d=VW), src)\
                        .then_inc(vg_ready, 1)
                over_groups(pool, group)

            @block.scalar
            def _(act):
                def exp_of(g, n):
                    t = n // GH
                    act.wait_ge(s_max, g * NU + n + 1)
                    after(act, t_mm[0], g * NU + n - 1)
                    if isinstance(g, int) is False or g * WIDE + wide_before(n - 1) > 0:
                        act.wait_ge(t_mm[1], g * WIDE + wide_before(n - 1))
                    nc.scalar.activation(probs[n % 2][:, 0:(t + 1) * P], s_ps[n % 2][:, 0:(t + 1) * P], ACT.Exp,
                                         bias=neg_max[:, n % 2:n % 2 + 1]).then_inc(s_exp, 1)

                def pt_out(g, n):
                    t, i = n // GH, n % GH
                    if t >= 4:
                        act.wait_ge(t_mm[1], g * WIDE + wide_before(n) + 1)
                        after(act, pv_mm, g * NT + t - 1)
                        nc.scalar.activation(pt[t % 2][i][:, 4:t + 1, :], t_ps[1][:, 0:t - 3, :], ACT.Copy)\
                            .then_inc(t_out[1], 1)

                def out_t(g, t):
                    act.wait_ge(pv_mm, g * NT + t + 1)
                    after(act, ob_t, g * NT + t - 1)
                    nc.scalar.activation(ot[t % 2][:, :], pv_ps[:, 0:P], ACT.Copy).then_inc(ot_out, 1)

                def group(g):
                    exp_of(g, 0)
                    for n in range(NU):
                        if n + 1 < NU:
                            exp_of(g, n + 1)
                        pt_out(g, n)
                        if n % GH == 1 and n > GH:
                            out_t(g, n // GH - 1)
                    out_t(g, NT - 1)
                over_groups(act, group)

            @block.vector
            def _(dve):
                def max_of(g, n):
                    t = n // GH
                    dve.wait_ge(s_mm, g * NU + n + 1)
                    after(dve, s_exp, g * NU + n - 1)
                    nc.vector.tensor_reduce(neg_max[:, n % 2:n % 2 + 1], s_ps[n % 2][:, 0:(t + 1) * P], AX.X,
                                            ALU.max, negate=True).then_inc(s_max, 1)

                def pt_out(g, n):
                    t, i = n // GH, n % GH
                    k = min(t + 1, 4)
                    dve.wait_ge(t_mm[0], g * NU + n + 1)
                    after(dve, pv_mm, g * NT + t - 1)
                    nc.vector.tensor_copy(pt[t % 2][i][:, 0:k, :], t_ps[0][:, 0:k, :]).then_inc(t_out[0], 1)

                def finish(g, t):
                    dve.wait_ge(ob_t, g * NT + t + 1)
                    got = ob_ps[:, 0:P].rearrange("p (h d) -> p h d", d=VW)
                    after(dve, o_out, g * NT + t)
                    nc.vector.reciprocal(rsum[:, :], got[:, :, DB]).then_inc(rs, 1)
                    dve.wait_ge(rs, g * NT + t + 1)
                    dst = o_sb[:, t, 0:GH * DB] if isinstance(g, int) else o_sb[:, t, ds(g * (GH * DB), GH * DB)]
                    nc.vector.scalar_tensor_tensor(
                        out=dst.rearrange("p (h d) -> p h d", d=DB), in0=got[:, :, 0:DB], scalar=float(E) ** -0.5,
                        in1=rsum[:, :].unsqueeze(2).broadcast_to([P, GH, DB]),
                        op0=ALU.mult, op1=ALU.mult).then_inc(o_out, 1)

                def group(g):
                    max_of(g, 0)
                    for n in range(NU):
                        if n + 1 < NU:
                            max_of(g, n + 1)
                        pt_out(g, n)
                        if n % GH == 2 and n > GH:
                            finish(g, n // GH - 1)
                    finish(g, NT - 1)
                over_groups(dve, group)

            @block.tensor
            def _(pe):
                def scores(g, n):
                    t, i = n // GH, n % GH
                    w = (t + 1) * P
                    after(pe, s_exp, g * NU + n - 1)
                    q = qst[:, i, t * P:(t + 1) * P] if isinstance(g, int) else \
                        qst[:, ds(g * GH + i, 1), t * P:(t + 1) * P].rearrange("p a c -> p (a c)")
                    for c in range(0, w, 512):
                        e = min(w, c + 512)
                        k = kst[:, i, c:e] if isinstance(g, int) else \
                            kst[:, ds(g * GH + i, 1), c:e].rearrange("p a c -> p (a c)")
                        last = nc.tensor.matmul(s_ps[n % 2][:, c:e], q, k, start=True, stop=e != w)
                    last = nc.tensor.matmul(s_ps[n % 2][:, w - P:w], m.ident_bf[:, :], m.mask[:, :],
                                            start=False, stop=True)
                    last.then_inc(s_mm, 1)

                def transpose_p(g, n):
                    t = n // GH
                    pe.wait_ge(s_exp, g * NU + n + 1)
                    for a in range(2 if t >= 4 else 1):
                        after(pe, t_out[a], g * (WIDE if a else NU) + (wide_before(n) if a else n))
                        for kb in range(4 * a, min(t + 1, 4 * a + 4)):
                            last = nc.tensor.transpose(t_ps[a][:, kb - 4 * a, :],
                                                       probs[n % 2][:, kb * P:(kb + 1) * P], m.ident[:, :])
                        last.then_inc(t_mm[a], 1)

                def times_v(g, t):
                    pe.wait_ge(t_out[0], g * NU + (t + 1) * GH)
                    if t >= 4:
                        pe.wait_ge(t_out[1], g * WIDE + (t - 3) * GH)
                    after(pe, ot_out, g * NT + t)
                    if t == 0:
                        pe.wait_ge(vg_ready, g + 1)
                    for kb in range(t + 1):
                        for i in range(GH):
                            last = nc.tensor.matmul(pv_ps[VW * i:VW * (i + 1), 0:P], vg[:, kb, VW * i:VW * (i + 1)],
                                                    pt[t % 2][i][:, kb, :], start=kb == 0, stop=kb == t)
                    last.then_inc(pv_mm, 1)

                def back(g, t):
                    pe.wait_ge(ot_out, g * NT + t + 1)
                    after(pe, o_out, g * NT + t)
                    nc.tensor.transpose(ob_ps[:, 0:P], ot[t % 2][:, :], m.ident[:, :]).then_inc(ob_t, 1)

                def group(g):
                    scores(g, 0)
                    for n in range(NU):
                        if n + 1 < NU:
                            scores(g, n + 1)
                        transpose_p(g, n)
                        if n % GH == 0 and n > 0:
                            times_v(g, n // GH - 1)
                        if n % GH == 2 and n > GH:
                            back(g, n // GH - 1)
                    times_v(g, NT - 1)
                    back(g, NT - 1)
                over_groups(pe, group)

    with ExitStack() as inner:
        ok = m.inner(inner, "bo")
        w_raw, w_hi, w_lo = ok.sb("w_raw", [P, NE, E]), ok.sb("w_hi", [P, NE, E], F32R), ok.sb("w_lo", [P, NE, E], F32R)
        bias = ok.sb("bias", [P, E])
        ot_hi, ot_lo = ok.sb("ot_hi", [P, NE, N], F32R), ok.sb("ot_lo", [P, NE, N], F32R)
        o_ps = [ok.ps(f"o_ps{i}", [P, NE, 2 * P]) for i in range(4)]
        y_ps = [ok.ps(f"y_ps{i}", [P, 512]) for i in range(2)]
        const_in, hi_set, w_split = ok.sem("const_in"), ok.sem("hi_set"), ok.sem("w_split")
        biased, o_t, hi_out, lo_out, y_mm, y_out = (ok.sem("biased"), ok.sem("o_t"), ok.sem("hi_out"), ok.sem("lo_out"),
                                                    ok.sem("y_mm"), ok.sem("y_out"))
        with nc.Block() as block:
            @block.sync
            def _(sp):
                sp.dma_start(w_raw[:, :, :], w_proj).then_inc(const_in, 16)
                sp.dma_start(bias[:, :], b_proj.broadcast_to([P, E])).then_inc(const_in, 16)

            @block.scalar
            def _(act):
                act.wait_ge(const_in, 32)
                nc.scalar.activation(w_hi[:, :, :], w_raw[:, :, :], ACT.Copy).then_inc(hi_set, 1)
                for u in range(4):
                    act.wait_ge(o_t, u + 1)
                    nc.scalar.activation(ot_hi[:, :, 2 * P * u:2 * P * (u + 1)], o_ps[u][:, :, :], ACT.Copy)\
                        .then_inc(hi_out, 1)

            @block.vector
            def _(dve):
                dve.wait_ge(const_in, 32)
                nc.vector.tensor_tensor(m.x[:, :, :], m.x[:, :, :], bias[:, :].unsqueeze(1).broadcast_to([P, NT, E]),
                                        ALU.add).then_inc(biased, 1)
                dve.wait_ge(hi_set, 1)
                nc.vector.tensor_tensor(w_lo[:, :, :], w_raw[:, :, :], f32(w_hi[:, :, :]), ALU.subtract)\
                    .then_inc(w_split, 1)
                for u in range(4):
                    dve.wait_ge(hi_out, u + 1)
                    cols = slice(2 * P * u, 2 * P * (u + 1))
                    nc.vector.tensor_tensor(ot_lo[:, :, cols], o_ps[u][:, :, :], f32(ot_hi[:, :, cols]),
                                            ALU.subtract).then_inc(lo_out, 1)
                dve.wait_ge(biased, 1)
                for t in range(NT):
                    dve.wait_ge(y_mm, t + 1)
                    nc.vector.tensor_tensor(m.x[:, t, :], m.x[:, t, :], y_ps[t % 2][:, 0:E], ALU.add).then_inc(y_out, 1)

            @block.tensor
            def _(pe):
                for u in range(4):
                    for e in range(NE):
                        for j in range(2):
                            last = nc.tensor.transpose(o_ps[u][:, e, j * P:(j + 1) * P],
                                                       o_sb[:, 2 * u + j, e * P:(e + 1) * P], m.ident[:, :])
                    last.then_inc(o_t, 1)
                pe.wait_ge(w_split, 1)
                for t in range(NT):
                    pe.wait_ge(lo_out, t // 2 + 1)
                    after(pe, y_out, t - 1)
                    rows = slice(t * P, (t + 1) * P)
                    for e in range(NE):
                        last = three(nc, y_ps[t % 2][:, 0:E], ot_hi[:, e, rows], ot_lo[:, e, rows],
                                     w_hi[:, e, :], w_lo[:, e, :], e == 0, e == NE - 1)
                    last.then_inc(y_mm, 1)


class Memory:

    def __init__(self, nc, scope, sems, tag):
        self.nc, self.scope, self.sems, self.tag = nc, scope, sems, tag

    def inner(self, scope, tag):
        return Memory(self.nc, scope, self.sems, tag)

    def sb(self, name, shape, dt=F32):
        return self.scope.enter_context(self.nc.sbuf_tensor(f"{self.tag}_{name}", shape, dt))

    def ps(self, name, shape, dt=F32):
        return self.scope.enter_context(self.nc.psum_tensor(f"{self.tag}_{name}", shape, dt))

    def sem(self, name):
        return self.sems.enter_context(self.nc.semaphore(f"{self.tag}_{name}"))


def program(nc, x, w_qkv, w_o, q_scale, k_scale, w_attn, b_attn, rope, w_proj, b_proj, gate, w13, w2a, w2b, out):
    with ExitStack() as ctx:
        m = Memory(nc, ctx, ctx, "m")
        m.x = m.sb("x", [P, NT, E])
        m.xnt = m.sb("xnt", [P, NE, N])
        m.xnt_hi = m.sb("xnt_hi", [P, NE, N], F32R)
        m.xnt_lo = m.sb("xnt_lo", [P, NE, N], F32R)
        m.ident = m.sb("ident", [P, P])
        m.ident_bf = m.sb("ident_bf", [P, P], BF16)
        m.mask = m.sb("mask", [P, P], BF16)
        made = m.sem("made")
        with nc.Block() as block:
            @block.gpsimd
            def _(pool):
                nc.gpsimd.memset(m.ident[:, :], 0.0).then_inc(made, 1)
                nc.gpsimd.memset(m.ident_bf[:, :], 0.0).then_inc(made, 1)
                nc.gpsimd.memset(m.mask[:, :], 0.0).then_inc(made, 1)
                pool.wait_ge(made, 3)
                for eye in (m.ident, m.ident_bf):
                    nc.gpsimd.affine_select(out=eye[:, :], in_=eye[:, :], compare_op=ALU.not_equal, fill=1.0,
                                            base=0, pattern=[[-1, P]], channel_multiplier=1)
                nc.gpsimd.affine_select(out=m.mask[:, :], in_=m.mask[:, :], compare_op=ALU.is_ge, fill=MASKED,
                                        base=0, pattern=[[-1, P]], channel_multiplier=1)
        for i, phase in enumerate(("a", "moe", "b", "moe")):
            with ExitStack() as scope:
                layer_norm(nc, scope, f"ln{i}", m, load=x if i == 0 else None, split_f32=phase == "moe")
            with ExitStack() as scope:
                if phase == "a":
                    attention_a(nc, scope, m, w_qkv, w_o, q_scale, k_scale)
                elif phase == "b":
                    attention_b(nc, scope, m, w_attn, b_attn, rope, w_proj, b_proj)
                else:
                    mixture(nc, scope, f"moe{i}", m, gate, w13, w2a, w2b, out=out if i == 3 else None)


def rope_table():
    freqs = np.float32(10000.0) ** (-(np.arange(0, DB, 2, dtype=np.float32) / np.float32(DB)))
    angle = np.outer(np.arange(HB, dtype=np.float32), freqs)
    cos = np.repeat(np.cos(angle), 2, axis=1)
    sin = np.stack([-np.sin(angle), np.sin(angle)], axis=-1)
    return np.stack([np.tile(cos.reshape(-1), 2), np.tile(sin.reshape(-1), 2)]).astype(np.float32)[None]


def kernel(**inputs):
    import concourse.bacc as bacc
    from concourse.bass_utils import run_bass_kernel_spmd

    def part(name):
        return np.asarray(inputs[name])

    def tiles(a):
        return np.ascontiguousarray(a.reshape(-1, P, *a.shape[1:]).swapaxes(0, 1))

    qkv = np.concatenate([part(f"L0_attn_a_w{c}") for c in "qkv"], axis=2)
    qkv = qkv.reshape(NE, P, HA, 3 * DA).transpose(2, 1, 0, 3)
    w1 = np.concatenate([part("L0_ffn_w1").reshape(UNITS - 1, F, E), part("L0_ffn_sw1")[None]])
    w3 = np.concatenate([part("L0_ffn_w3").reshape(UNITS - 1, F, E), part("L0_ffn_sw3")[None]])
    w13 = np.concatenate([w1, w3], axis=1).transpose(0, 2, 1).reshape(UNITS, NE, P, 2 * F).transpose(0, 2, 1, 3)
    w2 = np.concatenate([part("L0_ffn_w2").transpose(0, 2, 1).reshape(UNITS - 1, F, E),
                         part("L0_ffn_sw2").T[None]])
    arrays = {
        "x": tiles(part("L0_attn_a_x")[0]),
        "w_qkv": np.ascontiguousarray(qkv),
        "w_o": np.ascontiguousarray(part("L0_attn_a_wo").transpose(1, 0, 2)),
        "q_scale": part("L0_attn_a_q_scale")[:, None],
        "k_scale": part("L0_attn_a_k_scale")[:, None],
        "w_attn": tiles(part("L0_attn_b_w_attn")),
        "b_attn": part("L0_attn_b_b_attn")[None],
        "rope": rope_table(),
        "w_proj": tiles(part("L0_attn_b_w_proj")),
        "b_proj": part("L0_attn_b_b_proj")[None],
        "gate": tiles(part("L0_ffn_gate_w").T),
        "w13": np.ascontiguousarray(w13),
        "w2a": np.ascontiguousarray(w2[:, 0:2 * P].reshape(UNITS, 2, P, E).transpose(0, 2, 1, 3)),
        "w2b": np.ascontiguousarray(w2[:, 2 * P:F]),
    }
    nc = bacc.Bacc("TRN2", target_bir_lowering=False, num_devices=1)
    aps = [nc.dram_tensor(f"in_{name}", a.shape, F32, kind="ExternalInput").ap() for name, a in arrays.items()]
    out = nc.dram_tensor("out", (P, NT, E), F32, kind="ExternalOutput").ap()
    program(nc, *aps, out)
    r = run_bass_kernel_spmd(nc, [{f"in_{name}": a for name, a in arrays.items()}], core_ids=[0])
    return r.results[0]["out"].transpose(1, 0, 2).reshape(1, N, E)
```

```python
from contextlib import ExitStack

import numpy as np

import concourse.bass as bass
from concourse import mybir

F32 = mybir.dt.float32
F32R = mybir.dt.float32r
BF16 = mybir.dt.bfloat16
I32 = mybir.dt.int32
ALU = mybir.AluOpType
ACT = mybir.ActivationFunctionType
AX = mybir.AxisListType
ds = bass.ds

P = 128
N = 1024
E = 256
NT = N // P
NE = E // P
HA, DA = 16, 128
HB, DB = 16, 16
EXPERTS, INTER = 16, 176
BLOCKS = (2 * N + EXPERTS * (P - 1)) // P
F = 2 * INTER
F3 = F - 2 * P
LN_EPS = 1e-5
RMS_EPS = 1e-6
MASKED = -1e30


class Chain:

    def __init__(self, eng, sem):
        self.eng, self.sem, self.base, self.n = eng, sem, 0, 0

    def begin(self, base):
        self.base, self.n = base, 0

    def __call__(self, ins):
        ins.then_inc(self.sem, 1)
        self.n += 1
        self.eng.wait_ge(self.sem, self.base + self.n)


def after(eng, sem, value):
    if isinstance(value, int) and value <= 0:
        return
    eng.wait_ge(sem, value)


def own_slot(eng, met):
    eng.sem_inc(met, 1)


def f32(ap):
    return ap.bitcast(F32)


def layer_norm(nc, scope, tag, m, xn=None, load=None, split_f32=False, more=()):
    more = dict(more)
    mk = m.inner(scope, tag)
    stats = mk.sb("stats", [P, NT, 6])
    mv = mk.sb("mv", [P, NT, 2])
    veps = mk.sb("veps", [P, NT])
    minus_half = mk.sb("minus_half", [P, NT])
    rstd = mk.sb("rstd", [P, NT])
    xn = mk.sb("xn", [P, NT, E]) if xn is None else xn
    xps = [mk.ps(f"xps{u}", [P, 2, 2 * P]) for u in range(NT // 2)]
    x_in = [mk.sem(f"x_in{u}") for u in range(2)]
    half_set = mk.sem("half_set")
    var_ready = mk.sem("var_ready")
    rstd_ready = mk.sem("rstd_ready")
    xn_ready = mk.sem("xn_ready")
    transposed = mk.sem("transposed")
    hi_ready = mk.sem("hi_ready")
    lo_ready = mk.sem("lo_ready")
    chain_sem = mk.sem("chain")

    with nc.Block() as block:
        if load is not None or "sync" in more:
            @block.sync
            def _(sp):
                if load is not None:
                    for u in range(2):
                        sp.dma_start(m.x[:, 4 * u:4 * u + 4, :], load[:, 4 * u:4 * u + 4, :]).then_inc(x_in[u], 16)
                if "sync" in more:
                    more["sync"](sp)

        @block.gpsimd
        def _(pool):
            nc.gpsimd.memset(minus_half[:], -0.5).then_inc(half_set, 1)
            pool.wait_ge(half_set, 1)
            pool.wait_ge(var_ready, 1)
            nc.gpsimd.tensor_tensor(rstd[:], veps[:], minus_half[:], ALU.pow).then_inc(rstd_ready, 1)
            if "pool" in more:
                more["pool"](pool)

        @block.vector
        def _(dve):
            chain = Chain(dve, chain_sem)
            for t in range(NT):
                if load is not None and t % 4 == 0:
                    dve.wait_ge(x_in[t // 4], 16)
                last = nc.vector.bn_stats(stats[:, t, :], m.x[:, t, :])
            chain(last)
            for t in range(NT):
                last = nc.vector.bn_aggr(mv[:, t, :], stats[:, t, :])
            chain(last)
            nc.vector.tensor_scalar(veps[:], mv[:, :, 1], LN_EPS, None, ALU.add).then_inc(var_ready, 1)
            dve.wait_ge(rstd_ready, 1)
            for t in range(NT):
                nc.vector.tensor_scalar(xn[:, t, :], m.x[:, t, :], mv[:, t, 0:1], rstd[:, t:t + 1],
                                        ALU.subtract, ALU.mult).then_inc(xn_ready, 1)
            for u in range(NT // 2):
                dve.wait_ge(hi_ready, u + 1)
                cols = slice(2 * P * u, 2 * P * (u + 1))
                nc.vector.tensor_tensor(m.xnt_lo[:, :, cols], xps[u][:, :, :], f32(m.xnt_hi[:, :, cols]),
                                        ALU.subtract).then_inc(lo_ready, 1)
            if "vector" in more:
                more["vector"](dve)

        @block.tensor
        def _(pe):
            for u in range(NT // 2):
                pe.wait_ge(xn_ready, 2 * u + 2)
                for e in range(NE):
                    for j in range(2):
                        last = nc.tensor.transpose(xps[u][:, e, j * P:(j + 1) * P],
                                                   xn[:, 2 * u + j, e * P:(e + 1) * P], m.ident[:, :])
                last.then_inc(transposed, 1)

        @block.scalar
        def _(act):
            if "scalar_first" in more:
                more["scalar_first"](act)
            for u in range(NT // 2):
                act.wait_ge(transposed, u + 1)
                cols = slice(2 * P * u, 2 * P * (u + 1))
                if split_f32:
                    nc.scalar.activation(m.xnt[:, :, cols], xps[u][:, :, :], ACT.Copy)
                nc.scalar.activation(m.xnt_hi[:, :, cols], xps[u][:, :, :], ACT.Copy).then_inc(hi_ready, 1)
            if "scalar" in more:
                more["scalar"](act)


def three(nc, out, w_hi, w_lo, x_hi, x_lo, start, stop, **kw):
    nc.tensor.matmul(out, w_hi, x_hi, start=start, stop=False, **kw)
    nc.tensor.matmul(out, w_hi, x_lo, start=False, stop=False, **kw)
    return nc.tensor.matmul(out, w_lo, x_hi, start=False, stop=stop, **kw)


def attention_a(nc, scope, m, x, w_qkv, w_o, q_scale, k_scale, more):
    mk = m.inner(scope, "a")
    sb, ps, sem = mk.sb, mk.ps, mk.sem
    C3 = 3 * DA
    w_raw = [sb(f"w_raw{i}", [P, NE, C3]) for i in range(2)]
    w_hi = sb("w_hi", [P, NE, C3], F32R)
    w_lo = sb("w_lo", [P, NE, C3], F32R)
    wo_raw = sb("wo_raw", [P, HA, E])
    wo_hi = sb("wo_hi", [P, E], F32R)
    wo_lo = sb("wo_lo", [P, E], F32R)
    scales = sb("scales", [P, 2])
    w_in = [sem(f"w_in{i}") for i in range(2)]
    const_in = sem("const_in")
    first_hi = sem("first_hi")
    w_split = sem("w_split")

    def load_first(sp):
        sp.dma_start(w_raw[0][:, :, :], w_qkv[0]).then_inc(w_in[0], 16)
        sp.dma_start(w_raw[1][:, :, :], w_qkv[1]).then_inc(w_in[1], 16)
        sp.dma_start(scales[:, 0:1], q_scale).then_inc(const_in, 16)
        sp.dma_start(scales[:, 1:2], k_scale).then_inc(const_in, 16)
        sp.dma_start(wo_raw[:, :, :], w_o).then_inc(const_in, 16)

    def first_high(act):
        act.wait_ge(w_in[0], 16)
        nc.scalar.activation(w_hi[:, :, :], w_raw[0][:, :, :], ACT.Copy).then_inc(first_hi, 1)

    def first_low(pool):
        pool.wait_ge(first_hi, 1)
        nc.gpsimd.tensor_tensor(w_lo[:, :, :], w_raw[0][:, :, :], f32(w_hi[:, :, :]), ALU.subtract).then_inc(w_split, 1)

    with ExitStack() as inner:
        layer_norm(nc, inner, "ln0", m, load=x,
                   more={"sync": load_first, "scalar_first": first_high, "pool": first_low})

    qkv = sb("qkv", [P, NT, C3])
    junk = sb("junk", [P, DA])
    ssq = sb("ssq", [P, NT, 2])
    msq = sb("msq", [P, NT, 2])
    minus_half = sb("minus_half", [P, NT])
    rrms = sb("rrms", [P, NT, 2])
    qk_hi = [sb(f"qk_hi{i}", [P, 2, N], F32R) for i in range(2)]
    qk_lo = [sb(f"qk_lo{i}", [P, 2, N], F32R) for i in range(2)]
    v_hi = [sb(f"v_hi{i}", [P, NT, DA], F32R) for i in range(2)]
    v_lo = [sb(f"v_lo{i}", [P, NT, DA], F32R) for i in range(2)]
    probs = [sb(f"probs{i}", [P, N]) for i in range(2)]
    pt_hi = [sb(f"pt_hi{i}", [P, NT, 2 * P], F32R) for i in range(2)]
    pt_lo = [sb(f"pt_lo{i}", [P, NT, 2 * P], F32R) for i in range(2)]
    neg_max = sb("neg_max", [P, 2])
    sums = [sb(f"sums{i}", [P, NT]) for i in range(2)]
    rsums = [sb(f"rsums{i}", [P, NT]) for i in range(2)]
    ot_hi = sb("ot_hi", [P, N], F32R)
    ot_lo = sb("ot_lo", [P, N], F32R)

    s_ps = [ps(f"s_ps{i}", [P, N]) for i in range(2)]
    t_ps = [ps(f"t_ps{i}", [P, 4, P]) for i in range(2)]
    pv_ps = ps("pv_ps", [P, 512])
    mm_ps = ps("mm_ps", [P, 512])

    half_set = sem("half_set")
    met = sem("met")
    wo_split = sem("wo_split")
    qkv_mm = sem("qkv_mm")
    qkv_out = sem("qkv_out")
    ms_ready = sem("ms_ready")
    rr_ready = sem("rr_ready")
    qk_scaled = sem("qk_scaled")
    qk_t = sem("qk_t")
    qk_hi_out = sem("qk_hi_out")
    qk_lo_out = sem("qk_lo_out")
    v_hi_out = sem("v_hi_out")
    v_lo_out = sem("v_lo_out")
    s_mm = sem("s_mm")
    s_max = sem("s_max")
    s_exp = sem("s_exp")
    p_t = sem("p_t")
    p_hi_out = sem("p_hi_out")
    p_lo_out = sem("p_lo_out")
    pv_mm = sem("pv_mm")
    o_hi_out = sem("o_hi_out")
    o_lo_out = sem("o_lo_out")
    op_mm = sem("op_mm")
    op_out = sem("op_out")
    rs_ready = sem("rs_ready")
    chain_sem = sem("chain")

    xs_cleared, zeros_set = sem("xs_cleared"), sem("zeros_set")
    zeros = sb("zeros", [P, E])

    PAIRS = HA // 2

    def each_head(eng, head):
        for c in range(2):
            head(c, c, True)
        with eng.Fori(1, PAIRS - 1) as i:
            for c in range(2):
                head(i * 2 + c, c, True)
        head(HA - 2, 0, True)
        head(HA - 1, 1, False)

    def bank_of(p, i):
        return pv_ps if isinstance(p, int) and p == 0 and i % 2 else mm_ps

    with nc.Block() as block:
        @block.sync
        def _(sp):
            more["sync"](sp)
            sp.wait_ge(zeros_set, 1)
            sp.dma_start(m.xs.rearrange("b p c -> p b c"),
                         zeros[:, :].unsqueeze(1).broadcast_to([P, BLOCKS, E])).then_inc(xs_cleared, 16)
            with sp.Fori(1, PAIRS) as i:
                for c in range(2):
                    sp.wait_ge(w_split, i * 2 + (c - 1))
                    sp.dma_start(w_raw[c][:, :, :],
                                 w_qkv[ds(i * 2 + c, 1)].rearrange("a p e c -> (a p) e c")).then_inc(w_in[c], 16)
            sp.wait_ge(xs_cleared, 16)

        @block.gpsimd
        def _(pool):
            def split_w(h, c):
                pool.wait_ge(w_in[c], (h // 2 if isinstance(h, int) else h[0]) * 16 + 16)
                after(pool, qkv_mm, (h if isinstance(h, int) else h[1]) * 8)
                own_slot(pool, met)
                nc.gpsimd.tensor_copy(w_hi[:, :, :], w_raw[c][:, :, :]).then_inc(pool_chain.sem, 1)
                pool_chain.n += 1
                pool.wait_ge(pool_chain.sem, pool_chain.base + pool_chain.n)
                nc.gpsimd.tensor_tensor(w_lo[:, :, :], w_raw[c][:, :, :], f32(w_hi[:, :, :]),
                                        ALU.subtract).then_inc(w_split, 1)

            pool_chain = Chain(pool, half_set)

            def prep_batch(p, b):
                tiles = slice(4 * b, 4 * b + 4)
                pool.wait_ge(ms_ready, p * 2 + (b + 1))
                nc.gpsimd.tensor_tensor(rrms[:, tiles, :].rearrange("p t c -> p (t c)"),
                                        msq[:, tiles, :].rearrange("p t c -> p (t c)"),
                                        minus_half[:, :], ALU.pow).then_inc(rr_ready, 1)
                pool.wait_ge(rr_ready, p * 2 + (b + 1))
                qk = qkv[:, tiles, 0:2 * DA].rearrange("p t (c d) -> p t c d", d=DA)
                nc.gpsimd.tensor_tensor(qk, qk, rrms[:, tiles, :].unsqueeze(3).broadcast_to([P, 4, 2, DA]),
                                        ALU.mult).then_inc(qk_scaled, 1)

            def prep_v(p, c):
                pool.wait_ge(v_hi_out, p + 1)
                nc.gpsimd.tensor_tensor(v_lo[c][:, :, :], qkv[:, :, 2 * DA:C3], f32(v_hi[c][:, :, :]),
                                        ALU.subtract).then_inc(v_lo_out, 1)

            nc.gpsimd.memset(zeros[:, :], 0.0).then_inc(zeros_set, 1)
            nc.gpsimd.memset(minus_half[:], -0.5).then_inc(half_set, 1)
            pool_chain.n = 1
            pool.wait_ge(half_set, 1)
            prep_batch(0, 0)
            prep_batch(0, 1)
            split_w(1, 1)
            prep_v(0, 0)
            pool.wait_ge(const_in, 48)
            base = pool_chain.n

            def split_wo(h):
                after(pool, op_mm, h * 4)
                own_slot(pool, met)
                nc.gpsimd.tensor_copy(wo_hi[:, :], wo_raw[:, ds(h, 1), :].rearrange("p a e -> p (a e)"))\
                    .then_inc(half_set, 1)
                pool_chain.n += 1
                pool.wait_ge(half_set, pool_chain.base + pool_chain.n)
                own_slot(pool, met)
                nc.gpsimd.tensor_tensor(wo_lo[:, :], wo_raw[:, ds(h, 1), :].rearrange("p a e -> p (a e)"),
                                        f32(wo_hi[:, :]), ALU.subtract).then_inc(wo_split, 1)

            def head(h, par, prep, i=None):
                first = isinstance(h, int) and h == 0
                pool_chain.begin(base + h * 2 - (0 if first else 1))
                if not first:
                    split_wo(h - 1)
                if prep:
                    prep_batch(h + 1, 0)
                    prep_batch(h + 1, 1)
                    if not (isinstance(h, int) and h == HA - 2):
                        split_w(h + 2 if isinstance(h, int) else (i + 1, h + 2), par)
                    prep_v(h + 1, 1 - par)

            head(0, 0, True)
            head(1, 1, True)
            with pool.Fori(1, PAIRS - 1) as i:
                for c in range(2):
                    head(i * 2 + c, c, True, i)
            head(HA - 2, 0, True)
            pool_chain.begin(base + (HA - 1) * 2 - 2)
            split_wo(HA - 2)
            pool_chain.begin(base + (HA - 1) * 2 - 1)
            split_wo(HA - 1)
            more["pool"](pool)

        @block.scalar
        def _(act):
            def qkv_tile(p, i):
                act.wait_ge(qkv_mm, p * 8 + (i + 1))
                if i == 0:
                    after(act, qk_t, p * 4)
                    after(act, v_lo_out, p)
                nc.scalar.activation(qkv[:, i, :], bank_of(p, i)[:, 0:C3], ACT.Copy).then_inc(qkv_out, 1)

            def qk_out(p, c, b):
                for r in range(2):
                    act.wait_ge(qk_t, p * 4 + (2 * b + r + 1))
                    if b == 0 and r == 0:
                        after(act, s_mm, (p - 1) * 8)
                    nc.scalar.activation(qk_hi[c][:, r, 512 * b:512 * (b + 1)],
                                         t_ps[r][:, :, :].rearrange("p a b -> p (a b)"), ACT.Copy,
                                         scale=scales[:, r:r + 1]).then_inc(qk_hi_out, 1)

            def v_out(p, c):
                act.wait_ge(qkv_out, p * 8 + 8)
                after(act, pv_mm, (p - 1) * 8)
                nc.scalar.activation(v_hi[c][:, :, :], qkv[:, :, 2 * DA:C3], ACT.Copy).then_inc(v_hi_out, 1)

            def exp_of(g, q, c, t):
                act.wait_ge(s_max, g + 1)
                after(act, p_t, g * 2 - 2)
                if t == 0:
                    after(act, rs_ready, (g - 8) // 8 if isinstance(g, int) else rs_before[0])
                nc.scalar.activation(probs[q][:, :], s_ps[q][:, :], ACT.Exp, bias=neg_max[:, q:q + 1],
                                     accum_out=sums[c][:, t:t + 1]).then_inc(s_exp, 1)

            rs_before = [None]

            def pt_out(g, t):
                J = t // 2
                for a in range(2):
                    act.wait_ge(p_t, g * 2 + (a + 1))
                    if t % 2 == 0 and a == 0:
                        after(act, pv_mm, g - 2)
                    nc.scalar.activation(pt_hi[J % 2][:, 4 * a:4 * a + 4, (t % 2) * P:(t % 2 + 1) * P],
                                         t_ps[a][:, :, :], ACT.Copy).then_inc(p_hi_out, 1)

            def o_out(J, j):
                act.wait_ge(pv_mm, J * 2 + 2)
                after(act, op_mm, J - 3)
                nc.scalar.activation(ot_hi[:, 2 * P * j:2 * P * (j + 1)], pv_ps[:, 0:2 * P], ACT.Copy)\
                    .then_inc(o_hi_out, 1)

            def head(h, par, prep):
                static = isinstance(h, int)
                for t in range(NT):
                    g = h * 8 + t
                    first = static and h == 0
                    if prep and t < 4:
                        qkv_tile(h + 1, 2 * t)
                    if not (first and t == 0):
                        pt_out(g - 1, (t - 1) % NT)
                    if t < NT - 1 or prep:
                        rs_before[0] = h
                        nt = (t + 1) % NT
                        exp_of(g + 1, (t + 1) % 2, par if t < NT - 1 else 1 - par, nt)
                    if prep and t < 4:
                        qkv_tile(h + 1, 2 * t + 1)
                    if t % 2 == 0 and not (first and t < 4):
                        j = (t // 2 + 2) % 4
                        o_out(h * 4 + (t // 2 - 2), j)
                    if prep and t in (3, 5):
                        qk_out(h + 1, 1 - par, (t - 3) // 2)
                    if prep and t == 4:
                        v_out(h + 1, 1 - par)

            act.wait_ge(const_in, 48)
            for i in range(NT):
                qkv_tile(0, i)
            for b in range(2):
                qk_out(0, 0, b)
            v_out(0, 0)
            exp_of(0, 0, 0, 0)
            each_head(act, head)
            pt_out(8 * HA - 1, NT - 1)
            o_out(4 * HA - 2, 2)
            o_out(4 * HA - 1, 3)

        @block.vector
        def _(dve):
            chain = Chain(dve, chain_sem)

            def squares(p, i):
                dve.wait_ge(qkv_out, p * 8 + (i + 1))
                for r in range(2):
                    qk = qkv[:, i, r * DA:(r + 1) * DA]
                    last = nc.vector.tensor_tensor_reduce(out=junk[:, :], in0=qk, in1=qk, scale=1.0, scalar=0.0,
                                                          op0=ALU.mult, op1=ALU.add,
                                                          accum_out=ssq[:, i, r:r + 1])
                    chain(last)

            def mean_squares(p, b):
                tiles = slice(4 * b, 4 * b + 4)
                nc.vector.tensor_scalar(msq[:, tiles, :], ssq[:, tiles, :], 1.0 / DA, RMS_EPS,
                                        ALU.mult, ALU.add).then_inc(ms_ready, 1)

            def qk_out(p, c, b):
                for r in range(2):
                    dve.wait_ge(qk_hi_out, p * 4 + (2 * b + r + 1))
                    cols = slice(512 * b, 512 * (b + 1))
                    nc.vector.scalar_tensor_tensor(
                        out=qk_lo[c][:, r, cols], in0=t_ps[r][:, :, :].rearrange("p a b -> p (a b)"),
                        scalar=scales[:, r:r + 1], in1=f32(qk_hi[c][:, r, cols]),
                        op0=ALU.mult, op1=ALU.subtract).then_inc(qk_lo_out, 1)

            def max_of(g, q):
                dve.wait_ge(s_mm, g + 1)
                after(dve, s_exp, g - 1)
                nc.vector.tensor_reduce(neg_max[:, q:q + 1], s_ps[q][:, :], AX.X, ALU.max,
                                        negate=True).then_inc(s_max, 1)

            def pt_out(g, t):
                for a in range(2):
                    dve.wait_ge(p_hi_out, g * 2 + (a + 1))
                    where = (slice(None), slice(4 * a, 4 * a + 4), slice((t % 2) * P, (t % 2 + 1) * P))
                    nc.vector.tensor_tensor(pt_lo[t // 2 % 2][where], t_ps[a][:, :, :],
                                            f32(pt_hi[t // 2 % 2][where]), ALU.subtract).then_inc(p_lo_out, 1)

            def o_out(J, j):
                dve.wait_ge(o_hi_out, J + 1)
                cols = slice(2 * P * j, 2 * P * (j + 1))
                nc.vector.tensor_tensor(ot_lo[:, cols], pv_ps[:, 0:2 * P], f32(ot_hi[:, cols]),
                                        ALU.subtract).then_inc(o_lo_out, 1)

            def invert(h, c):
                dve.wait_ge(s_exp, h * 8 + 8)
                nc.vector.reciprocal(rsums[c][:, :], sums[c][:, :]).then_inc(rs_ready, 1)
                dve.wait_ge(rs_ready, h + 1)

            def project(h, c, j):
                dve.wait_ge(op_mm, h * 4 + (j + 1))
                for k in range(2):
                    t = 2 * j + k
                    last = nc.vector.scalar_tensor_tensor(
                        out=m.x[:, t, :], in0=mm_ps[:, k * E:(k + 1) * E], scalar=rsums[c][:, t:t + 1],
                        in1=m.x[:, t, :], op0=ALU.mult, op1=ALU.add)
                last.then_inc(op_out, 1)

            def head(h, par, prep):
                first = isinstance(h, int) and h == 0
                chain.begin(base + h * 16)
                for t in range(NT):
                    g = h * 8 + t
                    if t < NT - 1 or prep:
                        max_of(g + 1, (t + 1) % 2)
                    if t >= 4 and not first:
                        project(h - 1, 1 - par, t - 4)
                    if prep and t < 4:
                        squares(h + 1, 2 * t)
                    if not (first and t == 0):
                        pt_out(g - 1, (t - 1) % NT)
                    if t == 0 and not first:
                        invert(h - 1, 1 - par)
                    if prep and t < 4:
                        squares(h + 1, 2 * t + 1)
                        if t % 2:
                            mean_squares(h + 1, t // 2)
                    if t % 2 == 0 and not (first and t < 4):
                        o_out(h * 4 + (t // 2 - 2), (t // 2 + 2) % 4)
                    if prep and t in (3, 5):
                        qk_out(h + 1, 1 - par, (t - 3) // 2)

            for i in range(NT):
                squares(0, i)
                if i % 4 == 3:
                    mean_squares(0, i // 4)
            for b in range(2):
                qk_out(0, 0, b)
            max_of(0, 0)
            base = chain.n
            each_head(dve, head)
            pt_out(8 * HA - 1, NT - 1)
            o_out(4 * HA - 2, 2)
            o_out(4 * HA - 1, 3)
            invert(HA - 1, 1)
            for j in range(4):
                project(HA - 1, 1, j)

        @block.tensor
        def _(pe):
            def qkv_tile(p, i):
                if i == 0:
                    pe.wait_ge(w_split, p + 1)
                    after(pe, op_out, (p - 2) * 4)
                    after(pe, qkv_out, p * 8)
                elif isinstance(p, int) and p == 0:
                    after(pe, qkv_out, i - 1)
                else:
                    pe.wait_ge(qkv_out, p * 8 + i)
                for e in range(NE):
                    rows = slice(i * P, (i + 1) * P)
                    last = three(nc, bank_of(p, i)[:, 0:C3], m.xnt_hi[:, e, rows], m.xnt_lo[:, e, rows],
                                 w_hi[:, e, :], w_lo[:, e, :], e == 0, e == NE - 1)
                last.then_inc(qkv_mm, 1)

            def qk_batch(p, b, g):
                pe.wait_ge(qk_scaled, p * 2 + (b + 1))
                for r in range(2):
                    if g is None:
                        after(pe, qk_lo_out, p * 4 + 2 * (b - 1) + r + 1)
                    else:
                        pe.wait_ge(p_lo_out, g * 2 + (r + 1))
                    for i in range(4):
                        last = nc.tensor.transpose(t_ps[r][:, i, :], qkv[:, 4 * b + i, r * DA:(r + 1) * DA],
                                                   m.ident[:, :])
                    last.then_inc(qk_t, 1)

            def scores(g, t, c):
                after(pe, s_exp, g - 1)
                for half in range(2):
                    cols = slice(512 * half, 512 * (half + 1))
                    rows = slice(t * P, (t + 1) * P)
                    last = three(nc, s_ps[t % 2][:, cols], qk_hi[c][:, 0, rows], qk_lo[c][:, 0, rows],
                                 qk_hi[c][:, 1, cols], qk_lo[c][:, 1, cols], True, True)
                last.then_inc(s_mm, 1)

            def transpose_p(g, t, qk_before):
                pe.wait_ge(s_exp, g + 1)
                for a in range(2):
                    after(pe, p_lo_out, g * 2 + (a - 1))
                    if qk_before is not None:
                        pe.wait_ge(qk_lo_out, qk_before + a)
                    for k in range(4):
                        kb = 4 * a + k
                        last = nc.tensor.transpose(t_ps[a][:, k, :], probs[t % 2][:, kb * P:(kb + 1) * P],
                                                   m.ident[:, :])
                    last.then_inc(p_t, 1)

            def pv_half(J, j, a, c):
                if a == 0:
                    pe.wait_ge(p_lo_out, J * 4 + 4)
                    after(pe, o_lo_out, J)
                    if j == 0:
                        pe.wait_ge(v_lo_out, pv_head[0] + 1)
                for k in range(4):
                    kb = 4 * a + k
                    last = three(nc, pv_ps[:, 0:2 * P], v_hi[c][:, kb, :], v_lo[c][:, kb, :],
                                 pt_hi[j % 2][:, kb, :], pt_lo[j % 2][:, kb, :], kb == 0, kb == NT - 1)
                last.then_inc(pv_mm, 1)

            pv_head = [0]

            def project(h, j):
                if j == 0:
                    pe.wait_ge(wo_split, h + 1)
                pe.wait_ge(o_lo_out, h * 4 + (j + 1))
                after(pe, op_out, h * 4 + j)
                for k in range(2):
                    rows = slice((2 * j + k) * P, (2 * j + k + 1) * P)
                    last = three(nc, mm_ps[:, k * E:(k + 1) * E], ot_hi[:, rows], ot_lo[:, rows],
                                 wo_hi[:, :], wo_lo[:, :], True, True)
                last.then_inc(op_mm, 1)

            def head(h, par, prep):
                first = isinstance(h, int) and h == 0
                for t in range(NT):
                    g = h * 8 + t
                    if t < NT - 1:
                        scores(g + 1, t + 1, par)
                    elif prep:
                        pe.wait_ge(qk_lo_out, h * 4 + 8)
                        scores(g + 1, 0, 1 - par)
                    if prep and t < 4:
                        qkv_tile(h + 1, 2 * t)
                    if t >= 4 and not first:
                        if t == 4 and prep:
                            pe.wait_ge(qkv_out, h * 8 + 16)
                        project(h - 1, t - 4)
                    if not (first and t == 0):
                        between = None
                        if t in (4, 6) and prep:
                            between = (h + 1) * 4 + (t - 3)
                        transpose_p(g - 1, (t - 1) % NT, between)
                    if not (first and t < 3):
                        s = t - 3
                        j = (s // 2) % 4
                        pv_head[0] = h if s >= 0 else h - 1
                        pv_half(h * 4 + s // 2, j, s % 2, par if s >= 0 else 1 - par)
                    if prep and t < 4:
                        qkv_tile(h + 1, 2 * t + 1)
                    if prep and t in (3, 5):
                        qk_batch(h + 1, (t - 3) // 2, g - 1)

            for i in range(NT):
                qkv_tile(0, i)
            for b in range(2):
                qk_batch(0, b, None)
            pe.wait_ge(qk_lo_out, 4)
            scores(0, 0, 0)
            each_head(pe, head)
            transpose_p(8 * HA - 1, NT - 1, None)
            pv_head[0] = HA - 1
            pv_half(4 * HA - 2, 2, 1, 1)
            pv_half(4 * HA - 1, 3, 0, 1)
            pv_half(4 * HA - 1, 3, 1, 1)
            for j in range(4):
                project(HA - 1, j)


def mixture(nc, scope, tag, m, w13, w2a, w2b, shared, more=(), store=None):
    more = dict(more)
    mk = m.inner(scope, tag)
    sb, ps, sem = mk.sb, mk.ps, mk.sem
    w13_sb = sb("w13_sb", [P, EXPERTS, NE, 2 * INTER])
    w2_sb = sb("w2_sb", [P, EXPERTS, 2, E])
    xn = sb("xn", [P, NT, E])
    w_in, w2_zero = sem("w_in"), sem("w2_zero")
    R2 = INTER - P

    def load_weights(sp):
        if "sync" in more:
            more["sync"](sp)
        for c in range(4):
            es = slice(4 * c, 4 * c + 4)
            sp.dma_start(w13_sb[:, es, :, :], w13[:, es]).then_inc(w_in, 16)
        sp.dma_start(w2_sb[:, :, 0, :], w2a).then_inc(w_in, 16)
        sp.wait_ge(w2_zero, 1)
        sp.dma_start(w2_sb[0:R2, :, 1, :], w2b).then_inc(w_in, 16)

    def zero_rows(pool):
        nc.gpsimd.memset(w2_sb[:, :, 1, :], 0.0).then_inc(w2_zero, 1)

    with ExitStack() as inner:
        layer_norm(nc, inner, f"{tag}_ln", m, xn=xn, split_f32=True, more={"sync": load_weights, "pool": zero_rows})

    G = [P, NT, EXPERTS]
    shifted, prob = sb("shifted", G), sb("prob", G)
    rank = sb("rank", [P, EXPERTS])
    hit, pick = sb("hit", G), [sb(f"pick{i}", G) for i in range(2)]
    chosen = sb("chosen", G, BF16)
    top = [sb(f"top{i}", [P, NT]) for i in range(2)]
    total, rtotal, key = sb("total", [P, NT]), sb("rtotal", [P, NT]), sb("key", [P, NT])
    slot = [sb(f"slot{i}", [P, NT]) for i in range(2)]
    slot_i = [sb(f"slot_i{i}", [P, NT], I32) for i in range(2)]
    steps = sb("steps", [P, NT])
    over = sb("over", [P, EXPERTS, NT])
    used = sb("used", [P, EXPERTS])
    scan = [sb(f"scan{i}", [P, 2 * EXPERTS]) for i in range(2)]
    base = sb("base", [P, EXPERTS])
    count_b = sb("count_b", [1, BLOCKS, EXPERTS])
    owner = sb("owner", [1, BLOCKS])
    owner_i = sb("owner_i", [1, BLOCKS], I32)

    xg = [sb(f"xg{i}", [P, E]) for i in range(4)]
    xt = [sb(f"xt{i}", [P, NE, P]) for i in range(2)]
    hid_b = [sb(f"hid_b{i}", [P, 2 * P]) for i in range(2)]
    ht_b = [sb(f"ht_b{i}", [P, 2, P]) for i in range(2)]
    y_b = [sb(f"y_b{i}", [P, E]) for i in range(2)]
    back = [xn, sb("back", [P, NT, E])]
    gated = [sb(f"gated{i}", [P, F]) for i in range(2)]
    act_b = [g[:, 0:INTER] for g in gated]
    hidden = [sb(f"hidden{i}", [P, 3 * P]) for i in range(2)]
    ht_hi = [sb(f"ht_hi{i}", [P, 3, P], F32R) for i in range(2)]
    ht_lo = [sb(f"ht_lo{i}", [P, 3, P], F32R) for i in range(2)]

    u_ps = [ps(f"u_ps{i}", [P, 512]) for i in range(2)]
    x_ps = [ps(f"x_ps{i}", [P, 512]) for i in range(2)]
    h_ps = [ps(f"h_ps{i}", [P, 512]) for i in range(2)]
    y_ps = [ps(f"y_ps{i}", [P, 512]) for i in range(2)]

    consts, logits, less_max, exped = sem("consts"), sem("logits"), sem("less_max"), sem("exped")
    chosen_set, counted, slots_set, owners_set = sem("chosen_set"), sem("counted"), sem("slots_set"), sem("owners_set")
    scattered = sem("scattered")
    gathered = [sem(f"gathered{i}") for i in range(2)]
    xg_in = [sem(f"xg_in{i}") for i in range(4)]
    b_xt, b_xt_out, b_up, b_silu, b_hid = sem("b_xt"), sem("b_xt_out"), sem("b_up"), sem("b_silu"), sem("b_hid")
    b_ht, b_ht_out, b_y, b_y_out = sem("b_ht"), sem("b_ht_out"), sem("b_y"), sem("b_y_out")
    b_stored = [sem(f"b_stored{i}") for i in range(2)]
    a_mm, b_mm, silu_out, h_out, h_t = sem("a_mm"), sem("b_mm"), sem("silu_out"), sem("h_out"), sem("h_t")
    h_hi_out, h_lo_out, y_mm, y_out = sem("h_hi_out"), sem("h_lo_out"), sem("y_mm"), sem("y_out")
    x_out, stored, chain_sem = sem("x_out"), sem("stored"), sem("chain")
    EARLY = 5

    def bc(ap):
        return ap.unsqueeze(2).broadcast_to(G)

    def steps_of_blocks(eng, step):
        fours = (BLOCKS - 5) // 4
        step(1, 1)
        step(2, 2)
        with eng.Fori(0, fours) as i:
            for k in range(3, 7):
                step(i * 4 + k, k % 4)
        for b in range(3 + 4 * fours, BLOCKS - 2):
            step(b, b % 4)

    with nc.Block() as block:
        @block.sync
        def _(sp):
            def load(b, c):
                src = m.xs[ds(b, 1)].rearrange("a p c -> (a p) c")
                sp.dma_start(xg[c][:, :], src).then_inc(xg_in[c], 16)

            def save(b, c):
                c %= 2
                sp.wait_ge(b_y_out, b + 1)
                dst = m.ys[ds(b, 1)].rearrange("a p c -> (a p) c")
                sp.dma_start(dst, y_b[c][:, :]).then_inc(b_stored[c], 16)

            sp.wait_ge(scattered, 16 * 2 * NT)
            for b in range(4):
                load(b, b)
            sp.wait_ge(b_xt, 1)
            load(4, 0)

            def step(b, c):
                if not (isinstance(b, int) and b + 4 >= BLOCKS):
                    sp.wait_ge(b_xt, b + 1)
                    load(b + 4, c)
                save(b - 1, (c + 3) % 4)

            steps_of_blocks(sp, step)
            for b in range(BLOCKS - 3, BLOCKS):
                save(b, b % 2)
            if store is not None:
                for t in range(NT):
                    sp.wait_ge(x_out, t + 1)
                    sp.dma_start(store[:, t, :], m.x[:, t, :]).then_inc(stored, 16)
                sp.wait_ge(stored, 16 * NT)

        @block.gpsimd
        def _(pool):
            for i in range(2):
                nc.gpsimd.memset(hidden[i][:, F:3 * P], 0.0)
                nc.gpsimd.memset(hid_b[i][:, INTER:2 * P], 0.0)
                nc.gpsimd.memset(scan[i][:, 0:EXPERTS], 0.0)
            for e in range(EXPERTS):
                nc.gpsimd.memset(rank[:, e:e + 1], float(EXPERTS - e))
            for j in range(NT):
                nc.gpsimd.memset(steps[:, j:j + 1], float(P * j))
            for b in range(BLOCKS):
                last = nc.gpsimd.memset(count_b[:, b, :], float(b))
            last.then_inc(consts, 1)
            if "pool" in more:
                more["pool"](pool)
            pool.wait_ge(slots_set, 1)
            for t in range(NT):
                for i in range(2):
                    nc.gpsimd.indirect_dma_start(m.xs.rearrange("b p c -> (b p) c"),
                                                 bass.IndirectOffsetOnAxis(ap=slot_i[i][:, t:t + 1], axis=0),
                                                 xn[:, t, :], None).then_inc(scattered, 16)
            pool.wait_ge(b_stored[0], 16 * ((BLOCKS + 1) // 2))
            pool.wait_ge(b_stored[1], 16 * (BLOCKS // 2))
            for t in range(NT):
                for i in range(2):
                    nc.gpsimd.indirect_dma_start(back[i][:, t, :], None, m.ys.rearrange("b p c -> (b p) c"),
                                                 bass.IndirectOffsetOnAxis(ap=slot_i[i][:, t:t + 1], axis=0))\
                        .then_inc(gathered[t // 4], 16)

        @block.scalar
        def _(act):
            act.wait_ge(less_max, 1)
            nc.scalar.activation(prob[:, :, :], shifted[:, :, :], ACT.Exp).then_inc(exped, 1)

            def shared_tile(t):
                act.wait_ge(a_mm, t + 1)
                after(act, h_out, t - 1)
                nc.scalar.activation(gated[t % 2][:, :], u_ps[0][:, 0:F], ACT.Silu).then_inc(silu_out, 1)
                act.wait_ge(h_t, t + 1)
                after(act, y_mm, t - 1)
                nc.scalar.activation(ht_hi[t % 2][:, :, :].rearrange("p a b -> p (a b)"), h_ps[0][:, 0:3 * P],
                                     ACT.Copy).then_inc(h_hi_out, 1)

            for t in range(EARLY):
                shared_tile(t)
            if "scalar" in more:
                more["scalar"](act)

            def xt_out(b, c):
                c %= 2
                act.wait_ge(b_xt, b + 1)
                after(act, b_up, b - 1)
                nc.scalar.activation(xt[c][:, :, :].rearrange("p a b -> p (a b)"), x_ps[c][:, 0:E], ACT.Copy)\
                    .then_inc(b_xt_out, 1)

            def silu(b, c):
                c %= 2
                act.wait_ge(b_up, b + 1)
                after(act, b_hid, b - 1)
                nc.scalar.activation(act_b[c], u_ps[c][:, 0:INTER], ACT.Silu).then_inc(b_silu, 1)

            def y_of(b, c):
                c %= 2
                act.wait_ge(b_y, b + 1)
                if not (isinstance(b, int) and b < 2):
                    act.wait_ge(b_stored[c], stored_before(b, c))
                nc.scalar.activation(y_b[c][:, :], y_ps[c][:, 0:E], ACT.Copy).then_inc(b_y_out, 1)

            def stored_before(b, c):
                return 16 * (b // 2) if isinstance(b, int) else (b - c) * 8

            xt_out(0, 0)
            xt_out(1, 1)
            silu(0, 0)

            silu(1, 1)
            xt_out(2, 0)

            def step(b, c):
                silu(b + 1, (c + 1) % 4)
                xt_out(b + 2, (c + 2) % 4)
                y_of(b - 1, (c + 3) % 4)

            steps_of_blocks(act, step)
            b = BLOCKS - 2
            silu(b + 1, (b + 1) % 2)
            y_of(b - 1, (b - 1) % 2)
            y_of(b, b % 2)
            y_of(b + 1, (b + 1) % 2)
            for t in range(EARLY, NT):
                shared_tile(t)

        @block.vector
        def _(dve):
            chain = Chain(dve, chain_sem)
            V = nc.vector
            dve.wait_ge(logits, 1)
            lg = x_ps[0][:, 0:NT * EXPERTS].rearrange("p (t e) -> p t e", e=EXPERTS)
            chain(V.tensor_reduce(key[:, :], lg, AX.X, ALU.max))
            V.tensor_tensor(shifted[:, :, :], lg, bc(key[:, :]), ALU.subtract).then_inc(less_max, 1)
            dve.wait_ge(exped, 1)
            chain(V.tensor_reduce(total[:, :], prob[:, :, :], AX.X, ALU.add))
            chain(V.reciprocal(rtotal[:, :], total[:, :]))
            chain(V.tensor_tensor(prob[:, :, :], prob[:, :, :], bc(rtotal[:, :]), ALU.mult))
            dve.wait_ge(consts, 1)

            def choose(scores, i):
                chain(V.tensor_reduce(top[i][:, :], scores[:, :, :], AX.X, ALU.max))
                chain(V.tensor_tensor(hit[:, :, :], scores[:, :, :], bc(top[i][:, :]), ALU.is_equal))
                chain(V.tensor_tensor(hit[:, :, :], hit[:, :, :],
                                      rank[:, :].unsqueeze(1).broadcast_to(G), ALU.mult))
                chain(V.tensor_reduce(key[:, :], hit[:, :, :], AX.X, ALU.max))
                chain(V.tensor_tensor(pick[i][:, :, :], hit[:, :, :], bc(key[:, :]), ALU.is_equal))

            choose(prob, 0)
            chain(V.scalar_tensor_tensor(out=shifted[:, :, :], in0=pick[0][:, :, :], scalar=-2.0,
                                         in1=prob[:, :, :], op0=ALU.mult, op1=ALU.add))
            choose(shifted, 1)
            V.tensor_tensor(chosen[:, :, :], pick[0][:, :, :], pick[1][:, :, :], ALU.add).then_inc(chosen_set, 1)

            dve.wait_ge(counted, 1)
            earlier = x_ps[1][:, 0:NT * EXPERTS].rearrange("p (t e) -> p t e", e=EXPERTS)
            counts = x_ps[1][:, NT * EXPERTS:NT * EXPERTS + EXPERTS]
            chain(V.tensor_tensor(over[:, :, :], counts.unsqueeze(2).broadcast_to([P, EXPERTS, NT]),
                                  steps[:, :].unsqueeze(1).broadcast_to([P, EXPERTS, NT]), ALU.is_gt))
            chain(V.tensor_reduce(used[:, :], over[:, :, :], AX.X, ALU.add))
            chain(V.tensor_copy(scan[0][:, EXPERTS:2 * EXPERTS], used[:, :]))
            for k in range(4):
                a, b, s = scan[k % 2], scan[(k + 1) % 2], 1 << k
                chain(V.tensor_tensor(b[:, EXPERTS:2 * EXPERTS], a[:, EXPERTS:2 * EXPERTS],
                                      a[:, EXPERTS - s:2 * EXPERTS - s], ALU.add))
            ends = scan[0][:, EXPERTS:2 * EXPERTS]
            chain(V.tensor_tensor(base[:, :], ends, used[:, :], ALU.subtract))
            chain(V.scalar_tensor_tensor(out=prob[:, :, :], in0=base[:, :].unsqueeze(1).broadcast_to(G),
                                         scalar=float(P), in1=earlier, op0=ALU.mult, op1=ALU.add))
            for i in range(2):
                chain(V.tensor_tensor(hit[:, :, :], prob[:, :, :], pick[i][:, :, :], ALU.mult))
                chain(V.tensor_reduce(slot[i][:, :], hit[:, :, :], AX.X, ALU.add))
                last = V.tensor_copy(slot_i[i][:, :], slot[i][:, :])
                if i == 0:
                    chain(last)
            last.then_inc(slots_set, 1)

            chain(V.tensor_tensor(count_b[:, :, :], ends[0:1, :].unsqueeze(1).broadcast_to([1, BLOCKS, EXPERTS]),
                                  count_b[:, :, :], ALU.is_le))
            chain(V.tensor_reduce(owner[:, :], count_b[:, :, :], AX.X, ALU.add))
            V.tensor_scalar(owner_i[:, :], owner[:, :], float(EXPERTS - 1), None, ALU.min).then_inc(owners_set, 1)

            def shared_tile(t):
                q = t % 2
                dve.wait_ge(silu_out, t + 1)
                dve.wait_ge(b_mm, t + 1)
                after(dve, h_t, t - 1)
                V.tensor_tensor(hidden[q][:, 0:F], gated[q][:, :], u_ps[1][:, 0:F], ALU.mult).then_inc(h_out, 1)
                dve.wait_ge(h_hi_out, t + 1)
                V.tensor_tensor(ht_lo[q][:, :, :].rearrange("p a b -> p (a b)"), h_ps[0][:, 0:3 * P],
                                f32(ht_hi[q][:, :, :]).rearrange("p a b -> p (a b)"),
                                ALU.subtract).then_inc(h_lo_out, 1)

            def shared_add(t):
                dve.wait_ge(y_mm, t + 1)
                V.tensor_tensor(m.x[:, t, :], m.x[:, t, :], y_ps[t % 2][:, 0:E], ALU.add).then_inc(y_out, 1)

            for t in range(EARLY):
                shared_tile(t)
                if t:
                    shared_add(t - 1)
            shared_add(EARLY - 1)
            if "vector" in more:
                more["vector"](dve)

            def hid(b, c):
                c %= 2
                dve.wait_ge(b_silu, b + 1)
                after(dve, b_ht, b - 1)
                V.tensor_tensor(hid_b[c][:, 0:INTER], act_b[c], u_ps[c][:, INTER:2 * INTER],
                                ALU.mult).then_inc(b_hid, 1)

            def ht_of(b, c):
                c %= 2
                dve.wait_ge(b_ht, b + 1)
                after(dve, b_y, b - 1)
                V.tensor_copy(ht_b[c][:, :, :].rearrange("p a b -> p (a b)"), h_ps[c][:, 0:2 * P])\
                    .then_inc(b_ht_out, 1)

            hid(0, 0)
            ht_of(0, 0)
            hid(1, 1)

            def step(b, c):
                ht_of(b, c)
                hid(b + 1, (c + 1) % 4)

            steps_of_blocks(dve, step)
            step(BLOCKS - 2, (BLOCKS - 2) % 2)
            ht_of(BLOCKS - 1, (BLOCKS - 1) % 2)
            for t in range(EARLY, NT):
                shared_tile(t)
                if t > EARLY:
                    shared_add(t - 1)
            shared_add(NT - 1)
            dve.wait_ge(y_out, NT)
            for t in range(NT):
                dve.wait_ge(gathered[t // 4], 16 * 8)
                for i in range(2):
                    last = V.scalar_tensor_tensor(out=m.x[:, t, :], in0=back[i][:, t, :], scalar=top[i][:, t:t + 1],
                                                  in1=m.x[:, t, :], op0=ALU.mult, op1=ALU.add)
                    if i == 0:
                        chain(last)
                last.then_inc(x_out, 1)

        @block.tensor
        def _(pe):
            for t in range(NT):
                for e in range(NE):
                    last = nc.tensor.matmul(x_ps[0][:, t * EXPERTS:(t + 1) * EXPERTS],
                                            m.xnt[:, e, t * P:(t + 1) * P], shared.gate[:, e, :],
                                            start=e == 0, stop=e == NE - 1)
            last.then_inc(logits, 1)

            def count():
                pe.wait_ge(chosen_set, 1)
                out = x_ps[1]
                W = NT * EXPERTS
                ch = chosen[:, :, :].rearrange("p t e -> p (t e)")
                nc.tensor.matmul(out[:, 0:W], m.before[:, :], ch, start=True, stop=False, skip_group_check=True)
                for s in range(1, NT):
                    nc.tensor.matmul(out[:, s * EXPERTS:W], m.ones_bf[:, :], ch[:, 0:W - s * EXPERTS],
                                     start=False, stop=False, skip_group_check=True)
                for t in range(NT):
                    last = nc.tensor.matmul(out[:, W:W + EXPERTS], m.ones_bf[:, :],
                                            ch[:, t * EXPERTS:(t + 1) * EXPERTS],
                                            start=False, stop=t == NT - 1, skip_group_check=True)
                last.then_inc(counted, 1)

            def shared_up(t):
                rows = slice(t * P, (t + 1) * P)
                if t == EARLY:
                    pe.wait_ge(b_hid, BLOCKS)
                for i, free, done in ((0, silu_out, a_mm), (1, h_out, b_mm)):
                    after(pe, free, t)
                    for e in range(NE):
                        last = three(nc, u_ps[i][:, 0:F], m.xnt_hi[:, e, rows], m.xnt_lo[:, e, rows],
                                     shared.hi13[:, e, i * F:(i + 1) * F], shared.lo13[:, e, i * F:(i + 1) * F],
                                     e == 0, e == NE - 1)
                    last.then_inc(done, 1)

            def shared_ht(t):
                pe.wait_ge(h_out, t + 1)
                after(pe, h_lo_out, t)
                if t == EARLY:
                    pe.wait_ge(b_ht_out, BLOCKS)
                for k in range(3):
                    last = nc.tensor.transpose(h_ps[0][:, k * P:(k + 1) * P], hidden[t % 2][:, k * P:(k + 1) * P],
                                               m.ident[:, :])
                last.then_inc(h_t, 1)

            def shared_down(t):
                pe.wait_ge(h_lo_out, t + 1)
                after(pe, y_out, t - 1)
                if t == EARLY:
                    pe.wait_ge(b_y_out, BLOCKS)
                q = t % 2
                for k in range(3):
                    r = P if k < 2 else F3
                    last = three(nc, y_ps[q][:, 0:E], ht_hi[q][0:r, k, :], ht_lo[q][0:r, k, :],
                                 shared.hi2[0:r, k, :], shared.lo2[0:r, k, :], k == 0, k == 2)
                last.then_inc(y_mm, 1)

            def shared_tiles(t0, t1, between):
                for t in range(t0, t1):
                    shared_up(t)
                    if t > t0:
                        shared_down(t - 1)
                    if t == t0:
                        between()
                    shared_ht(t)
                shared_down(t1 - 1)

            shared_tiles(0, EARLY, count)

            def expert_of(b):
                return pe.value_load(owner_i[0:1, b:b + 1] if isinstance(b, int) else owner_i[0:1, ds(b, 1)],
                                     min_val=0, max_val=EXPERTS - 1)

            def x_t(b, c):
                pe.wait_ge(xg_in[c], 16 * (b // 4) + 16 if isinstance(b, int) else (b - c) * 4 + 16)
                after(pe, b_xt_out, b - 1)
                for e in range(NE):
                    last = nc.tensor.transpose(x_ps[c % 2][:, e * P:(e + 1) * P], xg[c][:, e * P:(e + 1) * P], m.ident[:, :])
                last.then_inc(b_xt, 1)

            def up(b, c):
                c %= 2
                e = expert_of(b)
                pe.wait_ge(b_xt_out, b + 1)
                after(pe, b_hid, b - 1)
                for k in range(NE):
                    w = w13_sb[:, ds(e, 1), k, :].rearrange("p a c -> p (a c)")
                    last = nc.tensor.matmul(u_ps[c][:, 0:2 * INTER], xt[c][:, k, :], w, start=k == 0, stop=k == NE - 1)
                last.then_inc(b_up, 1)

            def h_tr(b, c):
                c %= 2
                pe.wait_ge(b_hid, b + 1)
                after(pe, b_ht_out, b - 1)
                for k in range(2):
                    last = nc.tensor.transpose(h_ps[c][:, k * P:(k + 1) * P], hid_b[c][:, k * P:(k + 1) * P], m.ident[:, :])
                last.then_inc(b_ht, 1)

            def down(b, c):
                c %= 2
                e = expert_of(b)
                pe.wait_ge(b_ht_out, b + 1)
                after(pe, b_y_out, b - 1)
                for k in range(2):
                    w = w2_sb[:, ds(e, 1), k, :].rearrange("p a c -> p (a c)")
                    last = nc.tensor.matmul(y_ps[c][:, 0:E], ht_b[c][:, k, :], w, start=k == 0, stop=k == 1)
                last.then_inc(b_y, 1)

            pe.wait_ge(owners_set, 1)
            pe.wait_ge(w_in, 16 * 6)
            pe.wait_ge(h_lo_out, EARLY)
            pe.wait_ge(y_out, EARLY)
            x_t(0, 0)
            x_t(1, 1)
            up(0, 0)
            up(1, 1)
            x_t(2, 2)
            h_tr(0, 0)

            def step(b, c):
                up(b + 1, (c + 1) % 4)
                x_t(b + 2, (c + 2) % 4)
                down(b - 1, (c + 3) % 4)
                h_tr(b, c)

            steps_of_blocks(pe, step)
            b = BLOCKS - 2
            up(b + 1, (b + 1) % 2)
            down(b - 1, (b - 1) % 2)
            h_tr(b, b % 2)
            down(b, b % 2)
            h_tr(b + 1, (b + 1) % 2)
            down(b + 1, (b + 1) % 2)
            shared_tiles(EARLY, NT, lambda: None)


def attention_b(nc, scope, m, w, w_proj, b_proj):
    mk = m.inner(scope, "b")
    S = 6 * DB
    VW = 32
    GH = 4
    v_ext = mk.sb("v_ext", [P, NT, HB, VW])
    qst = mk.sb("qst", [P, HB, N], BF16)
    kst = mk.sb("kst", [P, HB, N], BF16)
    o_sb = mk.sb("o_sb", [P, NT, E])

    QS = "hmlhmh"
    KS = "hhhmml"
    with ExitStack() as inner:
        pk = m.inner(inner, "bp")
        NB = 3
        res = [pk.sb(f"res{i}", [P, 2, HB, DB]) for i in range(2)]
        stack = [pk.sb(f"stack{i}", [P, 2, HB, 8, DB], BF16) for i in range(NB)]
        qk_ps = [pk.ps(f"qk_ps{i}", [P, 512]) for i in range(2)]
        v_ps = [pk.ps(f"v_ps{i}", [P, 512]) for i in range(2)]
        st_ps = [pk.ps(f"st_ps{i}", [P, 8, P], BF16) for i in range(4)]
        zeros_set, v_set = pk.sem("zeros_set"), pk.sem("v_set")
        qkv_mm, v_out, high, resid, mid, low = (pk.sem("qkv_mm"), pk.sem("v_out"), pk.sem("high"), pk.sem("resid"),
                                                pk.sem("mid"), pk.sem("low"))
        high_copied, stacked, st_t = pk.sem("high_copied"), pk.sem("stacked"), pk.sem("st_t")
        q_stored, k_stored = pk.sem("q_stored"), pk.sem("k_stored")

        def qk_of(t):
            return qk_ps[t % 2][:, :].rearrange("p (r h d) -> p r h d", r=2, d=DB)

        with nc.Block() as block:
            @block.gpsimd
            def _(pool):
                for b in range(NB):
                    nc.gpsimd.memset(stack[b][:, :, :, S // DB:8, :], 0.0).then_inc(zeros_set, 1)
                pool.wait_ge(zeros_set, NB)
                for b in range(NB):
                    for i in range(GH):
                        sel = stack[b][:, 1, :, S // DB, :].rearrange("p (g h) (k j) -> p h j g k", h=GH, j=GH)
                        nc.gpsimd.memset(sel[:, i, i, :, 0:3], 1.0)
                nc.gpsimd.memset(v_ext[:, :, :, DB:DB + 1], 1.0)
                nc.gpsimd.memset(v_ext[:, :, :, DB + 1:VW], 0.0).then_inc(v_set, 1)
                for t in range(NT):
                    s = stack[t % NB]
                    pool.wait_ge(high, t + 1)
                    for i in (3, 5):
                        nc.gpsimd.tensor_copy(s[:, 0, :, i, :], s[:, 0, :, 0, :])
                    for i in (1, 2):
                        last = nc.gpsimd.tensor_copy(s[:, 1, :, i, :], s[:, 1, :, 0, :])
                    last.then_inc(high_copied, 1)

            @block.scalar
            def _(act):
                def store(t, k):
                    act.wait_ge(st_t, t * 4 + k + 1)
                    nc.scalar.activation(qst[:, 8 * k:8 * k + 8, t * P:(t + 1) * P], st_ps[k][:, :, :],
                                         ACT.Copy).then_inc(q_stored, 1)

                act.wait_ge(v_set, 1)
                for t in range(NT + 2):
                    if t < NT:
                        act.wait_ge(qkv_mm, t + 1)
                        after(act, st_t, (t - NB + 1) * 4)
                        nc.scalar.activation(stack[t % NB][:, :, :, 0, :], qk_of(t), ACT.Copy).then_inc(high, 1)
                    if t >= 2:
                        store(t - 2, 0)
                    if t < NT:
                        act.wait_ge(resid, t + 1)
                        nc.scalar.activation(stack[t % NB][:, :, :, 4, :], res[t % 2][:, :, :, :], ACT.Copy)\
                            .then_inc(mid, 1)
                        nc.scalar.activation(v_ext[:, t, :, 0:DB],
                                             v_ps[t % 2][:, 0:E].rearrange("p (h d) -> p h d", d=DB), ACT.Copy)\
                            .then_inc(v_out, 1)
                    if t >= 2:
                        store(t - 2, 1)

            @block.vector
            def _(dve):
                def store(t, k):
                    dve.wait_ge(st_t, t * 4 + k + 3)
                    nc.vector.tensor_copy(kst[:, 8 * k:8 * k + 8, t * P:(t + 1) * P], st_ps[2 + k][:, :, :])\
                        .then_inc(k_stored, 1)

                for t in range(NT + 2):
                    s = stack[t % NB]
                    if t < NT:
                        dve.wait_ge(high, t + 1)
                        after(dve, low, t - 1)
                        nc.vector.tensor_tensor(res[t % 2][:, :, :, :], qk_of(t), s[:, :, :, 0, :],
                                                ALU.subtract).then_inc(resid, 1)
                    if t >= 2:
                        store(t - 2, 0)
                    if t < NT:
                        dve.wait_ge(mid, t + 1)
                        for r, letters in ((0, QS), (1, KS)):
                            last = nc.vector.tensor_tensor(s[:, r, :, letters.index("l"), :], res[t % 2][:, r, :, :],
                                                           s[:, r, :, 4, :], ALU.subtract)
                        last.then_inc(low, 1)
                        for r, letters in ((0, QS), (1, KS)):
                            last = nc.vector.tensor_copy(s[:, r, :, letters.index("m"), :], s[:, r, :, 4, :])
                        last.then_inc(stacked, 1)
                    if t >= 2:
                        store(t - 2, 1)

            @block.tensor
            def _(pe):
                def project(t):
                    after(pe, resid, t - 1)
                    after(pe, v_out, t - 1)
                    rows = slice(t * P, (t + 1) * P)
                    for bank, cols in ((qk_ps[t % 2][:, :], slice(0, 2 * E)),
                                       (v_ps[t % 2][:, 0:E], slice(2 * E, 3 * E))):
                        for e in range(NE):
                            three(nc, bank, m.xnt_hi[:, e, rows], m.xnt_lo[:, e, rows],
                                  w.hi[:, e, cols], w.lo[:, e, cols], e == 0, False)
                        nc.tensor.matmul(bank, w.ones[:, :], w.bias_hi[:, cols], start=False, stop=False)
                        last = nc.tensor.matmul(bank, w.ones[:, :], w.bias_lo[:, cols], start=False, stop=True)
                    last.then_inc(qkv_mm, 1)

                def transpose_stacks(t):
                    pe.wait_ge(stacked, t + 1)
                    pe.wait_ge(high_copied, t + 1)
                    for k in range(4):
                        after(pe, q_stored if k < 2 else k_stored, t * 2 - 1 + k % 2)
                        for i in range(8):
                            last = nc.tensor.transpose(
                                st_ps[k][:, i, :],
                                stack[t % NB][:, k // 2, 8 * (k % 2) + i, :, :].rearrange("p s d -> p (s d)"),
                                m.ident_bf[:, :])
                        last.then_inc(st_t, 1)

                for t in range(NT + 2):
                    if t < NT:
                        project(t)
                    if t >= 2:
                        transpose_stacks(t - 2)

    with ExitStack() as inner:
        ak = m.inner(inner, "ba")
        HALF = NT // 2
        C = N // 2
        vg = ak.sb("vg", [P, NT, GH * VW])
        pt = [[ak.sb(f"pt{j}{i}", [P, N]) for i in range(GH)] for j in range(2)]
        neg = [ak.sb(f"neg{k}", [P, NT, GH]) for k in range(2)]
        rest = ak.sb("rest", [P, HALF, GH])
        parts = [ak.sb(f"parts{k}", [P, HALF, VW], BF16) for k in range(2)]
        parts_t = ak.sb("parts_t", [P, C], BF16)
        ot = [ak.sb(f"ot{i}", [P, C]) for i in range(2)]
        rsum = ak.sb("rsum", [P, HALF, GH])
        max_ps = [ak.ps(f"max_ps{i}", [P, 512]) for i in range(2)]
        st_ps = [ak.ps(f"st_ps{i}", [P, N]) for i in range(2)]
        pv_ps = ak.ps("pv_ps", [P, 512])
        mix_ps = ak.ps("mix_ps", [P, 512])
        V_PARTS = [(slice(0, 4), 3), (slice(4, 6), 4), (slice(6, 8), 5)]
        met, parts_zero, vg_ready = ak.sem("met"), ak.sem("parts_zero"), ak.sem("vg_ready")
        max_mm = ak.sem("max_mm")
        max_out = ak.sem("max_out")
        parts_set = ak.sem("parts_set")
        parts_mm = ak.sem("parts_mm")
        parts_out = ak.sem("parts_out")
        folded = ak.sem("folded")
        st_mm = ak.sem("st_mm")
        st_exp = ak.sem("st_exp")
        pv_mm = ak.sem("pv_mm")
        ot_out = ak.sem("ot_out")
        ob_t = ak.sem("ob_t")
        o_out = ak.sem("o_out")
        rs, chain_sem = ak.sem("rs"), ak.sem("chain")
        GROUPS = HB // GH

        def units_of(t, c0, c1):
            per = min(GH, C // (c1 - c0))
            return [(t, range(i, i + per), c0, c1) for i in range(0, GH, per)]

        max_units = [u for t in range(HALF) for u in units_of(t, 0, (t + 1) * P)]
        MA = len(max_units)
        for t in range(HALF, NT):
            max_units += units_of(t, 0, C) + units_of(t, C, (t + 1) * P)
        MU = len(max_units)
        assert MU % 2 == 0

        def tile_of(c, kb, offset):
            return (kb, min(C, (c + 1) * C - kb * P), offset)

        slots2 = []
        for c in range(2):
            for kb in range(0, (c + 1) * HALF, 2):
                first = tile_of(c, kb, 0)
                slots2.append((c, [first, tile_of(c, kb + 1, first[1])]))
        SL = len(slots2)
        FIRST = [j for j in range(SL) if j == 0 or slots2[j][0] != slots2[j - 1][0]]
        LAST = [FIRST[1] - 1, SL - 1]
        PU = SL * GH
        assert SL % 2 == 0

        PIECES = 4
        LAG = GH + 1
        EARLY = FIRST[1] * GH

        def max_steps(g, u):
            if isinstance(g, int) and g == 0:
                n, k = EARLY - 2, MU - MA
                if u < n:
                    return [(0, MA + i) for i in range(k * u // n, k * (u + 1) // n)]
                n = PU - EARLY
                u = max(u, EARLY) - EARLY if u >= EARLY else -1
                return [(1, i) for i in range(MU * u // n, MU * (u + 1) // n)] if u >= 0 else []
            if last_group(g):
                return []
            return [(g + 1, i) for i in range(MU * u // PU, MU * (u + 1) // PU)]

        def at(g, first, others):
            return first if isinstance(g, int) and g == 0 else others

        def of_heads(tensor, g, i, rows, c0, c1):
            return tensor[rows, g * GH + i, c0:c1] if isinstance(g, int) else \
                tensor[rows, ds(g * GH + i, 1), c0:c1].rearrange("p a c -> p (a c)")

        def over_groups(eng, group):
            group(0)
            with eng.Fori(1, GROUPS - 1) as g:
                group(g)
            group(GROUPS - 1)

        def last_group(g):
            return isinstance(g, int) and g == GROUPS - 1

        with nc.Block() as block:
            @block.gpsimd
            def _(pool):
                for k in range(2):
                    last = nc.gpsimd.memset(parts[k][:, :, :], 0.0)
                last.then_inc(parts_zero, 1)

                def group(g):
                    for tiles, slot in V_PARTS:
                        after(pool, pv_mm, (g * SL + (slot + 1 - SL)) * PIECES)
                        src = v_ext[:, tiles, g * GH:(g + 1) * GH, :] if isinstance(g, int) else \
                            v_ext[:, tiles, ds(g * GH, GH), :]
                        own_slot(pool, met)
                        nc.gpsimd.tensor_copy(vg[:, tiles, :].rearrange("p t (h d) -> p t h d", d=VW), src)\
                            .then_inc(vg_ready, 1)
                over_groups(pool, group)

            @block.scalar
            def _(act):
                def copy_parts(n):
                    act.wait_ge(parts_mm, n + 1)
                    after(act, folded, n)
                    nc.scalar.activation(parts_t[S:P, :], mix_ps[S:P, :], ACT.Copy).then_inc(parts_out, 1)

                def exp_of(g, u):
                    j, i = u // GH, u % GH
                    act.wait_ge(st_mm, g * PU + u + 1)
                    after(act, pv_mm, (g * SL + (j - 1)) * PIECES)
                    w = sum(w for _, w, _ in slots2[j][1])
                    nc.scalar.activation(pt[j % 2][i][:, 0:w], st_ps[u % 2][:, 0:w], ACT.Exp).then_inc(st_exp, 1)

                def out_t(g, c):
                    act.wait_ge(pv_mm, (g * SL + (LAST[c] + 1)) * PIECES)
                    after(act, ob_t, g * 2 + (c - 1))
                    nc.scalar.activation(ot[c][:, :], pv_ps[:, :], ACT.Copy).then_inc(ot_out, 1)

                def group(g):
                    for u in range(PU):
                        exp_of(g, u)
                        if u == at(g, 7, 2):
                            copy_parts(g * 2 + 1)
                        if u == LAG - 1 and not (isinstance(g, int) and g == 0):
                            out_t(g - 1, 1)
                        if u == at(g, 15, 10) and not last_group(g):
                            copy_parts(g * 2 + 2)
                        if u == FIRST[1] * GH + LAG - 1:
                            out_t(g, 0)

                copy_parts(0)
                over_groups(act, group)
                out_t(GROUPS - 1, 1)

            @block.vector
            def _(dve):
                chain = Chain(dve, chain_sem)

                def max_of(g, k):
                    t, heads, c0, c1 = max_units[k]
                    w = c1 - c0
                    dve.wait_ge(max_mm, g * MU + k + 1)
                    nc.vector.tensor_reduce(
                        neg[c0 // C][:, t, heads[0]:heads[-1] + 1],
                        max_ps[k % 2][:, 0:len(heads) * w].rearrange("p (h c) -> p h c", c=w),
                        AX.X, ALU.max, negate=True).then_inc(max_out, 1)
                    if k == MA - 1:
                        split_max(g, 0)
                    if k == MU - 1:
                        split_max(g, 1)

                def split_max(g, c):
                    tiles = slice(c * HALF, (c + 1) * HALF)
                    dve.wait_ge(max_out, g * MU + (MU if c else MA))
                    after(dve, parts_mm, g * 2 + (c - 1))
                    chain.begin(g * 7 + 3 * c)
                    if c:
                        chain(nc.vector.tensor_tensor(neg[0][:, tiles, :], neg[0][:, tiles, :],
                                                      neg[1][:, tiles, :], ALU.min))
                    high, mid, low = (parts[c][:, :, k * GH:(k + 1) * GH] for k in range(3))
                    chain(nc.vector.tensor_copy(high, neg[0][:, tiles, :]))
                    chain(nc.vector.tensor_tensor(rest[:, :, :], neg[0][:, tiles, :], high, ALU.subtract))
                    chain(nc.vector.tensor_copy(mid, rest[:, :, :]))
                    nc.vector.tensor_tensor(low, rest[:, :, :], mid, ALU.subtract).then_inc(parts_set, 1)

                def fold(g, c):
                    dve.wait_ge(parts_out, g * 2 + c + 1)
                    cols = slice(c * C, (c + 1) * C)
                    dst = qst[S:P, g * GH:(g + 1) * GH, cols] if isinstance(g, int) else \
                        qst[S:P, ds(g * GH, GH), cols]
                    nc.vector.tensor_copy(dst, parts_t[S:P, :].unsqueeze(1).broadcast_to([P - S, GH, C]))\
                        .then_inc(folded, 1)

                def finish(g, c):
                    dve.wait_ge(ob_t, g * 2 + c + 1)
                    got = mix_ps[:, :].rearrange("p (t h d) -> p t h d", h=GH, d=VW)
                    after(dve, o_out, g * 2 + c)
                    nc.vector.reciprocal(rsum[:, :, :], got[:, :, :, DB]).then_inc(rs, 1)
                    dve.wait_ge(rs, g * 2 + c + 1)
                    tiles = slice(c * HALF, (c + 1) * HALF)
                    dst = o_sb[:, tiles, g * GH * DB:(g + 1) * GH * DB] if isinstance(g, int) else \
                        o_sb[:, tiles, ds(g * (GH * DB), GH * DB)]
                    nc.vector.scalar_tensor_tensor(
                        out=dst.rearrange("p t (h d) -> p t h d", d=DB), in0=got[:, :, :, 0:DB],
                        scalar=float(E) ** -0.5, in1=rsum[:, :, :].unsqueeze(3).broadcast_to([P, HALF, GH, DB]),
                        op0=ALU.mult, op1=ALU.mult).then_inc(o_out, 1)

                def group(g):
                    for u in range(PU):
                        for of, k in max_steps(g, u):
                            max_of(of, k)
                        if u == at(g, 7, 4):
                            fold(g, 1)
                        if u == 8 and not (isinstance(g, int) and g == 0):
                            finish(g - 1, 1)
                        if u == at(g, 16, 12) and not last_group(g):
                            fold(g + 1, 0)
                        if u == 18:
                            finish(g, 0)

                dve.wait_ge(parts_zero, 1)
                for k in range(MA):
                    max_of(0, k)
                fold(0, 0)
                over_groups(dve, group)
                finish(GROUPS - 1, 1)

            @block.tensor
            def _(pe):
                def max_scores(g, k):
                    t, heads, c0, c1 = max_units[k]
                    w = c1 - c0
                    after(pe, max_out, g * MU + k - 1)
                    for n, i in enumerate(heads):
                        out = max_ps[k % 2][:, n * w:(n + 1) * w]
                        masked = c1 > t * P
                        last = nc.tensor.matmul(out, of_heads(qst, g, i, slice(0, S), t * P, (t + 1) * P),
                                                of_heads(kst, g, i, slice(0, S), c0, c1),
                                                start=True, stop=not masked)
                        if masked:
                            last = nc.tensor.matmul(out[:, w - P:w], m.ident_bf[:, :], m.mask[:, :],
                                                    start=False, stop=True)
                    last.then_inc(max_mm, 1)

                def mix_free(uses_parts, uses_out):
                    after(pe, parts_out, uses_parts)
                    after(pe, o_out, uses_out)

                def parts_tr(g, c, outs):
                    pe.wait_ge(parts_set, g * 2 + c + 1)
                    mix_free(g * 2 + c, outs)
                    for t in range(HALF):
                        last = nc.tensor.matmul(mix_ps[S:P, t * P:(t + 1) * P], parts[c][:, t, :], m.ident_bf[:, :],
                                                start=True, stop=True)
                    last.then_inc(parts_mm, 1)

                def scores_t(g, u):
                    j, i = u // GH, u % GH
                    c, tiles = slots2[j]
                    after(pe, st_exp, g * PU + u - 1)
                    if i == 0 and j in FIRST:
                        pe.wait_ge(folded, g * 2 + c + 1)
                    for kb, w, offset in tiles:
                        out = st_ps[u % 2][:, offset:offset + w]
                        masked = kb >= c * HALF
                        last = nc.tensor.matmul(out, of_heads(kst, g, i, slice(0, P), kb * P, (kb + 1) * P),
                                                of_heads(qst, g, i, slice(0, P), (c + 1) * C - w, (c + 1) * C),
                                                start=True, stop=not masked)
                        if masked:
                            last = nc.tensor.matmul(out[:, 0:P], m.ident_bf[:, :], m.mask_t[:, :],
                                                    start=False, stop=True)
                    last.then_inc(st_mm, 1)

                def times_v(g, n):
                    j, a, half = n // PIECES, n % PIECES // 2, n % 2
                    c, tiles = slots2[j]
                    kb, w, offset = tiles[a]
                    x, y = w // 2 * half, w // 2 * (half + 1)
                    pe.wait_ge(st_exp, g * PU + (j + 1) * GH)
                    if j in FIRST and n % PIECES == 0:
                        after(pe, ot_out, g * 2 + c)
                    pe.wait_ge(vg_ready, g * 3 + (1 + (kb >= 4) + (kb >= 6)))
                    for i in range(GH):
                        last = nc.tensor.matmul(pv_ps[VW * i:VW * (i + 1), C - w + x:C - w + y],
                                                vg[:, kb, VW * i:VW * (i + 1)],
                                                pt[j % 2][i][:, offset + x:offset + y],
                                                start=kb == 0 and half == 0,
                                                stop=j in LAST and a == 1, skip_group_check=True)
                    last.then_inc(pv_mm, 1)

                def back(g, c, outs):
                    pe.wait_ge(ot_out, g * 2 + c + 1)
                    mix_free(outs, g * 2 + c)
                    for t in range(HALF):
                        last = nc.tensor.transpose(mix_ps[:, t * P:(t + 1) * P], ot[c][:, t * P:(t + 1) * P],
                                                   m.ident[:, :])
                    last.then_inc(ob_t, 1)

                def group(g):
                    first = isinstance(g, int) and g == 0
                    for u in range(PU):
                        scores_t(g, u)
                        beside = max_steps(g, u)
                        for of, k in beside[0:len(beside) // 2]:
                            max_scores(of, k)
                        if u < LAG and not first:
                            times_v(g - 1, PU - LAG + u)
                        if u >= LAG:
                            times_v(g, u - LAG)
                        for of, k in beside[len(beside) // 2:]:
                            max_scores(of, k)
                        if u == at(g, 7, 1):
                            parts_tr(g, 1, g * 2 - 1)
                        if u == 6 and not first:
                            back(g - 1, 1, g * 2 + 2)
                        if u == at(g, 14, 9) and not last_group(g):
                            parts_tr(g + 1, 0, g * 2)
                        if u == 16:
                            back(g, 0, g * 2 + (2 if last_group(g) else 3))

                for k in range(MA):
                    max_scores(0, k)
                parts_tr(0, 0, 0)
                over_groups(pe, group)
                for n in range(PU - LAG, PU):
                    times_v(GROUPS - 1, n)
                back(GROUPS - 1, 1, 2 * GROUPS)

    with ExitStack() as inner:
        ok = m.inner(inner, "bo")
        w_raw, w_hi, w_lo = ok.sb("w_raw", [P, NE, E]), ok.sb("w_hi", [P, NE, E], F32R), ok.sb("w_lo", [P, NE, E], F32R)
        bias = ok.sb("bias", [P, E])
        w_in, hi_set, w_split = ok.sem("w_in"), ok.sem("hi_set"), ok.sem("w_split")
        ot_hi, ot_lo = ok.sb("ot_hi", [P, NE, N], F32R), ok.sb("ot_lo", [P, NE, N], F32R)
        o_ps = [ok.ps(f"o_ps{i}", [P, NE, 2 * P]) for i in range(4)]
        y_ps = [ok.ps(f"y_ps{i}", [P, 512]) for i in range(2)]
        biased, o_t, hi_out, lo_out, y_mm, y_out = (ok.sem("biased"), ok.sem("o_t"), ok.sem("hi_out"), ok.sem("lo_out"),
                                                    ok.sem("y_mm"), ok.sem("y_out"))
        with nc.Block() as block:
            @block.sync
            def _(sp):
                sp.dma_start(w_raw[:, :, :], w_proj).then_inc(w_in, 16)
                sp.dma_start(bias[:, :], b_proj.broadcast_to([P, E])).then_inc(w_in, 16)

            @block.scalar
            def _(act):
                act.wait_ge(w_in, 32)
                nc.scalar.activation(w_hi[:, :, :], w_raw[:, :, :], ACT.Copy).then_inc(hi_set, 1)
                for u in range(4):
                    act.wait_ge(o_t, u + 1)
                    nc.scalar.activation(ot_hi[:, :, 2 * P * u:2 * P * (u + 1)], o_ps[u][:, :, :], ACT.Copy)\
                        .then_inc(hi_out, 1)

            @block.vector
            def _(dve):
                dve.wait_ge(w_in, 32)
                dve.wait_ge(hi_set, 1)
                nc.vector.tensor_tensor(w_lo[:, :, :], w_raw[:, :, :], f32(w_hi[:, :, :]), ALU.subtract)\
                    .then_inc(w_split, 1)
                nc.vector.tensor_tensor(m.x[:, :, :], m.x[:, :, :], bias[:, :].unsqueeze(1).broadcast_to([P, NT, E]),
                                        ALU.add).then_inc(biased, 1)
                for u in range(4):
                    dve.wait_ge(hi_out, u + 1)
                    cols = slice(2 * P * u, 2 * P * (u + 1))
                    nc.vector.tensor_tensor(ot_lo[:, :, cols], o_ps[u][:, :, :], f32(ot_hi[:, :, cols]),
                                            ALU.subtract).then_inc(lo_out, 1)
                dve.wait_ge(biased, 1)
                for t in range(NT):
                    dve.wait_ge(y_mm, t + 1)
                    nc.vector.tensor_tensor(m.x[:, t, :], m.x[:, t, :], y_ps[t % 2][:, 0:E], ALU.add).then_inc(y_out, 1)

            @block.tensor
            def _(pe):
                for u in range(4):
                    for e in range(NE):
                        for j in range(2):
                            last = nc.tensor.transpose(o_ps[u][:, e, j * P:(j + 1) * P],
                                                       o_sb[:, 2 * u + j, e * P:(e + 1) * P], m.ident[:, :])
                    last.then_inc(o_t, 1)
                pe.wait_ge(w_split, 1)
                for t in range(NT):
                    pe.wait_ge(lo_out, t // 2 + 1)
                    after(pe, y_out, t - 1)
                    rows = slice(t * P, (t + 1) * P)
                    for e in range(NE):
                        last = three(nc, y_ps[t % 2][:, 0:E], ot_hi[:, e, rows], ot_lo[:, e, rows],
                                     w_hi[:, e, :], w_lo[:, e, :], e == 0, e == NE - 1)
                    last.then_inc(y_mm, 1)


class SharedExpert:

    def __init__(self, m):
        self.hi13, self.lo13 = m.sb("s13_hi", [P, NE, 2 * F], F32R), m.sb("s13_lo", [P, NE, 2 * F], F32R)
        self.gate = m.sb("gate", [P, NE, EXPERTS])
        self.hi2, self.lo2 = m.sb("s2_hi", [P, 3, E], F32R), m.sb("s2_lo", [P, 3, E], F32R)

    def steps(self, nc, m, gate, s13, s2a, s2b):
        raw13, raw2 = m.sb("s13_raw", [P, NE, 2 * F]), m.sb("s2_raw", [P, 3, E])
        loaded, hi_set, lo_set = m.sem("s_loaded"), m.sem("s_hi_set"), m.sem("s_lo_set")
        parts = [(raw13[:, :, :], self.hi13[:, :, :], self.lo13[:, :, :]),
                 (raw2[:, 0:2, :], self.hi2[:, 0:2, :], self.lo2[:, 0:2, :]),
                 (raw2[0:F3, 2, :], self.hi2[0:F3, 2, :], self.lo2[0:F3, 2, :])]

        def load(sp):
            for (raw, _, _), src in zip(parts, (s13, s2a, s2b)):
                sp.dma_start(raw, src).then_inc(loaded, 16)
            sp.dma_start(self.gate[:, :, :], gate).then_inc(loaded, 16)

        def split(pool):
            pool.wait_ge(loaded, 64)
            for raw, hi, _ in parts:
                nc.gpsimd.tensor_copy(hi, raw).then_inc(hi_set, 1)
            pool.wait_ge(hi_set, 3)
            for raw, hi, lo in parts:
                nc.gpsimd.tensor_tensor(lo, raw, f32(hi), ALU.subtract).then_inc(lo_set, 1)

        return {"sync": load, "pool": split}


class AttentionWeights:

    def __init__(self, m):
        self.hi, self.lo = m.sb("hi", [P, NE, 3 * E], F32R), m.sb("lo", [P, NE, 3 * E], F32R)
        self.bias_hi, self.bias_lo = m.sb("bias_hi", [1, 3 * E], F32R), m.sb("bias_lo", [1, 3 * E], F32R)
        self.ones = m.sb("ones", [1, P], F32R)

    def steps(self, nc, m, ones, w_attn, b_attn, rope):
        raw, raw_bias = m.sb("raw", [P, NE, 3 * E]), m.sb("raw_bias", [1, 3 * E])
        turn = m.sb("turn", [P, 2, E])
        by_sin = m.sb("by_sin", [P, NE, 2, E])
        loaded, by_sines, by_cosines, rotated = m.sem("loaded"), m.sem("by_sines"), m.sem("by_cosines"), m.sem("rotated")
        hi_set, lo_set = m.sem("hi_set"), m.sem("lo_set")
        pairs = [(raw[:, :, :], self.hi[:, :, :], self.lo[:, :, :]),
                 (raw_bias[:, :], self.bias_hi[:, :], self.bias_lo[:, :])]

        def load(sp):
            sp.dma_start(raw[:, :, :], w_attn).then_inc(loaded, 16)
            sp.dma_start(raw_bias[:, :], b_attn).then_inc(loaded, 16)
            sp.dma_start(turn[:, :, :], rope.broadcast_to([P, 2, E])).then_inc(loaded, 16)

        def rotate(pool):
            pool.wait_ge(loaded, 16 * 3)
            done = 0
            for rows, n, w in ((P, NE, raw[:, :, 0:2 * E]), (1, 1, raw_bias[:, 0:2 * E].unsqueeze(1))):
                w = w.rearrange("p n (r c) -> p n r c", r=2)
                sines = by_sin[0:rows, 0:n, :, :]

                def table(k):
                    return turn[0:rows, k, :].unsqueeze(1).unsqueeze(1).broadcast_to([rows, n, 2, E])

                for e in range(n):
                    for k in range(2):
                        last = nc.gpsimd.tensor_tensor(sines[:, e, :, k::2], w[:, e, :, 1 - k::2],
                                                       table(1)[:, e, :, k::2], ALU.mult)
                last.then_inc(by_sines, 1)
                done += 1
                pool.wait_ge(by_sines, done)
                for e in range(n):
                    last = nc.gpsimd.tensor_tensor(w[:, e], w[:, e], table(0)[:, e], ALU.mult)
                last.then_inc(by_cosines, 1)
                pool.wait_ge(by_cosines, done)
                for e in range(n):
                    last = nc.gpsimd.tensor_tensor(w[:, e], w[:, e], sines[:, e], ALU.add)
                last.then_inc(rotated, 1)
                pool.wait_ge(rotated, done)

        def high(act):
            act.wait_ge(rotated, 2)
            nc.scalar.activation(self.ones[:, :], ones[0:1, :], ACT.Copy)
            for whole, hi, _ in pairs:
                nc.scalar.activation(hi, whole, ACT.Copy).then_inc(hi_set, 1)

        def low(dve):
            dve.wait_ge(hi_set, len(pairs))
            for whole, hi, lo in pairs:
                nc.vector.tensor_tensor(lo, whole, f32(hi), ALU.subtract).then_inc(lo_set, 1)

        return {"sync": load, "pool": rotate, "scalar": high, "vector": low}


class Memory:

    def __init__(self, nc, scope, tag):
        self.nc, self.scope, self.tag = nc, scope, tag

    def inner(self, scope, tag):
        return Memory(self.nc, scope, tag)

    def sb(self, name, shape, dt=F32):
        return self.scope.enter_context(self.nc.sbuf_tensor(f"{self.tag}_{name}", shape, dt))

    def ps(self, name, shape, dt=F32):
        return self.scope.enter_context(self.nc.psum_tensor(f"{self.tag}_{name}", shape, dt))

    def sem(self, name):
        return self.nc.alloc_semaphore(f"{self.tag}_{name}")


def program(nc, x, w_qkv, w_o, q_scale, k_scale, w_attn, b_attn, rope, w_proj, b_proj, gate, w13, w2a, w2b,
            s13, s2a, s2b, out):
    with ExitStack() as ctx:
        m = Memory(nc, ctx, "m")
        m.x = m.sb("x", [P, NT, E])
        m.xnt = m.sb("xnt", [P, NE, N])
        m.xnt_hi = m.sb("xnt_hi", [P, NE, N], F32R)
        m.xnt_lo = m.sb("xnt_lo", [P, NE, N], F32R)
        m.ident = m.sb("ident", [P, P])
        m.ident_bf = m.sb("ident_bf", [P, P], BF16)
        m.mask = m.sb("mask", [P, P], BF16)
        m.mask_t = m.sb("mask_t", [P, P], BF16)
        m.before = m.sb("before", [P, P], BF16)
        m.ones_bf = m.sb("ones_bf", [P, P], BF16)
        m.xs = nc.dram_tensor("sorted_rows", (BLOCKS, P, E), F32, kind="Internal").ap()
        m.ys = nc.dram_tensor("sorted_results", (BLOCKS, P, E), F32, kind="Internal").ap()
        shared = SharedExpert(m)
        made = m.sem("made")
        with nc.Block() as block:
            @block.gpsimd
            def _(pool):
                nc.gpsimd.memset(m.ident[:, :], 0.0).then_inc(made, 1)
                nc.gpsimd.memset(m.ident_bf[:, :], 0.0).then_inc(made, 1)
                nc.gpsimd.memset(m.mask[:, :], 0.0).then_inc(made, 1)
                nc.gpsimd.memset(m.mask_t[:, :], 0.0).then_inc(made, 1)
                nc.gpsimd.memset(m.before[:, :], 1.0).then_inc(made, 1)
                nc.gpsimd.memset(m.ones_bf[:, :], 1.0).then_inc(made, 1)
                pool.wait_ge(made, 6)
                for eye in (m.ident, m.ident_bf):
                    nc.gpsimd.affine_select(out=eye[:, :], in_=eye[:, :], compare_op=ALU.not_equal, fill=1.0,
                                            base=0, pattern=[[-1, P]], channel_multiplier=1)
                nc.gpsimd.affine_select(out=m.mask[:, :], in_=m.mask[:, :], compare_op=ALU.is_ge, fill=MASKED,
                                        base=0, pattern=[[-1, P]], channel_multiplier=1)
                nc.gpsimd.affine_select(out=m.mask_t[:, :], in_=m.mask_t[:, :], compare_op=ALU.is_ge, fill=MASKED,
                                        base=0, pattern=[[1, P]], channel_multiplier=-1)
                nc.gpsimd.affine_select(out=m.before[:, :], in_=m.before[:, :], compare_op=ALU.is_gt, fill=0.0,
                                        base=0, pattern=[[1, P]], channel_multiplier=-1)
        with nc.cleanup_on_exit(), ExitStack() as scope:
            attention_a(nc, scope, m, x, w_qkv, w_o, q_scale, k_scale,
                        more=shared.steps(nc, m.inner(scope, "sh"), gate, s13, s2a, s2b))
        with ExitStack() as until_b:
            weights_b = AttentionWeights(m.inner(until_b, "wb"))
            with nc.cleanup_on_exit(), ExitStack() as scope:
                mixture(nc, scope, "moe1", m, w13, w2a, w2b, shared,
                        more=weights_b.steps(nc, m.inner(scope, "wb"), m.ones_bf, w_attn, b_attn, rope))
            with ExitStack() as scope:
                layer_norm(nc, scope, "ln2", m)
            with nc.cleanup_on_exit(), ExitStack() as scope:
                attention_b(nc, scope, m, weights_b, w_proj, b_proj)
        with ExitStack() as scope:
            mixture(nc, scope, "moe3", m, w13, w2a, w2b, shared, store=out)


def rope_table():
    freqs = np.float32(10000.0) ** (-(np.arange(0, DB, 2, dtype=np.float32) / np.float32(DB)))
    angle = np.outer(np.arange(HB, dtype=np.float32), freqs)
    cos = np.repeat(np.cos(angle), 2, axis=1)
    sin = np.stack([-np.sin(angle), np.sin(angle)], axis=-1)
    return np.stack([cos.reshape(-1), sin.reshape(-1)]).astype(np.float32)[None]


def kernel(**inputs):
    import concourse.bacc as bacc
    from concourse.bass_utils import run_bass_kernel_spmd

    def part(name):
        return np.asarray(inputs[name])

    def tiles(a):
        return np.ascontiguousarray(a.reshape(-1, P, *a.shape[1:]).swapaxes(0, 1))

    qkv = np.concatenate([part(f"L0_attn_a_w{c}") for c in "qkv"], axis=2)
    qkv = qkv.reshape(NE, P, HA, 3 * DA).transpose(2, 1, 0, 3)
    w13 = np.concatenate([part("L0_ffn_w1"), part("L0_ffn_w3")], axis=1)
    w13 = w13.reshape(EXPERTS, 2 * INTER, NE, P).transpose(3, 0, 2, 1)
    w2 = part("L0_ffn_w2").transpose(2, 0, 1)
    s13 = np.concatenate([part("L0_ffn_sw1"), part("L0_ffn_sw3")])
    s2 = part("L0_ffn_sw2").T
    arrays = {
        "x": tiles(part("L0_attn_a_x")[0]),
        "w_qkv": np.ascontiguousarray(qkv),
        "w_o": np.ascontiguousarray(part("L0_attn_a_wo").transpose(1, 0, 2)),
        "q_scale": part("L0_attn_a_q_scale")[:, None],
        "k_scale": part("L0_attn_a_k_scale")[:, None],
        "w_attn": tiles(part("L0_attn_b_w_attn")),
        "b_attn": part("L0_attn_b_b_attn")[None],
        "rope": rope_table(),
        "w_proj": tiles(part("L0_attn_b_w_proj")),
        "b_proj": part("L0_attn_b_b_proj")[None],
        "gate": tiles(part("L0_ffn_gate_w").T),
        "w13": np.ascontiguousarray(w13),
        "w2a": np.ascontiguousarray(w2[0:P]),
        "w2b": np.ascontiguousarray(w2[P:INTER]),
        "s13": tiles(s13.T),
        "s2a": tiles(s2[0:2 * P]),
        "s2b": np.ascontiguousarray(s2[2 * P:F]),
    }
    nc = bacc.Bacc("TRN2", target_bir_lowering=False, num_devices=1)
    aps = [nc.dram_tensor(f"in_{name}", a.shape, F32, kind="ExternalInput").ap() for name, a in arrays.items()]
    out = nc.dram_tensor("out", (P, NT, E), F32, kind="ExternalOutput").ap()
    program(nc, *aps, out)
    r = run_bass_kernel_spmd(nc, [{f"in_{name}": a for name, a in arrays.items()}], core_ids=[0])
    return r.results[0]["out"].transpose(1, 0, 2).reshape(1, N, E)
```

```python
from contextlib import ExitStack

import numpy as np

import concourse.bass as bass
from concourse import mybir

F32 = mybir.dt.float32
F32R = mybir.dt.float32r
BF16 = mybir.dt.bfloat16
I32 = mybir.dt.int32
ALU = mybir.AluOpType
ACT = mybir.ActivationFunctionType
AX = mybir.AxisListType
ds = bass.ds

P = 128
N = 1024
E = 256
NT = N // P
NE = E // P
HA, DA = 16, 128
HB, DB = 16, 16
EXPERTS, INTER = 16, 176
W = E + 1
BLOCKS = (2 * N + EXPERTS * (P - 1)) // P
F = 2 * INTER
F3 = F - 2 * P
LN_EPS = 1e-5
RMS_EPS = 1e-6
MASKED = -1e30


class Chain:

    def __init__(self, eng, sem):
        self.eng, self.sem, self.base, self.n = eng, sem, 0, 0

    def begin(self, base):
        self.base, self.n = base, 0

    def __call__(self, ins):
        ins.then_inc(self.sem, 1)
        self.n += 1
        self.eng.wait_ge(self.sem, self.base + self.n)


def after(eng, sem, value):
    if isinstance(value, int) and value <= 0:
        return
    eng.wait_ge(sem, value)


def own_slot(eng, met):
    eng.sem_inc(met, 1)


def f32(ap):
    return ap.bitcast(F32)


def layer_norm(nc, scope, tag, m, xn=None, x_in=None, split_f32=False, per_pair=None, more=()):
    more = dict(more)
    mk = m.inner(scope, tag)
    mv = mk.sb("mv", [P, NT, 2])
    veps = mk.sb("veps", [P, NT])
    minus_half = mk.sb("minus_half", [P, NT])
    rstd = mk.sb("rstd", [P, NT])
    xn = mk.sb("xn", [P, NT, E]) if xn is None else xn
    xps = [mk.ps(f"xps{u}", [P, 2, 2 * P]) for u in range(NT // 2)]
    half_set = mk.sem("half_set")
    var_ready = mk.sem("var_ready")
    rstd_ready = mk.sem("rstd_ready")
    xn_ready = mk.sem("xn_ready")
    transposed = mk.sem("transposed")
    hi_ready = mk.sem("hi_ready")
    lo_ready = mk.sem("lo_ready")
    chain_sem = mk.sem("chain")

    with nc.Block() as block:
        if "sync" in more:
            @block.sync
            def _(sp):
                more["sync"](sp)

        @block.gpsimd
        def _(pool):
            nc.gpsimd.memset(minus_half[:], -0.5).then_inc(half_set, 1)
            pool.wait_ge(half_set, 1)
            pool.wait_ge(var_ready, 1)
            nc.gpsimd.tensor_tensor(rstd[:], veps[:], minus_half[:], ALU.pow).then_inc(rstd_ready, 1)
            if "pool" in more:
                more["pool"](pool)

        @block.vector
        def _(dve):
            chain = Chain(dve, chain_sem)
            if x_in is not None:
                for t in range(NT):
                    dve.wait_ge(x_in[t // 2], 16)
                    last = nc.vector.bn_stats(m.stats[:, t, :], m.x[:, t, :])
                chain(last)
            for t in range(NT):
                last = nc.vector.bn_aggr(mv[:, t, :], m.stats[:, t, :])
            chain(last)
            nc.vector.tensor_scalar(veps[:], mv[:, :, 1], LN_EPS, None, ALU.add).then_inc(var_ready, 1)
            dve.wait_ge(rstd_ready, 1)
            for t in range(NT):
                nc.vector.tensor_scalar(xn[:, t, :], m.x[:, t, :], mv[:, t, 0:1], rstd[:, t:t + 1],
                                        ALU.subtract, ALU.mult).then_inc(xn_ready, 1)
            for u in range(NT // 2):
                dve.wait_ge(hi_ready, u + 1)
                cols = slice(2 * P * u, 2 * P * (u + 1))
                nc.vector.tensor_tensor(m.xnt_lo[:, :, cols], xps[u][:, :, :], f32(m.xnt_hi[:, :, cols]),
                                        ALU.subtract).then_inc(lo_ready, 1)
            if "vector" in more:
                more["vector"](dve)

        @block.tensor
        def _(pe):
            for u in range(NT // 2):
                pe.wait_ge(xn_ready, 2 * u + 2)
                for e in range(NE):
                    for j in range(2):
                        last = nc.tensor.transpose(xps[u][:, e, j * P:(j + 1) * P],
                                                   xn[:, 2 * u + j, e * P:(e + 1) * P], m.ident[:, :])
                last.then_inc(transposed, 1)
                if per_pair is not None and u > 0:
                    pe.wait_ge(hi_ready, u)
                    per_pair(u - 1)
            if per_pair is not None:
                pe.wait_ge(hi_ready, NT // 2)
                per_pair(NT // 2 - 1)

        @block.scalar
        def _(act):
            if "scalar_first" in more:
                more["scalar_first"](act)
            for u in range(NT // 2):
                act.wait_ge(transposed, u + 1)
                cols = slice(2 * P * u, 2 * P * (u + 1))
                if split_f32:
                    nc.scalar.activation(m.xnt[:, :, cols], xps[u][:, :, :], ACT.Copy)
                nc.scalar.activation(m.xnt_hi[:, :, cols], xps[u][:, :, :], ACT.Copy).then_inc(hi_ready, 1)
            if "scalar" in more:
                more["scalar"](act)


def three(nc, out, w_hi, w_lo, x_hi, x_lo, start, stop, **kw):
    nc.tensor.matmul(out, w_hi, x_hi, start=start, stop=False, **kw)
    nc.tensor.matmul(out, w_hi, x_lo, start=False, stop=False, **kw)
    return nc.tensor.matmul(out, w_lo, x_hi, start=False, stop=stop, **kw)


def attention_a(nc, scope, m, x_in, w_qkv, w_o, q_scale, k_scale, rank, steps, dest, spare, more):
    mk = m.inner(scope, "a")
    sb, ps, sem = mk.sb, mk.ps, mk.sem
    C3 = 3 * DA
    w_raw = [sb(f"w_raw{i}", [P, NE, C3]) for i in range(2)]
    w_hi = sb("w_hi", [P, NE, C3], F32R)
    w_lo = sb("w_lo", [P, NE, C3], F32R)
    wo_raw = sb("wo_raw", [P, HA, E])
    wo_hi = sb("wo_hi", [P, E], F32R)
    wo_lo = sb("wo_lo", [P, E], F32R)
    scales = sb("scales", [P, 2])
    spare_ids = sb("spare_ids", [P, 4], I32)
    const_loads = 7
    w_in = [sem(f"w_in{i}") for i in range(2)]
    const_in = sem("const_in")
    first_hi = sem("first_hi")
    w_split = sem("w_split")

    def load_first(sp):
        sp.dma_start(w_raw[0][:, :, :], w_qkv[0]).then_inc(w_in[0], 16)
        sp.dma_start(w_raw[1][:, :, :], w_qkv[1]).then_inc(w_in[1], 16)
        sp.dma_start(scales[:, 0:1], q_scale).then_inc(const_in, 16)
        sp.dma_start(scales[:, 1:2], k_scale).then_inc(const_in, 16)
        sp.dma_start(wo_raw[:, :, :], w_o).then_inc(const_in, 16)
        for tile, src in ((m.rank[:, :], rank), (m.steps[:, :], steps), (m.dest[:, :, :], dest),
                          (spare_ids[:, :], spare)):
            sp.dma_start(tile, src).then_inc(const_in, 16)

    def first_high(act):
        act.wait_ge(w_in[0], 16)
        nc.scalar.activation(w_hi[:, :, :], w_raw[0][:, :, :], ACT.Copy).then_inc(first_hi, 1)

    def first_low(pool):
        pool.wait_ge(first_hi, 1)
        nc.gpsimd.tensor_tensor(w_lo[:, :, :], w_raw[0][:, :, :], f32(w_hi[:, :, :]), ALU.subtract).then_inc(w_split, 1)

    with ExitStack() as inner:
        layer_norm(nc, inner, "ln0", m, x_in=x_in,
                   more={"sync": load_first, "scalar_first": first_high, "pool": first_low})

    qkv = sb("qkv", [P, NT, C3])
    junk = sb("junk", [P, DA])
    ssq = sb("ssq", [P, NT, 2])
    msq = sb("msq", [P, NT, 2])
    minus_half = sb("minus_half", [P, NT])
    rrms = sb("rrms", [P, NT, 2])
    qk_hi = [sb(f"qk_hi{i}", [P, 2, N], F32R) for i in range(2)]
    qk_lo = [sb(f"qk_lo{i}", [P, 2, N], F32R) for i in range(2)]
    v_hi = [sb(f"v_hi{i}", [P, NT, DA], F32R) for i in range(2)]
    v_lo = [sb(f"v_lo{i}", [P, NT, DA], F32R) for i in range(2)]
    probs = [sb(f"probs{i}", [P, N]) for i in range(2)]
    pt_hi = [sb(f"pt_hi{i}", [P, NT, 2 * P], F32R) for i in range(2)]
    pt_lo = [sb(f"pt_lo{i}", [P, NT, 2 * P], F32R) for i in range(2)]
    neg_max = sb("neg_max", [P, 2])
    sums = [sb(f"sums{i}", [P, NT]) for i in range(2)]
    rsums = [sb(f"rsums{i}", [P, NT]) for i in range(2)]
    ot_hi = sb("ot_hi", [P, N], F32R)
    ot_lo = sb("ot_lo", [P, N], F32R)

    s_ps = [ps(f"s_ps{i}", [P, N]) for i in range(2)]
    t_ps = [ps(f"t_ps{i}", [P, 4, P]) for i in range(2)]
    pv_ps = ps("pv_ps", [P, 512])
    mm_ps = ps("mm_ps", [P, 512])

    half_set = sem("half_set")
    met = sem("met")
    wo_split = sem("wo_split")
    qkv_mm = sem("qkv_mm")
    qkv_out = sem("qkv_out")
    ms_ready = sem("ms_ready")
    rr_ready = sem("rr_ready")
    qk_scaled = sem("qk_scaled")
    qk_t = sem("qk_t")
    qk_hi_out = sem("qk_hi_out")
    qk_lo_out = sem("qk_lo_out")
    v_hi_out = sem("v_hi_out")
    v_lo_out = sem("v_lo_out")
    s_mm = sem("s_mm")
    s_max = sem("s_max")
    s_exp = sem("s_exp")
    p_t = sem("p_t")
    p_hi_out = sem("p_hi_out")
    p_lo_out = sem("p_lo_out")
    pv_mm = sem("pv_mm")
    o_hi_out = sem("o_hi_out")
    o_lo_out = sem("o_lo_out")
    op_mm = sem("op_mm")
    op_out = sem("op_out")
    rs_ready = sem("rs_ready")
    chain_sem = sem("chain")

    xs_cleared, zeros_set = sem("xs_cleared"), sem("zeros_set")
    blank = sb("blank", [P, 4, W])

    PAIRS = HA // 2

    def each_head(eng, head):
        for c in range(2):
            head(c, c, True)
        with eng.Fori(1, PAIRS - 1) as i:
            for c in range(2):
                head(i * 2 + c, c, True)
        head(HA - 2, 0, True)
        head(HA - 1, 1, False)

    def last_bank(j):
        return s_ps[0] if j % 2 else mm_ps

    def bank_of(p, i):
        return pv_ps if isinstance(p, int) and p == 0 and i % 2 else mm_ps

    with nc.Block() as block:
        @block.sync
        def _(sp):
            more["sync"](sp)
            sp.wait_ge(zeros_set, 1)
            for rows in m.xs.values():
                for k in range(4):
                    dst = rows[k::4].rearrange("b p c -> p b c")
                    sp.dma_start(dst, blank[:, k:k + 1, :].broadcast_to([P, dst.shape[1], W]))\
                        .then_inc(xs_cleared, 16)
            with sp.Fori(1, PAIRS) as i:
                for c in range(2):
                    sp.wait_ge(w_split, i * 2 + (c - 1))
                    sp.dma_start(w_raw[c][:, :, :],
                                 w_qkv[ds(i * 2 + c, 1)].rearrange("a p e c -> (a p) e c")).then_inc(w_in[c], 16)
            sp.wait_ge(xs_cleared, 16 * 8)

        @block.gpsimd
        def _(pool):
            def split_w(h, c):
                pool.wait_ge(w_in[c], (h // 2 if isinstance(h, int) else h[0]) * 16 + 16)
                after(pool, qkv_mm, (h if isinstance(h, int) else h[1]) * 8)
                own_slot(pool, met)
                nc.gpsimd.tensor_copy(w_hi[:, :, :], w_raw[c][:, :, :]).then_inc(pool_chain.sem, 1)
                pool_chain.n += 1
                pool.wait_ge(pool_chain.sem, pool_chain.base + pool_chain.n)
                nc.gpsimd.tensor_tensor(w_lo[:, :, :], w_raw[c][:, :, :], f32(w_hi[:, :, :]),
                                        ALU.subtract).then_inc(w_split, 1)

            pool_chain = Chain(pool, half_set)

            def prep_batch(p, b):
                tiles = slice(4 * b, 4 * b + 4)
                pool.wait_ge(ms_ready, p * 2 + (b + 1))
                nc.gpsimd.tensor_tensor(rrms[:, tiles, :].rearrange("p t c -> p (t c)"),
                                        msq[:, tiles, :].rearrange("p t c -> p (t c)"),
                                        minus_half[:, :], ALU.pow).then_inc(rr_ready, 1)
                pool.wait_ge(rr_ready, p * 2 + (b + 1))
                qk = qkv[:, tiles, 0:2 * DA].rearrange("p t (c d) -> p t c d", d=DA)
                nc.gpsimd.tensor_tensor(qk, qk, rrms[:, tiles, :].unsqueeze(3).broadcast_to([P, 4, 2, DA]),
                                        ALU.mult).then_inc(qk_scaled, 1)

            def prep_v(p, c):
                pool.wait_ge(v_hi_out, p + 1)
                nc.gpsimd.tensor_tensor(v_lo[c][:, :, :], qkv[:, :, 2 * DA:C3], f32(v_hi[c][:, :, :]),
                                        ALU.subtract).then_inc(v_lo_out, 1)

            nc.gpsimd.memset(blank[:, :, 0:E], 0.0)
            pool.wait_ge(const_in, const_loads * 16)
            nc.gpsimd.tensor_copy(blank[:, :, E:W].bitcast(I32), spare_ids[:, :].unsqueeze(2)).then_inc(zeros_set, 1)
            nc.gpsimd.memset(minus_half[:], -0.5).then_inc(half_set, 1)
            pool_chain.n = 1
            pool.wait_ge(half_set, 1)
            prep_batch(0, 0)
            prep_batch(0, 1)
            split_w(1, 1)
            prep_v(0, 0)
            pool.wait_ge(const_in, const_loads * 16)
            base = pool_chain.n

            def split_wo(h):
                after(pool, op_mm, h * 4)
                own_slot(pool, met)
                nc.gpsimd.tensor_copy(wo_hi[:, :], wo_raw[:, ds(h, 1), :].rearrange("p a e -> p (a e)"))\
                    .then_inc(half_set, 1)
                pool_chain.n += 1
                pool.wait_ge(half_set, pool_chain.base + pool_chain.n)
                own_slot(pool, met)
                nc.gpsimd.tensor_tensor(wo_lo[:, :], wo_raw[:, ds(h, 1), :].rearrange("p a e -> p (a e)"),
                                        f32(wo_hi[:, :]), ALU.subtract).then_inc(wo_split, 1)

            def head(h, par, prep, i=None):
                first = isinstance(h, int) and h == 0
                pool_chain.begin(base + h * 2 - (0 if first else 1))
                if not first:
                    split_wo(h - 1)
                if prep:
                    prep_batch(h + 1, 0)
                    prep_batch(h + 1, 1)
                    if not (isinstance(h, int) and h == HA - 2):
                        split_w(h + 2 if isinstance(h, int) else (i + 1, h + 2), par)
                    prep_v(h + 1, 1 - par)

            head(0, 0, True)
            head(1, 1, True)
            with pool.Fori(1, PAIRS - 1) as i:
                for c in range(2):
                    head(i * 2 + c, c, True, i)
            head(HA - 2, 0, True)
            pool_chain.begin(base + (HA - 1) * 2 - 2)
            split_wo(HA - 2)
            pool_chain.begin(base + (HA - 1) * 2 - 1)
            more["pool"](pool)
            split_wo(HA - 1)

        @block.scalar
        def _(act):
            def qkv_tile(p, i):
                act.wait_ge(qkv_mm, p * 8 + (i + 1))
                if i == 0:
                    after(act, qk_t, p * 4)
                    after(act, v_lo_out, p)
                nc.scalar.activation(qkv[:, i, :], bank_of(p, i)[:, 0:C3], ACT.Copy).then_inc(qkv_out, 1)

            def qk_out(p, c, b):
                for r in range(2):
                    act.wait_ge(qk_t, p * 4 + (2 * b + r + 1))
                    if b == 0 and r == 0:
                        after(act, s_mm, (p - 1) * 8)
                    nc.scalar.activation(qk_hi[c][:, r, 512 * b:512 * (b + 1)],
                                         t_ps[r][:, :, :].rearrange("p a b -> p (a b)"), ACT.Copy,
                                         scale=scales[:, r:r + 1]).then_inc(qk_hi_out, 1)

            def v_out(p, c):
                act.wait_ge(qkv_out, p * 8 + 8)
                after(act, pv_mm, (p - 1) * 8)
                nc.scalar.activation(v_hi[c][:, :, :], qkv[:, :, 2 * DA:C3], ACT.Copy).then_inc(v_hi_out, 1)

            def exp_of(g, q, c, t):
                act.wait_ge(s_max, g + 1)
                after(act, p_t, g * 2 - 2)
                if t == 0:
                    after(act, rs_ready, (g - 8) // 8 if isinstance(g, int) else rs_before[0])
                nc.scalar.activation(probs[q][:, :], s_ps[q][:, :], ACT.Exp, bias=neg_max[:, q:q + 1],
                                     accum_out=sums[c][:, t:t + 1]).then_inc(s_exp, 1)

            rs_before = [None]

            def pt_out(g, t):
                J = t // 2
                for a in range(2):
                    act.wait_ge(p_t, g * 2 + (a + 1))
                    if t % 2 == 0 and a == 0:
                        after(act, pv_mm, g - 2)
                    nc.scalar.activation(pt_hi[J % 2][:, 4 * a:4 * a + 4, (t % 2) * P:(t % 2 + 1) * P],
                                         t_ps[a][:, :, :], ACT.Copy).then_inc(p_hi_out, 1)

            def o_out(J, j):
                act.wait_ge(pv_mm, J * 2 + 2)
                after(act, op_mm, J - 3)
                nc.scalar.activation(ot_hi[:, 2 * P * j:2 * P * (j + 1)], pv_ps[:, 0:2 * P], ACT.Copy)\
                    .then_inc(o_hi_out, 1)

            def head(h, par, prep):
                static = isinstance(h, int)
                for t in range(NT):
                    g = h * 8 + t
                    first = static and h == 0
                    if prep and t < 4:
                        qkv_tile(h + 1, 2 * t)
                    if not (first and t == 0):
                        pt_out(g - 1, (t - 1) % NT)
                    if t < NT - 1 or prep:
                        rs_before[0] = h
                        nt = (t + 1) % NT
                        exp_of(g + 1, (t + 1) % 2, par if t < NT - 1 else 1 - par, nt)
                    if prep and t < 4:
                        qkv_tile(h + 1, 2 * t + 1)
                    if t % 2 == 0 and not (first and t < 4):
                        j = (t // 2 + 2) % 4
                        o_out(h * 4 + (t // 2 - 2), j)
                    if prep and t in (3, 5):
                        qk_out(h + 1, 1 - par, (t - 3) // 2)
                    if prep and t == 4:
                        v_out(h + 1, 1 - par)

            act.wait_ge(const_in, const_loads * 16)
            for i in range(NT):
                qkv_tile(0, i)
            for b in range(2):
                qk_out(0, 0, b)
            v_out(0, 0)
            exp_of(0, 0, 0, 0)
            each_head(act, head)
            pt_out(8 * HA - 1, NT - 1)
            o_out(4 * HA - 2, 2)
            o_out(4 * HA - 1, 3)

        @block.vector
        def _(dve):
            chain = Chain(dve, chain_sem)

            def squares(p, i):
                dve.wait_ge(qkv_out, p * 8 + (i + 1))
                for r in range(2):
                    qk = qkv[:, i, r * DA:(r + 1) * DA]
                    last = nc.vector.tensor_tensor_reduce(out=junk[:, :], in0=qk, in1=qk, scale=1.0, scalar=0.0,
                                                          op0=ALU.mult, op1=ALU.add,
                                                          accum_out=ssq[:, i, r:r + 1])
                    chain(last)

            def mean_squares(p, b):
                tiles = slice(4 * b, 4 * b + 4)
                nc.vector.tensor_scalar(msq[:, tiles, :], ssq[:, tiles, :], 1.0 / DA, RMS_EPS,
                                        ALU.mult, ALU.add).then_inc(ms_ready, 1)

            def qk_out(p, c, b):
                for r in range(2):
                    dve.wait_ge(qk_hi_out, p * 4 + (2 * b + r + 1))
                    cols = slice(512 * b, 512 * (b + 1))
                    nc.vector.scalar_tensor_tensor(
                        out=qk_lo[c][:, r, cols], in0=t_ps[r][:, :, :].rearrange("p a b -> p (a b)"),
                        scalar=scales[:, r:r + 1], in1=f32(qk_hi[c][:, r, cols]),
                        op0=ALU.mult, op1=ALU.subtract).then_inc(qk_lo_out, 1)

            def max_of(g, q):
                dve.wait_ge(s_mm, g + 1)
                after(dve, s_exp, g - 1)
                nc.vector.tensor_reduce(neg_max[:, q:q + 1], s_ps[q][:, :], AX.X, ALU.max,
                                        negate=True).then_inc(s_max, 1)

            def pt_out(g, t):
                for a in range(2):
                    dve.wait_ge(p_hi_out, g * 2 + (a + 1))
                    where = (slice(None), slice(4 * a, 4 * a + 4), slice((t % 2) * P, (t % 2 + 1) * P))
                    nc.vector.tensor_tensor(pt_lo[t // 2 % 2][where], t_ps[a][:, :, :],
                                            f32(pt_hi[t // 2 % 2][where]), ALU.subtract).then_inc(p_lo_out, 1)

            def o_out(J, j):
                dve.wait_ge(o_hi_out, J + 1)
                cols = slice(2 * P * j, 2 * P * (j + 1))
                nc.vector.tensor_tensor(ot_lo[:, cols], pv_ps[:, 0:2 * P], f32(ot_hi[:, cols]),
                                        ALU.subtract).then_inc(o_lo_out, 1)

            def invert(h, c):
                dve.wait_ge(s_exp, h * 8 + 8)
                nc.vector.reciprocal(rsums[c][:, :], sums[c][:, :]).then_inc(rs_ready, 1)
                dve.wait_ge(rs_ready, h + 1)

            def project(h, c, j, bank=mm_ps):
                dve.wait_ge(op_mm, h * 4 + (j + 1))
                for k in range(2):
                    t = 2 * j + k
                    last = nc.vector.scalar_tensor_tensor(
                        out=m.x[:, t, :], in0=bank[:, k * E:(k + 1) * E], scalar=rsums[c][:, t:t + 1],
                        in1=m.x[:, t, :], op0=ALU.mult, op1=ALU.add)
                last.then_inc(op_out, 1)

            def head(h, par, prep):
                first = isinstance(h, int) and h == 0
                chain.begin(base + h * 16)
                for t in range(NT):
                    g = h * 8 + t
                    if t < NT - 1 or prep:
                        max_of(g + 1, (t + 1) % 2)
                    if t >= 4 and not first:
                        project(h - 1, 1 - par, t - 4)
                    if prep and t < 4:
                        squares(h + 1, 2 * t)
                    if not (first and t == 0):
                        pt_out(g - 1, (t - 1) % NT)
                    if t == 0 and not first:
                        invert(h - 1, 1 - par)
                    if prep and t < 4:
                        squares(h + 1, 2 * t + 1)
                        if t % 2:
                            mean_squares(h + 1, t // 2)
                    if t % 2 == 0 and not (first and t < 4):
                        o_out(h * 4 + (t // 2 - 2), (t // 2 + 2) % 4)
                    if prep and t in (3, 5):
                        qk_out(h + 1, 1 - par, (t - 3) // 2)

            for i in range(NT):
                squares(0, i)
                if i % 4 == 3:
                    mean_squares(0, i // 4)
            for b in range(2):
                qk_out(0, 0, b)
            max_of(0, 0)
            base = chain.n
            each_head(dve, head)
            pt_out(8 * HA - 1, NT - 1)
            o_out(4 * HA - 2, 2)
            o_out(4 * HA - 1, 3)
            invert(HA - 1, 1)
            for j in range(4):
                project(HA - 1, 1, j, last_bank(j))
                dve.wait_ge(op_out, 4 * HA - 3 + j)
                for t in (2 * j, 2 * j + 1):
                    nc.vector.bn_stats(m.stats[:, t, :], m.x[:, t, :])

        @block.tensor
        def _(pe):
            def qkv_tile(p, i):
                if i == 0:
                    pe.wait_ge(w_split, p + 1)
                    after(pe, op_out, (p - 2) * 4)
                    after(pe, qkv_out, p * 8)
                elif isinstance(p, int) and p == 0:
                    after(pe, qkv_out, i - 1)
                else:
                    pe.wait_ge(qkv_out, p * 8 + i)
                for e in range(NE):
                    rows = slice(i * P, (i + 1) * P)
                    last = three(nc, bank_of(p, i)[:, 0:C3], m.xnt_hi[:, e, rows], m.xnt_lo[:, e, rows],
                                 w_hi[:, e, :], w_lo[:, e, :], e == 0, e == NE - 1)
                last.then_inc(qkv_mm, 1)

            def qk_batch(p, b, g):
                pe.wait_ge(qk_scaled, p * 2 + (b + 1))
                for r in range(2):
                    if g is None:
                        after(pe, qk_lo_out, p * 4 + 2 * (b - 1) + r + 1)
                    else:
                        pe.wait_ge(p_lo_out, g * 2 + (r + 1))
                    for i in range(4):
                        last = nc.tensor.transpose(t_ps[r][:, i, :], qkv[:, 4 * b + i, r * DA:(r + 1) * DA],
                                                   m.ident[:, :])
                    last.then_inc(qk_t, 1)

            def scores(g, t, c):
                after(pe, s_exp, g - 1)
                for half in range(2):
                    cols = slice(512 * half, 512 * (half + 1))
                    rows = slice(t * P, (t + 1) * P)
                    last = three(nc, s_ps[t % 2][:, cols], qk_hi[c][:, 0, rows], qk_lo[c][:, 0, rows],
                                 qk_hi[c][:, 1, cols], qk_lo[c][:, 1, cols], True, True)
                last.then_inc(s_mm, 1)

            def transpose_p(g, t, qk_before):
                pe.wait_ge(s_exp, g + 1)
                for a in range(2):
                    after(pe, p_lo_out, g * 2 + (a - 1))
                    if qk_before is not None:
                        pe.wait_ge(qk_lo_out, qk_before + a)
                    for k in range(4):
                        kb = 4 * a + k
                        last = nc.tensor.transpose(t_ps[a][:, k, :], probs[t % 2][:, kb * P:(kb + 1) * P],
                                                   m.ident[:, :])
                    last.then_inc(p_t, 1)

            def pv_half(J, j, a, c):
                if a == 0:
                    pe.wait_ge(p_lo_out, J * 4 + 4)
                    after(pe, o_lo_out, J)
                    if j == 0:
                        pe.wait_ge(v_lo_out, pv_head[0] + 1)
                for k in range(4):
                    kb = 4 * a + k
                    last = three(nc, pv_ps[:, 0:2 * P], v_hi[c][:, kb, :], v_lo[c][:, kb, :],
                                 pt_hi[j % 2][:, kb, :], pt_lo[j % 2][:, kb, :], kb == 0, kb == NT - 1)
                last.then_inc(pv_mm, 1)

            pv_head = [0]

            def project(h, j, bank=mm_ps, last=False):
                if j == 0:
                    pe.wait_ge(wo_split, h + 1)
                pe.wait_ge(o_lo_out, h * 4 + (j + 1))
                after(pe, op_out, h * 4 + (j - 1 if last and j > 0 else j))
                for k in range(2):
                    rows = slice((2 * j + k) * P, (2 * j + k + 1) * P)
                    ins = three(nc, bank[:, k * E:(k + 1) * E], ot_hi[:, rows], ot_lo[:, rows],
                                wo_hi[:, :], wo_lo[:, :], True, True)
                ins.then_inc(op_mm, 1)

            def head(h, par, prep):
                first = isinstance(h, int) and h == 0
                for t in range(NT):
                    g = h * 8 + t
                    if t < NT - 1:
                        scores(g + 1, t + 1, par)
                    elif prep:
                        pe.wait_ge(qk_lo_out, h * 4 + 8)
                        scores(g + 1, 0, 1 - par)
                    if prep and t < 4:
                        qkv_tile(h + 1, 2 * t)
                    if t >= 4 and not first:
                        if t == 4 and prep:
                            pe.wait_ge(qkv_out, h * 8 + 16)
                        project(h - 1, t - 4)
                    if not (first and t == 0):
                        between = None
                        if t in (4, 6) and prep:
                            between = (h + 1) * 4 + (t - 3)
                        transpose_p(g - 1, (t - 1) % NT, between)
                    if not (first and t < 3):
                        s = t - 3
                        j = (s // 2) % 4
                        pv_head[0] = h if s >= 0 else h - 1
                        pv_half(h * 4 + s // 2, j, s % 2, par if s >= 0 else 1 - par)
                    if prep and t < 4:
                        qkv_tile(h + 1, 2 * t + 1)
                    if prep and t in (3, 5):
                        qk_batch(h + 1, (t - 3) // 2, g - 1)

            for i in range(NT):
                qkv_tile(0, i)
            for b in range(2):
                qk_batch(0, b, None)
            pe.wait_ge(qk_lo_out, 4)
            scores(0, 0, 0)
            each_head(pe, head)
            transpose_p(8 * HA - 1, NT - 1, None)
            pv_head[0] = HA - 1
            pv_half(4 * HA - 2, 2, 1, 1)
            pv_half(4 * HA - 1, 3, 0, 1)
            pv_half(4 * HA - 1, 3, 1, 1)
            for j in range(4):
                project(HA - 1, j, last_bank(j), last=True)


def mixture(nc, scope, tag, m, w13, w2a, w2b, shared, more=(), store=None):
    more = dict(more)
    mk = m.inner(scope, tag)
    sb, ps, sem = mk.sb, mk.ps, mk.sem
    w13_sb = sb("w13_sb", [P, EXPERTS, NE, 2 * INTER])
    w2_sb = sb("w2_sb", [P, EXPERTS, 2, E])
    rows_sb = [sb(f"rows{i}", [P, NT, W]) for i in range(2)]
    xn = rows_sb[0][:, :, 0:E]
    x_ps = [ps("x_ps0", [P, 512])]
    w_in, w2_zero, logits = sem("w_in"), sem("w2_zero"), sem("logits")
    R2 = INTER - P

    def load_weights(sp):
        if "sync" in more:
            more["sync"](sp)
        for c in range(4):
            es = slice(4 * c, 4 * c + 4)
            sp.dma_start(w13_sb[:, es, :, :], w13[:, es]).then_inc(w_in, 16)
        sp.dma_start(w2_sb[:, :, 0, :], w2a).then_inc(w_in, 16)
        sp.wait_ge(w2_zero, 1)
        sp.dma_start(w2_sb[0:R2, :, 1, :], w2b).then_inc(w_in, 16)

    def zero_rows(pool):
        nc.gpsimd.memset(w2_sb[:, :, 1, :], 0.0).then_inc(w2_zero, 1)

    def gate_pair(u):
        for t in (2 * u, 2 * u + 1):
            for e in range(NE):
                last = nc.tensor.matmul(x_ps[0][:, t * EXPERTS:(t + 1) * EXPERTS], m.xnt[:, e, t * P:(t + 1) * P],
                                        shared.gate[:, e, :], start=e == 0, stop=e == NE - 1)
        last.then_inc(logits, 1)

    with ExitStack() as inner:
        layer_norm(nc, inner, f"{tag}_ln", m, xn=xn, split_f32=True, per_pair=gate_pair,
                   more={"sync": load_weights, "pool": zero_rows})

    G = [P, NT, EXPERTS]
    shifted, prob, rest = sb("shifted", G), sb("prob", G), sb("rest", G)
    G2 = [P, 2, NT, EXPERTS]
    pick, hit2 = sb("pick", G2), sb("hit2", G2)
    hit = hit2[:, 0]
    chosen = sb("chosen", G, BF16)
    top, picked = sb("top", [P, 2, NT]), sb("picked", [P, 2, NT])
    total, rtotal, key = sb("total", [P, NT]), sb("rtotal", [P, NT]), sb("key", [P, NT])
    slot_i = sb("slot_i", [P, 2, NT], I32)
    over = rest[:, :, :].rearrange("p t e -> p (t e)").rearrange("p (e t) -> p e t", t=NT)
    scan = [sb(f"scan{i}", [P, 2 * EXPERTS]) for i in range(3)]
    count_b = sb("count_b", [1, BLOCKS, EXPERTS])
    owner = sb("owner", [1, BLOCKS])
    owner_i = sb("owner_i", [1, BLOCKS], I32)

    xg = [sb(f"xg{i}", [P, W]) for i in range(4)]
    dest_b = [sb(f"dest_b{i}", [P, 1], I32) for i in range(4)]
    xt = [sb(f"xt{i}", [P, NE, P]) for i in range(2)]
    hid_b = [sb(f"hid_b{i}", [P, 2 * P]) for i in range(2)]
    ht_b = [sb(f"ht_b{i}", [P, 2, P]) for i in range(2)]
    y_b = [sb(f"y_b{i}", [P, E]) for i in range(2)]
    back = [rows[:, :, 0:E] for rows in rows_sb]
    gated = [sb(f"gated{i}", [P, F]) for i in range(2)]
    act_b = [g[:, 0:INTER] for g in gated]
    hidden = [sb(f"hidden{i}", [P, 3 * P]) for i in range(2)]
    ht_hi = [sb(f"ht_hi{i}", [P, 3, P], F32R) for i in range(2)]
    ht_lo = [sb(f"ht_lo{i}", [P, 3, P], F32R) for i in range(2)]

    u_ps = [ps(f"u_ps{i}", [P, 512]) for i in range(2)]
    x_ps.append(ps("x_ps1", [P, 512]))
    h_ps = [ps(f"h_ps{i}", [P, 512]) for i in range(2)]
    y_ps = [ps(f"y_ps{i}", [P, 512]) for i in range(2)]

    consts, rows_copied, less_max, exped = sem("consts"), sem("rows_copied"), sem("less_max"), sem("exped")
    dests_set, b_dest = sem("dests_set"), sem("b_dest")
    chosen_set, counted, slots_set, owners_set = sem("chosen_set"), sem("counted"), sem("slots_set"), sem("owners_set")
    scattered, met = sem("scattered"), sem("met")
    gathered = [sem(f"gathered{i}") for i in range(NT // 2)]
    xg_in = [sem(f"xg_in{i}") for i in range(4)]
    b_xt, b_xt_out, b_up, b_silu, b_hid = sem("b_xt"), sem("b_xt_out"), sem("b_up"), sem("b_silu"), sem("b_hid")
    b_ht, b_ht_out, b_y, b_y_out = sem("b_ht"), sem("b_ht_out"), sem("b_y"), sem("b_y_out")
    b_stored = [sem(f"b_stored{i}") for i in range(2)]
    a_mm, b_mm, silu_out, h_out, h_t = sem("a_mm"), sem("b_mm"), sem("silu_out"), sem("h_out"), sem("h_t")
    h_hi_out, h_lo_out, y_mm, y_out = sem("h_hi_out"), sem("h_lo_out"), sem("y_mm"), sem("y_out")
    x_out, stored, chain_sem = sem("x_out"), sem("stored"), sem("chain")
    EARLY = 6

    def bc(ap):
        return ap.unsqueeze(2).broadcast_to(G)

    def steps_of_blocks(eng, step):
        eights = (BLOCKS - 5) // 8
        step(1, 1)
        step(2, 2)
        with eng.Fori(0, eights) as i:
            for k in range(3, 11):
                step(i * 8 + k, k % 4)
        for b in range(3 + 8 * eights, BLOCKS - 2):
            step(b, b % 4)

    with nc.Block() as block:
        @block.sync
        def _(sp):
            def load(b, c):
                src = m.xs[tag][ds(b, 1)].rearrange("a p c -> (a p) c")
                sp.dma_start(xg[c][:, :], src).then_inc(xg_in[c], 16)

            sp.wait_ge(scattered, 16 * 2 * NT)
            for b in range(4):
                load(b, b)

            def step(b, c):
                if not (isinstance(b, int) and b + 4 >= BLOCKS):
                    sp.wait_ge(b_xt, b + 1)
                    sp.wait_ge(b_dest, b + 1)
                    load(b + 4, c)

            step(0, 0)
            steps_of_blocks(sp, step)
            sp.wait_ge(b_stored[0], 16 * ((BLOCKS + 1) // 2))
            sp.wait_ge(b_stored[1], 16 * (BLOCKS // 2))
            results = m.ys[0:2 * N].rearrange("(p t i) c -> p i t c", t=NT, i=2)
            for h in range(NT // 2):
                tiles = slice(2 * h, 2 * h + 2)
                for i in range(2):
                    sp.dma_start(back[i][:, tiles, :], results[:, i, tiles, :]).then_inc(gathered[h], 16)
            for h in range(NT // 2):
                sp.wait_ge(gathered[h], 32)
            if store is not None:
                for t in range(NT):
                    sp.wait_ge(x_out, t + 1)
                    sp.dma_start(store[:, t, :], m.x[:, t, :]).then_inc(stored, 16)
                sp.wait_ge(stored, 16 * NT)

        @block.gpsimd
        def _(pool):
            for i in range(2):
                nc.gpsimd.memset(hidden[i][:, F:3 * P], 0.0)
                nc.gpsimd.memset(hid_b[i][:, INTER:2 * P], 0.0)
            for i in range(3):
                nc.gpsimd.memset(scan[i][:, 0:EXPERTS], 0.0)
            for b in range(BLOCKS):
                last = nc.gpsimd.memset(count_b[:, b, :], float(b))
            last.then_inc(consts, 1)
            for i in range(2):
                nc.gpsimd.tensor_copy(rows_sb[i][:, :, E:E + 1].bitcast(I32), m.dest[:, i, :].unsqueeze(2))\
                    .then_inc(dests_set, 1)
            pool.wait_ge(dests_set, 2)
            pool.wait_ge(rows_copied, 1)
            pool.wait_ge(slots_set, 1)
            for t in range(NT):
                for i in range(2):
                    nc.gpsimd.indirect_dma_start(m.xs[tag].rearrange("b p c -> (b p) c"),
                                                 bass.IndirectOffsetOnAxis(ap=slot_i[:, i, t:t + 1], axis=0),
                                                 rows_sb[i][:, t, :], None).then_inc(scattered, 16)

            if "pool" in more:
                more["pool"](pool)

            def send(b, c):
                pool.wait_ge(b_dest, b + 1)
                pool.wait_ge(b_y_out, b + 1)
                own_slot(pool, met)
                nc.gpsimd.indirect_dma_start(m.ys, bass.IndirectOffsetOnAxis(ap=dest_b[c][:, :], axis=0),
                                             y_b[c % 2][:, :], None).then_inc(b_stored[c % 2], 16)

            send(0, 0)
            steps_of_blocks(pool, send)
            for b in range(BLOCKS - 2, BLOCKS):
                send(b, b % 4)

        @block.scalar
        def _(act):
            nc.scalar.activation(rows_sb[1][:, :, 0:E], xn, ACT.Copy).then_inc(rows_copied, 1)
            act.wait_ge(less_max, 1)
            nc.scalar.activation(prob[:, :, :], shifted[:, :, :], ACT.Exp).then_inc(exped, 1)

            def shared_tile(t):
                act.wait_ge(a_mm, t + 1)
                after(act, h_out, t - 1)
                nc.scalar.activation(gated[t % 2][:, :], u_ps[0][:, 0:F], ACT.Silu).then_inc(silu_out, 1)
                act.wait_ge(h_t, t + 1)
                after(act, y_mm, t - 1)
                nc.scalar.activation(ht_hi[t % 2][:, :, :].rearrange("p a b -> p (a b)"), h_ps[0][:, 0:3 * P],
                                     ACT.Copy).then_inc(h_hi_out, 1)

            for t in range(EARLY):
                shared_tile(t)

            def xt_out(b, c):
                c %= 2
                act.wait_ge(b_xt, b + 1)
                after(act, b_up, b - 1)
                nc.scalar.activation(xt[c][:, :, :].rearrange("p a b -> p (a b)"), x_ps[c][:, 0:E], ACT.Copy)\
                    .then_inc(b_xt_out, 1)

            def silu(b, c):
                c %= 2
                act.wait_ge(b_up, b + 1)
                after(act, b_hid, b - 1)
                nc.scalar.activation(act_b[c], u_ps[c][:, 0:INTER], ACT.Silu).then_inc(b_silu, 1)

            def y_of(b, c):
                c %= 2
                act.wait_ge(b_y, b + 1)
                if not (isinstance(b, int) and b < 2):
                    act.wait_ge(b_stored[c], stored_before(b, c))
                nc.scalar.activation(y_b[c][:, :], y_ps[c][:, 0:E], ACT.Copy).then_inc(b_y_out, 1)

            def stored_before(b, c):
                return 16 * (b // 2) if isinstance(b, int) else (b - c) * 8

            xt_out(0, 0)
            xt_out(1, 1)
            silu(0, 0)

            silu(1, 1)
            xt_out(2, 0)

            def step(b, c):
                silu(b + 1, (c + 1) % 4)
                xt_out(b + 2, (c + 2) % 4)
                y_of(b - 1, (c + 3) % 4)

            steps_of_blocks(act, step)
            b = BLOCKS - 2
            silu(b + 1, (b + 1) % 2)
            y_of(b - 1, (b - 1) % 2)
            y_of(b, b % 2)
            y_of(b + 1, (b + 1) % 2)
            for t in range(EARLY, NT):
                shared_tile(t)
            if "scalar" in more:
                more["scalar"](act)

        @block.vector
        def _(dve):
            chain = Chain(dve, chain_sem)
            V = nc.vector
            dve.wait_ge(logits, NT // 2)
            lg = x_ps[0][:, 0:NT * EXPERTS].rearrange("p (t e) -> p t e", e=EXPERTS)
            rank = m.rank[:, :].unsqueeze(1).broadcast_to(G)
            chain(V.tensor_reduce(key[:, :], lg, AX.X, ALU.max))
            V.tensor_tensor(shifted[:, :, :], lg, bc(key[:, :]), ALU.subtract).then_inc(less_max, 1)
            dve.wait_ge(less_max, 1)
            chain(V.scalar_tensor_tensor(out=hit, in0=shifted[:, :, :], scalar=0.0, in1=rank,
                                         op0=ALU.is_equal, op1=ALU.mult))
            chain(V.tensor_reduce(key[:, :], hit, AX.X, ALU.max))
            chain(V.tensor_tensor(pick[:, 0], hit, bc(key[:, :]), ALU.is_equal))
            chain(V.scalar_tensor_tensor(out=rest[:, :, :], in0=pick[:, 0], scalar=MASKED,
                                         in1=shifted[:, :, :], op0=ALU.mult, op1=ALU.add))
            chain(V.tensor_reduce(key[:, :], rest[:, :, :], AX.X, ALU.max))
            chain(V.tensor_tensor(hit, rest[:, :, :], bc(key[:, :]), ALU.is_equal))
            chain(V.tensor_tensor(hit, hit, rank, ALU.mult))
            chain(V.tensor_reduce(key[:, :], hit, AX.X, ALU.max))
            chain(V.tensor_tensor(pick[:, 1], hit, bc(key[:, :]), ALU.is_equal))
            V.tensor_tensor(chosen[:, :, :], pick[:, 0], pick[:, 1], ALU.add).then_inc(chosen_set, 1)

            dve.wait_ge(counted, 1)
            earlier = x_ps[1][:, 0:NT * EXPERTS].rearrange("p (t e) -> p t e", e=EXPERTS)
            counts = x_ps[1][:, NT * EXPERTS:NT * EXPERTS + EXPERTS]
            chain(V.tensor_tensor(over, counts.unsqueeze(2).broadcast_to([P, EXPERTS, NT]),
                                  m.steps[:, :].unsqueeze(1).broadcast_to([P, EXPERTS, NT]), ALU.is_gt))
            dve.wait_ge(consts, 1)
            chain(V.tensor_reduce(scan[0][:, EXPERTS:2 * EXPERTS], over, AX.X, ALU.add))
            for k in range(4):
                a, b, s = scan[(0, 1, 2, 1)[k]], scan[(1, 2, 1, 2)[k]], 1 << k
                chain(V.tensor_tensor(b[:, EXPERTS:2 * EXPERTS], a[:, EXPERTS:2 * EXPERTS],
                                      a[:, EXPERTS - s:2 * EXPERTS - s], ALU.add))
            ends = scan[2][:, EXPERTS:2 * EXPERTS]
            starts = scan[2][:, EXPERTS - 1:2 * EXPERTS - 1]
            chain(V.scalar_tensor_tensor(out=rest[:, :, :], in0=starts.unsqueeze(1).broadcast_to(G),
                                         scalar=float(P), in1=earlier, op0=ALU.mult, op1=ALU.add))
            chain(V.tensor_tensor(hit2[:, :, :, :], rest[:, :, :].unsqueeze(1).broadcast_to(G2), pick[:, :, :, :],
                                  ALU.mult))
            chain(V.tensor_reduce(picked[:, :, :], hit2[:, :, :, :], AX.X, ALU.add))
            V.tensor_copy(slot_i[:, :, :], picked[:, :, :]).then_inc(slots_set, 1)

            def set_owners():
                chain(V.tensor_tensor(count_b[:, :, :], ends[0:1, :].unsqueeze(1).broadcast_to([1, BLOCKS, EXPERTS]),
                                      count_b[:, :, :], ALU.is_le))
                chain(V.tensor_reduce(owner[:, :], count_b[:, :, :], AX.X, ALU.add))
                V.tensor_scalar(owner_i[:, :], owner[:, :], float(EXPERTS - 1), None, ALU.min).then_inc(owners_set, 1)

            def set_weights():
                dve.wait_ge(exped, 1)
                dve.wait_ge(slots_set, 1)
                chain(V.tensor_reduce(total[:, :], prob[:, :, :], AX.X, ALU.add))
                chain(V.reciprocal(rtotal[:, :], total[:, :]))
                chain(V.tensor_tensor(hit2[:, :, :, :], prob[:, :, :].unsqueeze(1).broadcast_to(G2), pick[:, :, :, :],
                                      ALU.mult))
                chain(V.tensor_reduce(picked[:, :, :], hit2[:, :, :, :], AX.X, ALU.add))
                chain(V.tensor_tensor(top[:, :, :], picked[:, :, :], rtotal[:, :].unsqueeze(1).broadcast_to([P, 2, NT]),
                                      ALU.mult))

            def shared_tile(t):
                q = t % 2
                dve.wait_ge(silu_out, t + 1)
                dve.wait_ge(b_mm, t + 1)
                after(dve, h_t, t - 1)
                V.tensor_tensor(hidden[q][:, 0:F], gated[q][:, :], u_ps[1][:, 0:F], ALU.mult).then_inc(h_out, 1)
                dve.wait_ge(h_hi_out, t + 1)
                V.tensor_tensor(ht_lo[q][:, :, :].rearrange("p a b -> p (a b)"), h_ps[0][:, 0:3 * P],
                                f32(ht_hi[q][:, :, :]).rearrange("p a b -> p (a b)"),
                                ALU.subtract).then_inc(h_lo_out, 1)

            def shared_add(t):
                dve.wait_ge(y_mm, t + 1)
                V.tensor_tensor(m.x[:, t, :], m.x[:, t, :], y_ps[t % 2][:, 0:E], ALU.add).then_inc(y_out, 1)

            for t in range(EARLY):
                shared_tile(t)
                if t == 1:
                    set_owners()
                if t == 2:
                    set_weights()
                if t:
                    shared_add(t - 1)
            shared_add(EARLY - 1)

            def hid(b, c):
                c %= 2
                dve.wait_ge(b_silu, b + 1)
                after(dve, b_ht, b - 1)
                V.tensor_tensor(hid_b[c][:, 0:INTER], act_b[c], u_ps[c][:, INTER:2 * INTER],
                                ALU.mult).then_inc(b_hid, 1)

            def ht_of(b, c):
                c %= 2
                dve.wait_ge(b_ht, b + 1)
                after(dve, b_y, b - 1)
                V.tensor_copy(ht_b[c][:, :, :].rearrange("p a b -> p (a b)"), h_ps[c][:, 0:2 * P])\
                    .then_inc(b_ht_out, 1)

            def dest_of(b, c):
                dve.wait_ge(b_xt, b + 1)
                if not (isinstance(b, int) and b < 4):
                    dve.wait_ge(b_stored[c % 2], 16 * (b // 2 - 1) if isinstance(b, int) else (b - c % 2) * 8 - 16)
                V.tensor_copy(dest_b[c][:, :], xg[c][:, E:E + 1].bitcast(I32)).then_inc(b_dest, 1)

            hid(0, 0)
            dest_of(0, 0)
            ht_of(0, 0)
            hid(1, 1)

            def step(b, c):
                dest_of(b, c)
                ht_of(b, c)
                hid(b + 1, (c + 1) % 4)

            steps_of_blocks(dve, step)
            step(BLOCKS - 2, (BLOCKS - 2) % 4)
            dest_of(BLOCKS - 1, (BLOCKS - 1) % 4)
            ht_of(BLOCKS - 1, (BLOCKS - 1) % 2)
            for t in range(EARLY, NT):
                shared_tile(t)
                if t > EARLY:
                    shared_add(t - 1)
            shared_add(NT - 1)
            if "vector" in more:
                more["vector"](dve)
            dve.wait_ge(y_out, NT)
            for h in range(NT // 2):
                dve.wait_ge(gathered[h], 32)
                for i in range(2):
                    for t in range(2 * h, 2 * h + 2):
                        last = V.scalar_tensor_tensor(out=m.x[:, t, :], in0=back[i][:, t, :],
                                                      scalar=top[:, i, t:t + 1], in1=m.x[:, t, :],
                                                      op0=ALU.mult, op1=ALU.add)
                        if i == 1:
                            last.then_inc(x_out, 1)
                    if i == 0:
                        chain(last)
                if store is None:
                    for t in range(2 * h, 2 * h + 2):
                        dve.wait_ge(x_out, t + 1)
                        V.bn_stats(m.stats[:, t, :], m.x[:, t, :])

        @block.tensor
        def _(pe):
            def count():
                pe.wait_ge(chosen_set, 1)
                out = x_ps[1]
                W = NT * EXPERTS
                ch = chosen[:, :, :].rearrange("p t e -> p (t e)")
                nc.tensor.matmul(out[:, 0:W], m.before[:, :], ch, start=True, stop=False, skip_group_check=True)
                for s in range(1, NT):
                    nc.tensor.matmul(out[:, s * EXPERTS:W], m.ones_bf[:, :], ch[:, 0:W - s * EXPERTS],
                                     start=False, stop=False, skip_group_check=True)
                for t in range(NT):
                    last = nc.tensor.matmul(out[:, W:W + EXPERTS], m.ones_bf[:, :],
                                            ch[:, t * EXPERTS:(t + 1) * EXPERTS],
                                            start=False, stop=t == NT - 1, skip_group_check=True)
                last.then_inc(counted, 1)

            def shared_up(t):
                rows = slice(t * P, (t + 1) * P)
                if t == EARLY:
                    pe.wait_ge(b_hid, BLOCKS)
                for i, free, done in ((0, silu_out, a_mm), (1, h_out, b_mm)):
                    after(pe, free, t)
                    for e in range(NE):
                        last = three(nc, u_ps[i][:, 0:F], m.xnt_hi[:, e, rows], m.xnt_lo[:, e, rows],
                                     shared.hi13[:, e, i * F:(i + 1) * F], shared.lo13[:, e, i * F:(i + 1) * F],
                                     e == 0, e == NE - 1)
                    last.then_inc(done, 1)

            def shared_ht(t):
                pe.wait_ge(h_out, t + 1)
                after(pe, h_lo_out, t)
                if t == EARLY:
                    pe.wait_ge(b_ht_out, BLOCKS)
                for k in range(3):
                    last = nc.tensor.transpose(h_ps[0][:, k * P:(k + 1) * P], hidden[t % 2][:, k * P:(k + 1) * P],
                                               m.ident[:, :])
                last.then_inc(h_t, 1)

            def shared_down(t):
                pe.wait_ge(h_lo_out, t + 1)
                after(pe, y_out, t - 1)
                if t == EARLY:
                    pe.wait_ge(b_y_out, BLOCKS)
                q = t % 2
                for k in range(3):
                    r = P if k < 2 else F3
                    last = three(nc, y_ps[q][:, 0:E], ht_hi[q][0:r, k, :], ht_lo[q][0:r, k, :],
                                 shared.hi2[0:r, k, :], shared.lo2[0:r, k, :], k == 0, k == 2)
                last.then_inc(y_mm, 1)

            def shared_tiles(t0, t1, between):
                for t in range(t0, t1):
                    shared_up(t)
                    if t > t0:
                        shared_down(t - 1)
                    if t == t0:
                        between()
                    shared_ht(t)
                shared_down(t1 - 1)

            shared_tiles(0, EARLY, count)

            def expert_of(b):
                return pe.value_load(owner_i[0:1, b:b + 1] if isinstance(b, int) else owner_i[0:1, ds(b, 1)],
                                     min_val=0, max_val=EXPERTS - 1)

            def x_t(b, c):
                pe.wait_ge(xg_in[c], 16 * (b // 4) + 16 if isinstance(b, int) else (b - c) * 4 + 16)
                after(pe, b_xt_out, b - 1)
                for e in range(NE):
                    cols = slice(e * P, (e + 1) * P)
                    last = nc.tensor.transpose(x_ps[c % 2][:, cols], xg[c][:, cols], m.ident[:, :])
                last.then_inc(b_xt, 1)

            def up(b, c):
                c %= 2
                e = expert_of(b)
                pe.wait_ge(b_xt_out, b + 1)
                after(pe, b_hid, b - 1)
                for k in range(NE):
                    w = w13_sb[:, ds(e, 1), k, :].rearrange("p a c -> p (a c)")
                    last = nc.tensor.matmul(u_ps[c][:, 0:2 * INTER], xt[c][:, k, :], w, start=k == 0, stop=k == NE - 1)
                last.then_inc(b_up, 1)

            def h_tr(b, c):
                c %= 2
                pe.wait_ge(b_hid, b + 1)
                after(pe, b_ht_out, b - 1)
                for k in range(2):
                    cols = slice(k * P, (k + 1) * P)
                    last = nc.tensor.transpose(h_ps[c][:, cols], hid_b[c][:, cols], m.ident[:, :])
                last.then_inc(b_ht, 1)

            def down(b, c):
                c %= 2
                e = expert_of(b)
                pe.wait_ge(b_ht_out, b + 1)
                after(pe, b_y_out, b - 1)
                for k in range(2):
                    w = w2_sb[:, ds(e, 1), k, :].rearrange("p a c -> p (a c)")
                    last = nc.tensor.matmul(y_ps[c][:, 0:E], ht_b[c][:, k, :], w, start=k == 0, stop=k == 1)
                last.then_inc(b_y, 1)

            pe.wait_ge(owners_set, 1)
            pe.wait_ge(w_in, 16 * 6)
            pe.wait_ge(h_lo_out, EARLY)
            pe.wait_ge(y_out, EARLY)
            x_t(0, 0)
            x_t(1, 1)
            up(0, 0)
            up(1, 1)
            x_t(2, 2)
            h_tr(0, 0)

            def step(b, c):
                up(b + 1, (c + 1) % 4)
                x_t(b + 2, (c + 2) % 4)
                down(b - 1, (c + 3) % 4)
                h_tr(b, c)

            steps_of_blocks(pe, step)
            b = BLOCKS - 2
            up(b + 1, (b + 1) % 2)
            down(b - 1, (b - 1) % 2)
            h_tr(b, b % 2)
            down(b, b % 2)
            h_tr(b + 1, (b + 1) % 2)
            down(b + 1, (b + 1) % 2)
            shared_tiles(EARLY, NT, lambda: None)


def attention_b(nc, scope, m, w, w_proj, b_proj):
    mk = m.inner(scope, "b")
    S = 6 * DB
    VW = 32
    GH = 4
    wp_raw = mk.sb("wp_raw", [P, NE, E])
    wp_hi, wp_lo = mk.sb("wp_hi", [P, NE, E], F32R), mk.sb("wp_lo", [P, NE, E], F32R)
    out_bias = mk.sb("out_bias", [P, E])
    v_ext = mk.sb("v_ext", [P, NT, HB, VW])
    qst = mk.sb("qst", [P, HB, N], BF16)
    kst = mk.sb("kst", [P, HB, N], BF16)
    o_sb = mk.sb("o_sb", [P, NT, E])

    QS = "hmlhmh"
    KS = "hhhmml"
    with ExitStack() as inner:
        pk = m.inner(inner, "bp")
        NB = 3
        res = [pk.sb(f"res{i}", [P, 2, HB, DB]) for i in range(2)]
        stack = [pk.sb(f"stack{i}", [P, 2, HB, 8, DB], BF16) for i in range(NB)]
        qk_ps = [pk.ps(f"qk_ps{i}", [P, 512]) for i in range(2)]
        v_ps = [pk.ps(f"v_ps{i}", [P, 512]) for i in range(2)]
        st_ps = [pk.ps(f"st_ps{i}", [P, 8, P], BF16) for i in range(4)]
        zeros_set, v_set = pk.sem("zeros_set"), pk.sem("v_set")
        qkv_mm, v_out, high, resid, mid, low = (pk.sem("qkv_mm"), pk.sem("v_out"), pk.sem("high"), pk.sem("resid"),
                                                pk.sem("mid"), pk.sem("low"))
        high_copied, stacked, st_t = pk.sem("high_copied"), pk.sem("stacked"), pk.sem("st_t")
        q_stored, k_stored = pk.sem("q_stored"), pk.sem("k_stored")

        def qk_of(t):
            return qk_ps[t % 2][:, :].rearrange("p (r h d) -> p r h d", r=2, d=DB)

        with nc.Block() as block:
            @block.gpsimd
            def _(pool):
                for b in range(NB):
                    nc.gpsimd.memset(stack[b][:, :, :, S // DB:8, :], 0.0).then_inc(zeros_set, 1)
                pool.wait_ge(zeros_set, NB)
                for b in range(NB):
                    for i in range(GH):
                        sel = stack[b][:, 1, :, S // DB, :].rearrange("p (g h) (k j) -> p h j g k", h=GH, j=GH)
                        nc.gpsimd.memset(sel[:, i, i, :, 0:3], 1.0)
                nc.gpsimd.memset(v_ext[:, :, :, DB:DB + 1], 1.0)
                nc.gpsimd.memset(v_ext[:, :, :, DB + 1:VW], 0.0).then_inc(v_set, 1)
                for t in range(NT):
                    s = stack[t % NB]
                    pool.wait_ge(high, t + 1)
                    for i in (3, 5):
                        nc.gpsimd.tensor_copy(s[:, 0, :, i, :], s[:, 0, :, 0, :])
                    for i in (1, 2):
                        last = nc.gpsimd.tensor_copy(s[:, 1, :, i, :], s[:, 1, :, 0, :])
                    last.then_inc(high_copied, 1)

            @block.scalar
            def _(act):
                def store(t, k):
                    act.wait_ge(st_t, t * 4 + k + 1)
                    nc.scalar.activation(qst[:, 8 * k:8 * k + 8, t * P:(t + 1) * P], st_ps[k][:, :, :],
                                         ACT.Copy).then_inc(q_stored, 1)

                act.wait_ge(v_set, 1)
                for t in range(NT + 2):
                    if t < NT:
                        act.wait_ge(qkv_mm, t + 1)
                        after(act, st_t, (t - NB + 1) * 4)
                        nc.scalar.activation(stack[t % NB][:, :, :, 0, :], qk_of(t), ACT.Copy).then_inc(high, 1)
                    if t >= 2:
                        store(t - 2, 0)
                    if t < NT:
                        act.wait_ge(resid, t + 1)
                        nc.scalar.activation(stack[t % NB][:, :, :, 4, :], res[t % 2][:, :, :, :], ACT.Copy)\
                            .then_inc(mid, 1)
                        nc.scalar.activation(v_ext[:, t, :, 0:DB],
                                             v_ps[t % 2][:, 0:E].rearrange("p (h d) -> p h d", d=DB), ACT.Copy)\
                            .then_inc(v_out, 1)
                    if t >= 2:
                        store(t - 2, 1)

            @block.vector
            def _(dve):
                def store(t, k):
                    dve.wait_ge(st_t, t * 4 + k + 3)
                    nc.vector.tensor_copy(kst[:, 8 * k:8 * k + 8, t * P:(t + 1) * P], st_ps[2 + k][:, :, :])\
                        .then_inc(k_stored, 1)

                for t in range(NT + 2):
                    s = stack[t % NB]
                    if t < NT:
                        dve.wait_ge(high, t + 1)
                        after(dve, low, t - 1)
                        nc.vector.tensor_tensor(res[t % 2][:, :, :, :], qk_of(t), s[:, :, :, 0, :],
                                                ALU.subtract).then_inc(resid, 1)
                    if t >= 2:
                        store(t - 2, 0)
                    if t < NT:
                        dve.wait_ge(mid, t + 1)
                        for r, letters in ((0, QS), (1, KS)):
                            last = nc.vector.tensor_tensor(s[:, r, :, letters.index("l"), :], res[t % 2][:, r, :, :],
                                                           s[:, r, :, 4, :], ALU.subtract)
                        last.then_inc(low, 1)
                        for r, letters in ((0, QS), (1, KS)):
                            last = nc.vector.tensor_copy(s[:, r, :, letters.index("m"), :], s[:, r, :, 4, :])
                        last.then_inc(stacked, 1)
                    if t >= 2:
                        store(t - 2, 1)

            @block.tensor
            def _(pe):
                def project(t):
                    after(pe, resid, t - 1)
                    after(pe, v_out, t - 1)
                    rows = slice(t * P, (t + 1) * P)
                    for bank, cols in ((qk_ps[t % 2][:, :], slice(0, 2 * E)),
                                       (v_ps[t % 2][:, 0:E], slice(2 * E, 3 * E))):
                        for e in range(NE):
                            three(nc, bank, m.xnt_hi[:, e, rows], m.xnt_lo[:, e, rows],
                                  w.hi[:, e, cols], w.lo[:, e, cols], e == 0, False)
                        nc.tensor.matmul(bank, w.ones[:, :], w.bias_hi[:, cols], start=False, stop=False)
                        last = nc.tensor.matmul(bank, w.ones[:, :], w.bias_lo[:, cols], start=False, stop=True)
                    last.then_inc(qkv_mm, 1)

                def transpose_stacks(t):
                    pe.wait_ge(stacked, t + 1)
                    pe.wait_ge(high_copied, t + 1)
                    for k in range(4):
                        after(pe, q_stored if k < 2 else k_stored, t * 2 - 1 + k % 2)
                        for i in range(8):
                            last = nc.tensor.transpose(
                                st_ps[k][:, i, :],
                                stack[t % NB][:, k // 2, 8 * (k % 2) + i, :, :].rearrange("p s d -> p (s d)"),
                                m.ident_bf[:, :])
                        last.then_inc(st_t, 1)

                for t in range(NT + 2):
                    if t < NT:
                        project(t)
                    if t >= 2:
                        transpose_stacks(t - 2)

    with ExitStack() as inner:
        ak = m.inner(inner, "ba")
        HALF = NT // 2
        C = N // 2
        vg = ak.sb("vg", [P, NT, GH * VW])
        pt = [[ak.sb(f"pt{j}{i}", [P, N]) for i in range(GH)] for j in range(2)]
        neg = [ak.sb(f"neg{k}", [P, NT, GH]) for k in range(2)]
        rest = ak.sb("rest", [P, HALF, GH])
        parts = [ak.sb(f"parts{k}", [P, HALF, VW], BF16) for k in range(2)]
        parts_t = ak.sb("parts_t", [P, C], BF16)
        ot = [ak.sb(f"ot{i}", [P, C]) for i in range(2)]
        rsum = ak.sb("rsum", [P, HALF, GH])
        max_ps = [ak.ps(f"max_ps{i}", [P, 512]) for i in range(2)]
        st_ps = [ak.ps(f"st_ps{i}", [P, N]) for i in range(2)]
        pv_ps = ak.ps("pv_ps", [P, 512])
        mix_ps = ak.ps("mix_ps", [P, 512])
        V_PARTS = [(slice(0, 4), 3), (slice(4, 6), 4), (slice(6, 8), 5)]
        met, parts_zero, vg_ready = ak.sem("met"), ak.sem("parts_zero"), ak.sem("vg_ready")
        max_mm = ak.sem("max_mm")
        max_out = ak.sem("max_out")
        parts_set = ak.sem("parts_set")
        parts_mm = ak.sem("parts_mm")
        parts_out = ak.sem("parts_out")
        folded = ak.sem("folded")
        st_mm = ak.sem("st_mm")
        st_exp = ak.sem("st_exp")
        pv_mm = ak.sem("pv_mm")
        ot_out = ak.sem("ot_out")
        ob_t = ak.sem("ob_t")
        o_out = ak.sem("o_out")
        rs, chain_sem = ak.sem("rs"), ak.sem("chain")
        GROUPS = HB // GH

        def units_of(t, c0, c1):
            per = min(GH, C // (c1 - c0))
            return [(t, range(i, i + per), c0, c1) for i in range(0, GH, per)]

        max_units = [u for t in range(HALF) for u in units_of(t, 0, (t + 1) * P)]
        MA = len(max_units)
        for t in range(HALF, NT):
            max_units += units_of(t, 0, C) + units_of(t, C, (t + 1) * P)
        MU = len(max_units)
        assert MU % 2 == 0

        def tile_of(c, kb, offset):
            return (kb, min(C, (c + 1) * C - kb * P), offset)

        slots2 = []
        for c in range(2):
            for kb in range(0, (c + 1) * HALF, 2):
                first = tile_of(c, kb, 0)
                slots2.append((c, [first, tile_of(c, kb + 1, first[1])]))
        SL = len(slots2)
        FIRST = [j for j in range(SL) if j == 0 or slots2[j][0] != slots2[j - 1][0]]
        LAST = [FIRST[1] - 1, SL - 1]
        PU = SL * GH
        assert SL % 2 == 0

        PIECES = 4
        LAG = GH + 1
        EARLY = FIRST[1] * GH

        def max_steps(g, u):
            if isinstance(g, int) and g == 0:
                n, k = EARLY - 2, MU - MA
                if u < n:
                    return [(0, MA + i) for i in range(k * u // n, k * (u + 1) // n)]
                n = PU - EARLY
                u = max(u, EARLY) - EARLY if u >= EARLY else -1
                return [(1, i) for i in range(MU * u // n, MU * (u + 1) // n)] if u >= 0 else []
            if last_group(g):
                return []
            return [(g + 1, i) for i in range(MU * u // PU, MU * (u + 1) // PU)]

        def at(g, first, others):
            return first if isinstance(g, int) and g == 0 else others

        def of_heads(tensor, g, i, rows, c0, c1):
            return tensor[rows, g * GH + i, c0:c1] if isinstance(g, int) else \
                tensor[rows, ds(g * GH + i, 1), c0:c1].rearrange("p a c -> p (a c)")

        def over_groups(eng, group):
            group(0)
            with eng.Fori(1, GROUPS - 1) as g:
                group(g)
            group(GROUPS - 1)

        def last_group(g):
            return isinstance(g, int) and g == GROUPS - 1

        wp_in, wp_hi_set, wp_lo_set, biased = (ak.sem("wp_in"), ak.sem("wp_hi_set"), ak.sem("wp_lo_set"),
                                               ak.sem("biased"))

        with nc.Block() as block:
            @block.sync
            def _(sp):
                sp.dma_start(wp_raw[:, :, :], w_proj).then_inc(wp_in, 16)
                sp.dma_start(out_bias[:, :], b_proj.broadcast_to([P, E])).then_inc(wp_in, 16)

            @block.gpsimd
            def _(pool):
                for k in range(2):
                    last = nc.gpsimd.memset(parts[k][:, :, :], 0.0)
                last.then_inc(parts_zero, 1)

                def group(g):
                    for tiles, slot in V_PARTS:
                        after(pool, pv_mm, (g * SL + (slot + 1 - SL)) * PIECES)
                        src = v_ext[:, tiles, g * GH:(g + 1) * GH, :] if isinstance(g, int) else \
                            v_ext[:, tiles, ds(g * GH, GH), :]
                        own_slot(pool, met)
                        nc.gpsimd.tensor_copy(vg[:, tiles, :].rearrange("p t (h d) -> p t h d", d=VW), src)\
                            .then_inc(vg_ready, 1)
                over_groups(pool, group)

            @block.scalar
            def _(act):
                def copy_parts(n):
                    act.wait_ge(parts_mm, n + 1)
                    after(act, folded, n)
                    nc.scalar.activation(parts_t[S:P, :], mix_ps[S:P, :], ACT.Copy).then_inc(parts_out, 1)

                def exp_of(g, u):
                    j, i = u // GH, u % GH
                    act.wait_ge(st_mm, g * PU + u + 1)
                    after(act, pv_mm, (g * SL + (j - 1)) * PIECES)
                    w = sum(w for _, w, _ in slots2[j][1])
                    nc.scalar.activation(pt[j % 2][i][:, 0:w], st_ps[u % 2][:, 0:w], ACT.Exp).then_inc(st_exp, 1)

                def out_t(g, c):
                    act.wait_ge(pv_mm, (g * SL + (LAST[c] + 1)) * PIECES)
                    after(act, ob_t, g * 2 + (c - 1))
                    nc.scalar.activation(ot[c][:, :], pv_ps[:, :], ACT.Copy).then_inc(ot_out, 1)

                def group(g):
                    for u in range(PU):
                        if u == LAG - 1 and not (isinstance(g, int) and g == 0):
                            out_t(g - 1, 1)
                        if u == FIRST[1] * GH + LAG - 1:
                            out_t(g, 0)
                        exp_of(g, u)
                        if u == at(g, 7, 2):
                            copy_parts(g * 2 + 1)
                        if u == at(g, 15, 11) and not last_group(g):
                            copy_parts(g * 2 + 2)

                act.wait_ge(wp_in, 32)
                nc.scalar.activation(wp_hi[:, :, :], wp_raw[:, :, :], ACT.Copy).then_inc(wp_hi_set, 1)
                copy_parts(0)
                over_groups(act, group)
                out_t(GROUPS - 1, 1)

            @block.vector
            def _(dve):
                chain = Chain(dve, chain_sem)

                def max_of(g, k):
                    t, heads, c0, c1 = max_units[k]
                    w = c1 - c0
                    dve.wait_ge(max_mm, g * MU + k + 1)
                    nc.vector.tensor_reduce(
                        neg[c0 // C][:, t, heads[0]:heads[-1] + 1],
                        max_ps[k % 2][:, 0:len(heads) * w].rearrange("p (h c) -> p h c", c=w),
                        AX.X, ALU.max, negate=True).then_inc(max_out, 1)
                    if k == MA - 1:
                        split_max(g, 0)
                    if k == MU - 1:
                        split_max(g, 1)

                def split_max(g, c):
                    tiles = slice(c * HALF, (c + 1) * HALF)
                    dve.wait_ge(max_out, g * MU + (MU if c else MA))
                    after(dve, parts_mm, g * 2 + (c - 1))
                    chain.begin(g * 7 + 3 * c)
                    if c:
                        chain(nc.vector.tensor_tensor(neg[0][:, tiles, :], neg[0][:, tiles, :],
                                                      neg[1][:, tiles, :], ALU.min))
                    high, mid, low = (parts[c][:, :, k * GH:(k + 1) * GH] for k in range(3))
                    chain(nc.vector.tensor_copy(high, neg[0][:, tiles, :]))
                    chain(nc.vector.tensor_tensor(rest[:, :, :], neg[0][:, tiles, :], high, ALU.subtract))
                    chain(nc.vector.tensor_copy(mid, rest[:, :, :]))
                    nc.vector.tensor_tensor(low, rest[:, :, :], mid, ALU.subtract).then_inc(parts_set, 1)

                def fold(g, c):
                    dve.wait_ge(parts_out, g * 2 + c + 1)
                    cols = slice(c * C, (c + 1) * C)
                    dst = qst[S:P, g * GH:(g + 1) * GH, cols] if isinstance(g, int) else \
                        qst[S:P, ds(g * GH, GH), cols]
                    nc.vector.tensor_copy(dst, parts_t[S:P, :].unsqueeze(1).broadcast_to([P - S, GH, C]))\
                        .then_inc(folded, 1)

                def finish(g, c):
                    dve.wait_ge(ob_t, g * 2 + c + 1)
                    got = mix_ps[:, :].rearrange("p (t h d) -> p t h d", h=GH, d=VW)
                    after(dve, o_out, g * 2 + c)
                    nc.vector.reciprocal(rsum[:, :, :], got[:, :, :, DB]).then_inc(rs, 1)
                    dve.wait_ge(rs, g * 2 + c + 1)
                    tiles = slice(c * HALF, (c + 1) * HALF)
                    dst = o_sb[:, tiles, g * GH * DB:(g + 1) * GH * DB] if isinstance(g, int) else \
                        o_sb[:, tiles, ds(g * (GH * DB), GH * DB)]
                    nc.vector.scalar_tensor_tensor(
                        out=dst.rearrange("p t (h d) -> p t h d", d=DB), in0=got[:, :, :, 0:DB],
                        scalar=float(E) ** -0.5, in1=rsum[:, :, :].unsqueeze(3).broadcast_to([P, HALF, GH, DB]),
                        op0=ALU.mult, op1=ALU.mult).then_inc(o_out, 1)

                def group(g):
                    for u in range(PU):
                        for of, k in max_steps(g, u):
                            max_of(of, k)
                        if u == at(g, 7, 4):
                            fold(g, 1)
                        if u == 8 and not (isinstance(g, int) and g == 0):
                            finish(g - 1, 1)
                        if u == at(g, 16, 13) and not last_group(g):
                            fold(g + 1, 0)
                        if u == 18:
                            finish(g, 0)

                dve.wait_ge(parts_zero, 1)
                for k in range(MA):
                    max_of(0, k)
                fold(0, 0)
                over_groups(dve, group)
                dve.wait_ge(wp_hi_set, 1)
                nc.vector.tensor_tensor(wp_lo[:, :, :], wp_raw[:, :, :], f32(wp_hi[:, :, :]), ALU.subtract)\
                    .then_inc(wp_lo_set, 1)
                nc.vector.tensor_tensor(m.x[:, :, :], m.x[:, :, :],
                                        out_bias[:, :].unsqueeze(1).broadcast_to([P, NT, E]), ALU.add)\
                    .then_inc(biased, 1)
                finish(GROUPS - 1, 1)

            @block.tensor
            def _(pe):
                def max_scores(g, k):
                    t, heads, c0, c1 = max_units[k]
                    w = c1 - c0
                    after(pe, max_out, g * MU + k - 1)
                    for n, i in enumerate(heads):
                        out = max_ps[k % 2][:, n * w:(n + 1) * w]
                        masked = c1 > t * P
                        last = nc.tensor.matmul(out, of_heads(qst, g, i, slice(0, S), t * P, (t + 1) * P),
                                                of_heads(kst, g, i, slice(0, S), c0, c1),
                                                start=True, stop=not masked)
                        if masked:
                            last = nc.tensor.matmul(out[:, w - P:w], m.ident_bf[:, :], m.mask[:, :],
                                                    start=False, stop=True)
                    last.then_inc(max_mm, 1)

                def mix_free(uses_parts, uses_out):
                    after(pe, parts_out, uses_parts)
                    after(pe, o_out, uses_out)

                def parts_tr(g, c, outs):
                    pe.wait_ge(parts_set, g * 2 + c + 1)
                    mix_free(g * 2 + c, outs)
                    for t in range(HALF):
                        last = nc.tensor.matmul(mix_ps[S:P, t * P:(t + 1) * P], parts[c][:, t, :], m.ident_bf[:, :],
                                                start=True, stop=True)
                    last.then_inc(parts_mm, 1)

                def scores_t(g, u):
                    j, i = u // GH, u % GH
                    c, tiles = slots2[j]
                    after(pe, st_exp, g * PU + u - 1)
                    if i == 0 and j in FIRST:
                        pe.wait_ge(folded, g * 2 + c + 1)
                    for kb, w, offset in tiles:
                        out = st_ps[u % 2][:, offset:offset + w]
                        masked = kb >= c * HALF
                        last = nc.tensor.matmul(out, of_heads(kst, g, i, slice(0, P), kb * P, (kb + 1) * P),
                                                of_heads(qst, g, i, slice(0, P), (c + 1) * C - w, (c + 1) * C),
                                                start=True, stop=not masked)
                        if masked:
                            last = nc.tensor.matmul(out[:, 0:P], m.ident_bf[:, :], m.mask_t[:, :],
                                                    start=False, stop=True)
                    last.then_inc(st_mm, 1)

                def times_v(g, n):
                    j, a, half = n // PIECES, n % PIECES // 2, n % 2
                    c, tiles = slots2[j]
                    kb, w, offset = tiles[a]
                    x, y = w // 2 * half, w // 2 * (half + 1)
                    pe.wait_ge(st_exp, g * PU + (j + 1) * GH)
                    if j in FIRST and n % PIECES == 0:
                        after(pe, ot_out, g * 2 + c)
                    pe.wait_ge(vg_ready, g * 3 + (1 + (kb >= 4) + (kb >= 6)))
                    for i in range(GH):
                        last = nc.tensor.matmul(pv_ps[VW * i:VW * (i + 1), C - w + x:C - w + y],
                                                vg[:, kb, VW * i:VW * (i + 1)],
                                                pt[j % 2][i][:, offset + x:offset + y],
                                                start=kb == 0 and half == 0,
                                                stop=j in LAST and a == 1, skip_group_check=True)
                    last.then_inc(pv_mm, 1)

                def back(g, c, outs):
                    pe.wait_ge(ot_out, g * 2 + c + 1)
                    mix_free(outs, g * 2 + c)
                    for t in range(HALF):
                        last = nc.tensor.transpose(mix_ps[:, t * P:(t + 1) * P], ot[c][:, t * P:(t + 1) * P],
                                                   m.ident[:, :])
                    last.then_inc(ob_t, 1)

                def group(g):
                    first = isinstance(g, int) and g == 0
                    for u in range(PU):
                        scores_t(g, u)
                        beside = max_steps(g, u)
                        for of, k in beside[0:len(beside) // 2]:
                            max_scores(of, k)
                        if u < LAG and not first:
                            times_v(g - 1, PU - LAG + u)
                        if u >= LAG:
                            times_v(g, u - LAG)
                        for of, k in beside[len(beside) // 2:]:
                            max_scores(of, k)
                        if u == at(g, 7, 1):
                            parts_tr(g, 1, g * 2 - 1)
                        if u == 6 and not first:
                            back(g - 1, 1, g * 2 + 2)
                        if u == at(g, 14, 10) and not last_group(g):
                            parts_tr(g + 1, 0, g * 2)
                        if u == 16:
                            back(g, 0, g * 2 + (2 if last_group(g) else 3))

                for k in range(MA):
                    max_scores(0, k)
                parts_tr(0, 0, 0)
                over_groups(pe, group)
                for n in range(PU - LAG, PU):
                    times_v(GROUPS - 1, n)
                back(GROUPS - 1, 1, 2 * GROUPS)

    with ExitStack() as inner:
        ok = m.inner(inner, "bo")
        ot_hi, ot_lo = ok.sb("ot_hi", [P, NE, N], F32R), ok.sb("ot_lo", [P, NE, N], F32R)
        o_ps = [ok.ps(f"o_ps{i}", [P, NE, 2 * P]) for i in range(4)]
        y_ps = [ok.ps(f"y_ps{i}", [P, 512]) for i in range(2)]
        o_t, hi_out, lo_out, y_mm, y_out = (ok.sem("o_t"), ok.sem("hi_out"), ok.sem("lo_out"),
                                                    ok.sem("y_mm"), ok.sem("y_out"))
        with nc.Block() as block:
            @block.scalar
            def _(act):
                for u in range(4):
                    act.wait_ge(o_t, u + 1)
                    nc.scalar.activation(ot_hi[:, :, 2 * P * u:2 * P * (u + 1)], o_ps[u][:, :, :], ACT.Copy)\
                        .then_inc(hi_out, 1)

            @block.vector
            def _(dve):
                for u in range(4):
                    dve.wait_ge(hi_out, u + 1)
                    cols = slice(2 * P * u, 2 * P * (u + 1))
                    nc.vector.tensor_tensor(ot_lo[:, :, cols], o_ps[u][:, :, :], f32(ot_hi[:, :, cols]),
                                            ALU.subtract).then_inc(lo_out, 1)
                for t in range(NT):
                    dve.wait_ge(y_mm, t + 1)
                    nc.vector.tensor_tensor(m.x[:, t, :], m.x[:, t, :], y_ps[t % 2][:, 0:E], ALU.add).then_inc(y_out, 1)
                    dve.wait_ge(y_out, t + 1)
                    nc.vector.bn_stats(m.stats[:, t, :], m.x[:, t, :])

            @block.tensor
            def _(pe):
                for u in range(4):
                    for e in range(NE):
                        for j in range(2):
                            last = nc.tensor.transpose(o_ps[u][:, e, j * P:(j + 1) * P],
                                                       o_sb[:, 2 * u + j, e * P:(e + 1) * P], m.ident[:, :])
                    last.then_inc(o_t, 1)
                for t in range(NT):
                    pe.wait_ge(lo_out, t // 2 + 1)
                    after(pe, y_out, t - 1)
                    rows = slice(t * P, (t + 1) * P)
                    for e in range(NE):
                        last = three(nc, y_ps[t % 2][:, 0:E], ot_hi[:, e, rows], ot_lo[:, e, rows],
                                     wp_hi[:, e, :], wp_lo[:, e, :], e == 0, e == NE - 1)
                    last.then_inc(y_mm, 1)


class SharedExpert:

    def __init__(self, m):
        self.hi13, self.lo13 = m.sb("s13_hi", [P, NE, 2 * F], F32R), m.sb("s13_lo", [P, NE, 2 * F], F32R)
        self.gate = m.sb("gate", [P, NE, EXPERTS])
        self.hi2, self.lo2 = m.sb("s2_hi", [P, 3, E], F32R), m.sb("s2_lo", [P, 3, E], F32R)

    def steps(self, nc, m, gate, s13, s2a, s2b):
        raw13, raw2 = m.sb("s13_raw", [P, NE, 2 * F]), m.sb("s2_raw", [P, 3, E])
        loaded, hi_set, lo_set = m.sem("s_loaded"), m.sem("s_hi_set"), m.sem("s_lo_set")
        parts = [(raw13[:, :, :], self.hi13[:, :, :], self.lo13[:, :, :]),
                 (raw2[:, 0:2, :], self.hi2[:, 0:2, :], self.lo2[:, 0:2, :]),
                 (raw2[0:F3, 2, :], self.hi2[0:F3, 2, :], self.lo2[0:F3, 2, :])]

        def load(sp):
            for (raw, _, _), src in zip(parts, (s13, s2a, s2b)):
                sp.dma_start(raw, src).then_inc(loaded, 16)
            sp.dma_start(self.gate[:, :, :], gate).then_inc(loaded, 16)

        def split(pool):
            pool.wait_ge(loaded, 64)
            for raw, hi, _ in parts:
                nc.gpsimd.tensor_copy(hi, raw).then_inc(hi_set, 1)
            pool.wait_ge(hi_set, 3)
            for raw, hi, lo in parts:
                nc.gpsimd.tensor_tensor(lo, raw, f32(hi), ALU.subtract).then_inc(lo_set, 1)

        return {"sync": load, "pool": split}


class AttentionWeights:

    def __init__(self, m):
        self.hi, self.lo = m.sb("hi", [P, NE, 3 * E], F32R), m.sb("lo", [P, NE, 3 * E], F32R)
        self.bias_hi, self.bias_lo = m.sb("bias_hi", [1, 3 * E], F32R), m.sb("bias_lo", [1, 3 * E], F32R)
        self.ones = m.sb("ones", [1, P], F32R)

    def steps(self, nc, m, ones, w_attn, b_attn, rope):
        raw, raw_bias = m.sb("raw", [P, NE, 3 * E]), m.sb("raw_bias", [1, 3 * E])
        turn = m.sb("turn", [P, 2, E])
        by_sin = m.sb("by_sin", [P, NE, 2, E])
        loaded, rotated = m.sem("loaded"), m.sem("rotated")
        by_sines, by_cosines = m.sem("by_sines"), m.sem("by_cosines")
        hi_set, lo_set = m.sem("hi_set"), m.sem("lo_set")
        pairs = [(raw[:, :, :], self.hi[:, :, :], self.lo[:, :, :]),
                 (raw_bias[:, :], self.bias_hi[:, :], self.bias_lo[:, :])]

        def load(sp):
            sp.dma_start(raw[:, :, :], w_attn).then_inc(loaded, 16)
            sp.dma_start(raw_bias[:, :], b_attn).then_inc(loaded, 16)
            sp.dma_start(turn[:, :, :], rope.broadcast_to([P, 2, E])).then_inc(loaded, 16)

        def rotate(pool):
            pool.wait_ge(loaded, 16 * 3)
            done = 0
            for rows, n, w in ((P, NE, raw[:, :, 0:2 * E]), (1, 1, raw_bias[:, 0:2 * E].unsqueeze(1))):
                w = w.rearrange("p n (r c) -> p n r c", r=2)
                sines = by_sin[0:rows, 0:n, :, :]

                def table(k):
                    return turn[0:rows, k, :].unsqueeze(1).unsqueeze(1).broadcast_to([rows, n, 2, E])

                for e in range(n):
                    for k in range(2):
                        last = nc.gpsimd.tensor_tensor(sines[:, e, :, k::2], w[:, e, :, 1 - k::2],
                                                       table(1)[:, e, :, k::2], ALU.mult)
                last.then_inc(by_sines, 1)
                done += 1
                pool.wait_ge(by_sines, done)
                for e in range(n):
                    last = nc.gpsimd.tensor_tensor(w[:, e], w[:, e], table(0)[:, e], ALU.mult)
                last.then_inc(by_cosines, 1)
                pool.wait_ge(by_cosines, done)
                for e in range(n):
                    last = nc.gpsimd.tensor_tensor(w[:, e], w[:, e], sines[:, e], ALU.add)
                last.then_inc(rotated, 1)
                pool.wait_ge(rotated, done)

        def high(act):
            act.wait_ge(rotated, 2)
            nc.scalar.activation(self.ones[:, :], ones[0:1, :], ACT.Copy)
            for whole, hi, _ in pairs:
                nc.scalar.activation(hi, whole, ACT.Copy).then_inc(hi_set, 1)

        def low(dve):
            dve.wait_ge(hi_set, len(pairs))
            for whole, hi, lo in pairs:
                nc.vector.tensor_tensor(lo, whole, f32(hi), ALU.subtract).then_inc(lo_set, 1)

        return {"sync": load, "pool": rotate, "scalar": high, "vector": low}


class Memory:

    def __init__(self, nc, scope, tag):
        self.nc, self.scope, self.tag = nc, scope, tag

    def inner(self, scope, tag):
        return Memory(self.nc, scope, tag)

    def sb(self, name, shape, dt=F32):
        return self.scope.enter_context(self.nc.sbuf_tensor(f"{self.tag}_{name}", shape, dt))

    def ps(self, name, shape, dt=F32):
        return self.scope.enter_context(self.nc.psum_tensor(f"{self.tag}_{name}", shape, dt))

    def sem(self, name):
        return self.nc.alloc_semaphore(f"{self.tag}_{name}")


def program(nc, x, w_qkv, w_o, q_scale, k_scale, w_attn, b_attn, rope, w_proj, b_proj, gate, w13, w2a, w2b,
            s13, s2a, s2b, rank, steps, dest, spare, out):
    with ExitStack() as ctx:
        m = Memory(nc, ctx, "m")
        m.x = m.sb("x", [P, NT, E])
        m.stats = m.sb("stats", [P, NT, 6])
        m.xnt = m.sb("xnt", [P, NE, N])
        m.xnt_hi = m.sb("xnt_hi", [P, NE, N], F32R)
        m.xnt_lo = m.sb("xnt_lo", [P, NE, N], F32R)
        m.ident = m.sb("ident", [P, P])
        m.ident_bf = m.sb("ident_bf", [P, P], BF16)
        m.mask = m.sb("mask", [P, P], BF16)
        m.mask_t = m.sb("mask_t", [P, P], BF16)
        m.before = m.sb("before", [P, P], BF16)
        m.ones_bf = m.sb("ones_bf", [P, P], BF16)
        m.rank = m.sb("rank", [P, EXPERTS])
        m.steps = m.sb("steps", [P, NT])
        m.dest = m.sb("dest", [P, 2, NT], I32)
        m.xs = {tag: nc.dram_tensor(f"sorted_rows_{tag}", (BLOCKS, P, W), F32, kind="Internal").ap()
                for tag in ("moe1", "moe3")}
        m.ys = nc.dram_tensor("results", (2 * N + 4 * P, E), F32, kind="Internal").ap()
        shared = SharedExpert(m)
        made = m.sem("made")
        x_in = [m.sem(f"x_in{u}") for u in range(NT // 2)]
        with nc.Block() as block:
            @block.sync
            def _(sp):
                for u in range(NT // 2):
                    sp.dma_start(m.x[:, 2 * u:2 * u + 2, :], x[:, 2 * u:2 * u + 2, :]).then_inc(x_in[u], 16)

            @block.gpsimd
            def _(pool):
                nc.gpsimd.memset(m.ident[:, :], 0.0).then_inc(made, 1)
                nc.gpsimd.memset(m.ident_bf[:, :], 0.0).then_inc(made, 1)
                nc.gpsimd.memset(m.mask[:, :], 0.0).then_inc(made, 1)
                nc.gpsimd.memset(m.mask_t[:, :], 0.0).then_inc(made, 1)
                nc.gpsimd.memset(m.before[:, :], 1.0).then_inc(made, 1)
                nc.gpsimd.memset(m.ones_bf[:, :], 1.0).then_inc(made, 1)
                pool.wait_ge(made, 6)
                for eye in (m.ident, m.ident_bf):
                    nc.gpsimd.affine_select(out=eye[:, :], in_=eye[:, :], compare_op=ALU.not_equal, fill=1.0,
                                            base=0, pattern=[[-1, P]], channel_multiplier=1)
                nc.gpsimd.affine_select(out=m.mask[:, :], in_=m.mask[:, :], compare_op=ALU.is_ge, fill=MASKED,
                                        base=0, pattern=[[-1, P]], channel_multiplier=1)
                nc.gpsimd.affine_select(out=m.mask_t[:, :], in_=m.mask_t[:, :], compare_op=ALU.is_ge, fill=MASKED,
                                        base=0, pattern=[[1, P]], channel_multiplier=-1)
                nc.gpsimd.affine_select(out=m.before[:, :], in_=m.before[:, :], compare_op=ALU.is_gt, fill=0.0,
                                        base=0, pattern=[[1, P]], channel_multiplier=-1)
        with nc.cleanup_on_exit(), ExitStack() as scope:
            attention_a(nc, scope, m, x_in, w_qkv, w_o, q_scale, k_scale, rank, steps, dest, spare,
                        more=shared.steps(nc, m.inner(scope, "sh"), gate, s13, s2a, s2b))
        with ExitStack() as until_b:
            weights_b = AttentionWeights(m.inner(until_b, "wb"))
            with nc.cleanup_on_exit(), ExitStack() as scope:
                mixture(nc, scope, "moe1", m, w13, w2a, w2b, shared,
                        more=weights_b.steps(nc, m.inner(scope, "wb"), m.ones_bf, w_attn, b_attn, rope))
            with ExitStack() as scope:
                layer_norm(nc, scope, "ln2", m)
            with nc.cleanup_on_exit(), ExitStack() as scope:
                attention_b(nc, scope, m, weights_b, w_proj, b_proj)
        with ExitStack() as scope:
            mixture(nc, scope, "moe3", m, w13, w2a, w2b, shared, store=out)


def rope_table():
    freqs = np.float32(10000.0) ** (-(np.arange(0, DB, 2, dtype=np.float32) / np.float32(DB)))
    angle = np.outer(np.arange(HB, dtype=np.float32), freqs)
    cos = np.repeat(np.cos(angle), 2, axis=1)
    sin = np.stack([-np.sin(angle), np.sin(angle)], axis=-1)
    return np.stack([cos.reshape(-1), sin.reshape(-1)]).astype(np.float32)[None]


def kernel(**inputs):
    import concourse.bacc as bacc
    from concourse.bass_utils import run_bass_kernel_spmd

    def part(name):
        return np.asarray(inputs[name])

    def tiles(a):
        return np.ascontiguousarray(a.reshape(-1, P, *a.shape[1:]).swapaxes(0, 1))

    qkv = np.concatenate([part(f"L0_attn_a_w{c}") for c in "qkv"], axis=2)
    qkv = qkv.reshape(NE, P, HA, 3 * DA).transpose(2, 1, 0, 3)
    w13 = np.concatenate([part("L0_ffn_w1"), part("L0_ffn_w3")], axis=1)
    w13 = w13.reshape(EXPERTS, 2 * INTER, NE, P).transpose(3, 0, 2, 1)
    w2 = part("L0_ffn_w2").transpose(2, 0, 1)
    s13 = np.concatenate([part("L0_ffn_sw1"), part("L0_ffn_sw3")])
    s2 = part("L0_ffn_sw2").T
    arrays = {
        "x": tiles(part("L0_attn_a_x")[0]),
        "w_qkv": np.ascontiguousarray(qkv),
        "w_o": np.ascontiguousarray(part("L0_attn_a_wo").transpose(1, 0, 2)),
        "q_scale": part("L0_attn_a_q_scale")[:, None],
        "k_scale": part("L0_attn_a_k_scale")[:, None],
        "w_attn": tiles(part("L0_attn_b_w_attn")),
        "b_attn": part("L0_attn_b_b_attn")[None],
        "rope": rope_table(),
        "w_proj": tiles(part("L0_attn_b_w_proj")),
        "b_proj": part("L0_attn_b_b_proj")[None],
        "gate": tiles(part("L0_ffn_gate_w").T),
        "w13": np.ascontiguousarray(w13),
        "w2a": np.ascontiguousarray(w2[0:P]),
        "w2b": np.ascontiguousarray(w2[P:INTER]),
        "s13": tiles(s13.T),
        "s2a": tiles(s2[0:2 * P]),
        "s2b": np.ascontiguousarray(s2[2 * P:F]),
        "rank": np.tile(EXPERTS - np.arange(EXPERTS, dtype=np.float32), (P, 1)),
        "steps": np.tile(P * np.arange(NT, dtype=np.float32), (P, 1)),
        "dest": np.ascontiguousarray(np.arange(2 * N, dtype=np.int32).reshape(P, NT, 2).swapaxes(1, 2)),
        "spare": np.ascontiguousarray(2 * N + np.arange(4 * P, dtype=np.int32).reshape(4, P).T),
    }
    nc = bacc.Bacc("TRN2", target_bir_lowering=False, num_devices=1)
    aps = [nc.dram_tensor(f"in_{name}", a.shape, I32 if a.dtype == np.int32 else F32, kind="ExternalInput").ap()
           for name, a in arrays.items()]
    out = nc.dram_tensor("out", (P, NT, E), F32, kind="ExternalOutput").ap()
    program(nc, *aps, out)
    r = run_bass_kernel_spmd(nc, [{f"in_{name}": a for name, a in arrays.items()}], core_ids=[0])
    return r.results[0]["out"].transpose(1, 0, 2).reshape(1, N, E)
```
